# Optimizing a Trainium2 kernel written in Bass

```python
import numpy as np
import jax
import jax.numpy as jnp

def _softmax(x, axis=-1):
    return jax.nn.softmax(x, axis=axis)

def _gelu(x):
    return jax.nn.gelu(x, approximate=True)

def _silu(x):
    return jax.nn.silu(x)

def _sigmoid(x):
    return jax.nn.sigmoid(x)

def _layernorm(x, axis=-1, eps=1e-05):
    m = jnp.mean(x, axis=axis, keepdims=True)
    v = jnp.var(x, axis=axis, keepdims=True)
    return (x - m) / jnp.sqrt(v + eps)

def _scatter_add(tgt, idx, src, axis=0):
    return tgt.at[idx].add(src)

def _segment_sum(src, seg, n):
    return jax.ops.segment_sum(src, seg, n)
kernel_name = 'mk_hybrid_d1_jaxref_r8_7cdc67'

def setup_inputs(seed: int=0):
    np.random.seed(seed)
    _w = jnp.asarray

    def _L0_attn_a_setup():
        import jax, jax.numpy as jnp
        import numpy as np
        B, T, HID = (2, 512, 256)
        H, K = (16, 128)
        BS = 64
        EPS = 1e-06
        SCALING = K ** (-0.5)
        key = jax.random.key(seed)
        ks = jax.random.split(key, 8)
        sin = HID ** (-0.5)
        sout = (H * K) ** (-0.5)
        return {'x': jax.random.normal(ks[0], (B, T, HID), jnp.float32), 'Wq': jax.random.normal(ks[1], (HID, H * K), jnp.float32) * sin, 'Wk': jax.random.normal(ks[2], (HID, H * K), jnp.float32) * sin, 'Wv': jax.random.normal(ks[3], (HID, H * K), jnp.float32) * sin, 'phi_scale': 1.0 + 0.1 * jax.random.normal(ks[4], (H, 1, K), jnp.float32), 'phi_bias': 0.1 * jax.random.normal(ks[5], (H, 1, K), jnp.float32), 'Wo': jax.random.normal(ks[6], (H * K, HID), jnp.float32) * sout, 'bo': jnp.zeros((HID,), jnp.float32)}
    _L0_attn_a_in = _L0_attn_a_setup()

    def _L0_attn_b_setup():
        import jax, jax.numpy as jnp
        import numpy as np
        B, T, D = (4, 256, 256)
        H = 16
        KD = D // 2
        VD = D
        DK = KD // H
        DV = VD // H
        LR = 16
        EPS = 1e-05
        GATE_LOGIT_NORMALIZER = 16.0
        key = jax.random.key(seed)
        ks = jax.random.split(key, 9)

        def w(k, shape):
            fan_in = shape[0]
            return (jax.random.normal(k, shape, jnp.float32) * fan_in ** (-0.5)).astype(jnp.float32)
        return {'x': jax.random.normal(ks[0], (B, T, D), jnp.float32), 'Wq': w(ks[1], (D, KD)), 'Wk': w(ks[2], (D, KD)), 'Wv': w(ks[3], (D, VD)), 'Wg': w(ks[4], (D, VD)), 'Wgk1': w(ks[5], (D, LR)), 'Wgk2': w(ks[6], (LR, KD)), 'bgk2': jnp.zeros((KD,), jnp.float32), 'norm_w': jnp.ones((DV,), jnp.float32), 'Wo': w(ks[7], (VD, D))}
    _L0_attn_b_in = _L0_attn_b_setup()

    def _L0_ffn_setup():
        import jax, jax.numpy as jnp
        import numpy as np
        HIDDEN = 256
        INTER = 704
        B, S = (2, 256)

        def _ternary(key, shape):
            return jax.random.randint(key, shape, -1, 2).astype(jnp.float32)
        key = jax.random.key(seed)
        ks = jax.random.split(key, 7)
        x = jax.random.normal(ks[0], (B, S, HIDDEN), dtype=jnp.float32)
        gate_w = _ternary(ks[1], (INTER, HIDDEN))
        up_w = _ternary(ks[2], (INTER, HIDDEN))
        down_w = _ternary(ks[3], (HIDDEN, INTER))
        gate_s = jax.random.uniform(ks[4], (INTER,), minval=0.01, maxval=0.1, dtype=jnp.float32)
        up_s = jax.random.uniform(ks[5], (INTER,), minval=0.01, maxval=0.1, dtype=jnp.float32)
        down_s = jax.random.uniform(ks[6], (HIDDEN,), minval=0.01, maxval=0.1, dtype=jnp.float32)
        return {'x': x, 'gate_w': gate_w, 'up_w': up_w, 'down_w': down_w, 'gate_s': gate_s, 'up_s': up_s, 'down_s': down_s}
    _L0_ffn_in = _L0_ffn_setup()
    _d = {'L0_attn_a_x': _L0_attn_a_in['x'], 'L0_attn_a_Wq': _L0_attn_a_in['Wq'], 'L0_attn_a_Wk': _L0_attn_a_in['Wk'], 'L0_attn_a_Wv': _L0_attn_a_in['Wv'], 'L0_attn_a_phi_scale': _L0_attn_a_in['phi_scale'], 'L0_attn_a_phi_bias': _L0_attn_a_in['phi_bias'], 'L0_attn_a_Wo': _L0_attn_a_in['Wo'], 'L0_attn_a_bo': _L0_attn_a_in['bo'], 'L0_attn_b_Wq': _L0_attn_b_in['Wq'], 'L0_attn_b_Wk': _L0_attn_b_in['Wk'], 'L0_attn_b_Wv': _L0_attn_b_in['Wv'], 'L0_attn_b_Wg': _L0_attn_b_in['Wg'], 'L0_attn_b_Wgk1': _L0_attn_b_in['Wgk1'], 'L0_attn_b_Wgk2': _L0_attn_b_in['Wgk2'], 'L0_attn_b_bgk2': _L0_attn_b_in['bgk2'], 'L0_attn_b_norm_w': _L0_attn_b_in['norm_w'], 'L0_attn_b_Wo': _L0_attn_b_in['Wo'], 'L0_ffn_gate_w': _L0_ffn_in['gate_w'], 'L0_ffn_up_w': _L0_ffn_in['up_w'], 'L0_ffn_down_w': _L0_ffn_in['down_w'], 'L0_ffn_gate_s': _L0_ffn_in['gate_s'], 'L0_ffn_up_s': _L0_ffn_in['up_s'], 'L0_ffn_down_s': _L0_ffn_in['down_s']}
    _x0 = _d['L0_attn_a_x']
    _d['L0_attn_a_x'] = jax.random.normal(jax.random.fold_in(jax.random.key(seed), 1), (16, 256, 256), dtype=_x0.dtype)
    del _x0
    return _d

def reference(L0_attn_a_x, L0_attn_a_Wq, L0_attn_a_Wk, L0_attn_a_Wv, L0_attn_a_phi_scale, L0_attn_a_phi_bias, L0_attn_a_Wo, L0_attn_a_bo, L0_attn_b_Wq, L0_attn_b_Wk, L0_attn_b_Wv, L0_attn_b_Wg, L0_attn_b_Wgk1, L0_attn_b_Wgk2, L0_attn_b_bgk2, L0_attn_b_norm_w, L0_attn_b_Wo, L0_ffn_gate_w, L0_ffn_up_w, L0_ffn_down_w, L0_ffn_gate_s, L0_ffn_up_s, L0_ffn_down_s):

    def _L0_attn_a_ref(x, Wq, Wk, Wv, phi_scale, phi_bias, Wo, bo):
        import jax, jax.numpy as jnp
        import numpy as np
        B, T, HID = (2, 512, 256)
        H, K = (16, 128)
        BS = 64
        EPS = 1e-06
        SCALING = K ** (-0.5)
        b, t, _ = x.shape
        nb = t // BS
        dt = x.dtype

        def proj(W):
            return (x @ W).reshape(b, t, H, K).transpose(0, 2, 1, 3).reshape(b, H, nb, BS, K)
        q_b, k_b, v_b = (proj(Wq), proj(Wk), proj(Wv))
        scores = jnp.einsum('bhntk,bhnsk->bhnts', q_b, k_b) * SCALING
        attn = jax.nn.softmax(scores.astype(jnp.float32), axis=-1).astype(dt)
        local = jnp.einsum('bhnts,bhnsk->bhntk', attn, v_b)
        ps = phi_scale[None, :, None]
        pb = phi_bias[None, :, None]
        phi = lambda z: jnp.clip(jax.nn.elu(z * ps + pb) + 1.0, 0.0, 10.0)
        phi_q = phi(q_b)
        phi_k = phi(k_b)
        pk_s = jnp.moveaxis(phi_k, 2, 0).astype(jnp.float32)
        pq_s = jnp.moveaxis(phi_q, 2, 0).astype(jnp.float32)
        v_s = jnp.moveaxis(v_b, 2, 0).astype(jnp.float32)

        def step(carry, xs):
            S, Z = carry
            pk, vn, pq = xs
            S = S + jnp.einsum('bhtk,bhtv->bhkv', pk, vn)
            Z = Z + pk.sum(axis=-2)
            num = jnp.einsum('bhtk,bhkv->bhtv', pq, S)
            den = jnp.maximum(jnp.einsum('bhtk,bhk->bht', pq, Z), EPS)[..., None]
            return ((S, Z), (num / den).astype(dt))
        S0 = jnp.zeros((b, H, K, K), jnp.float32)
        Z0 = jnp.zeros((b, H, K), jnp.float32)
        _, glob = jax.lax.scan(step, (S0, Z0), (pk_s, v_s, pq_s))
        glob = jnp.moveaxis(glob, 0, 2)
        hybrid = (local + glob).reshape(b, H, t, K).transpose(0, 2, 1, 3).reshape(b, t, H * K)
        return hybrid @ Wo + bo

    def _L0_attn_b_ref(x, Wq, Wk, Wv, Wg, Wgk1, Wgk2, bgk2, norm_w, Wo):
        import jax, jax.numpy as jnp
        import numpy as np
        B, T, D = (4, 256, 256)
        H = 16
        KD = D // 2
        VD = D
        DK = KD // H
        DV = VD // H
        LR = 16
        EPS = 1e-05
        GATE_LOGIT_NORMALIZER = 16.0
        b, t, _ = x.shape
        dv = norm_w.shape[0]
        vd = Wv.shape[1]
        h = vd // dv
        dk = Wq.shape[1] // h
        scale = dk ** (-0.5)
        q = (x @ Wq).reshape(b, t, h, dk) * scale
        k = (x @ Wk).reshape(b, t, h, dk)
        v = (x @ Wv).reshape(b, t, h, dv)
        gk = jax.nn.log_sigmoid(x @ Wgk1 @ Wgk2 + bgk2) / GATE_LOGIT_NORMALIZER
        gk = gk.reshape(b, t, h, dk)
        qT = jnp.moveaxis(q, 1, 0)
        kT = jnp.moveaxis(k, 1, 0)
        vT = jnp.moveaxis(v, 1, 0)
        gT = jnp.moveaxis(gk, 1, 0)

        def step(S, inp):
            qt, kt, vt, gt = inp
            S = S * jnp.exp(gt)[..., None] + kt[..., None] * vt[..., None, :]
            ot = jnp.einsum('bhk,bhkv->bhv', qt, S)
            return (S, ot)
        S0 = jnp.zeros((b, h, dk, dv), x.dtype)
        _, o = jax.lax.scan(step, S0, (qT, kT, vT, gT))
        o = jnp.moveaxis(o, 0, 1)
        g = (x @ Wg).reshape(b, t, h, dv)
        o = o * jax.lax.rsqrt(jnp.mean(o * o, axis=-1, keepdims=True) + EPS) * norm_w
        o = o * (g * jax.nn.sigmoid(g))
        return o.reshape(b, t, vd) @ Wo

    def _L0_ffn_ref(x, gate_w, up_w, down_w, gate_s, up_s, down_s):
        import jax, jax.numpy as jnp
        import numpy as np
        HIDDEN = 256
        INTER = 704
        B, S = (2, 256)

        def _ternary(key, shape):
            return jax.random.randint(key, shape, -1, 2).astype(jnp.float32)
        b, s, h = x.shape
        xf = x.reshape(b * s, h)
        g = jnp.einsum('th,ih->ti', xf, gate_w) * gate_s
        u = jnp.einsum('th,ih->ti', xf, up_w) * up_s
        hdn = jax.nn.silu(g) * u
        out = jnp.einsum('ti,hi->th', hdn, down_w) * down_s
        return out.reshape(b, s, -1)
    x = L0_attn_a_x
    x = x + _L0_attn_a_ref(_layernorm(x, axis=-1), L0_attn_a_Wq, L0_attn_a_Wk, L0_attn_a_Wv, L0_attn_a_phi_scale, L0_attn_a_phi_bias, L0_attn_a_Wo, L0_attn_a_bo)
    x = x + _L0_ffn_ref(_layernorm(x, axis=-1), L0_ffn_gate_w, L0_ffn_up_w, L0_ffn_down_w, L0_ffn_gate_s, L0_ffn_up_s, L0_ffn_down_s)
    x = x + _L0_attn_b_ref(_layernorm(x, axis=-1), L0_attn_b_Wq, L0_attn_b_Wk, L0_attn_b_Wv, L0_attn_b_Wg, L0_attn_b_Wgk1, L0_attn_b_Wgk2, L0_attn_b_bgk2, L0_attn_b_norm_w, L0_attn_b_Wo)
    x = x + _L0_ffn_ref(_layernorm(x, axis=-1), L0_ffn_gate_w, L0_ffn_up_w, L0_ffn_down_w, L0_ffn_gate_s, L0_ffn_up_s, L0_ffn_down_s)
    return x

_drawn_inputs = setup_inputs


def setup_inputs(seed=0):
    import zlib

    import numpy as np

    out = dict(_drawn_inputs(seed))
    spreads = {'L0_attn_a_bo': (0.0, 0.1), 'L0_attn_b_bgk2': (0.0, 0.423), 'L0_attn_b_norm_w': (1.0, 0.2)}
    factors = {'L0_attn_a_phi_scale': 8.0, 'L0_attn_a_phi_bias': 8.0}
    for name, (base, spread) in spreads.items():
        noise = np.random.default_rng([zlib.crc32(name.encode()), seed]).standard_normal(out[name].shape)
        drawn = base * np.exp(spread * noise) if base else spread * noise
        out[name] = jnp.asarray(drawn.astype(out[name].dtype))
    for name, factor in factors.items():
        out[name] = (out[name] * factor).astype(out[name].dtype)
    return out
```

```python
from contextlib import ExitStack

import concourse.bass as bass
from concourse import mybir

F32 = mybir.dt.float32
F32R = mybir.dt.float32r
ALU = mybir.AluOpType
ACT = mybir.ActivationFunctionType
AX_X = mybir.AxisListType.X

P = 128
B = 16
T = 256
D = 256
TT = T // P
KT = D // P
H = 16
HD = 128
BS = 64
SCALING = float(HD) ** -0.5
LN_EPS = 1e-5
DEN_EPS = 1e-6
PHI_TOP = 10.0
VB = 4
LAG = 8


def value(i, rate, k):
    if isinstance(i, int):
        v = i * rate + k
        return v if v > 0 else None
    assert k > 0
    return i * rate + k


def need(eng, sem, i, rate, k):
    v = value(i, rate, k)
    if v is not None:
        eng.wait_ge(sem, v)


def attention_a(nc, io, x_in, x_out):
    with ExitStack() as ctx:
        def sb(name, shape, dt=F32):
            return ctx.enter_context(nc.sbuf_tensor("a_" + name, shape, dt))

        def ps(name, shape):
            return ctx.enter_context(nc.psum_tensor("a_" + name, shape, F32))

        def sem(name):
            return ctx.enter_context(nc.semaphore("a_" + name))

        w_hi = [sb(f"w{n}_hi", [P, KT, H * HD], F32R) for n in "qkv"]
        w_lo = [sb(f"w{n}_lo", [P, KT, H * HD], F32R) for n in "qkv"]
        wo = sb("wo", [P, H, D])
        w_stage = sb("w_stage", [P, 2, KT, 4 * HD])
        phi_s = sb("phi_s", [P, H])
        phi_b = sb("phi_b", [P, H])
        phi_b1 = sb("phi_b1", [P, H])
        bo_bc = sb("bo_bc", [P, D])
        ident = sb("ident", [P, P])
        ones = sb("ones", [P, P])
        at_mask = sb("at_mask", [P, T + P])
        x_ln = sb("x_ln", [P, TT, D])
        x_res = sb("x_res", [P, TT, D])
        y = sb("y", [P, TT, D])
        xn = sb("xn", [P, TT, D])
        stats = sb("stats", [P, TT, 6])
        stats_count = sb("stats_count", [P, TT])
        mv = sb("mv", [P, TT, 2])
        var_eps = sb("var_eps", [P, TT])
        half = sb("half", [P, TT])
        rstd = sb("rstd", [P, TT])
        xt_hi = sb("xt_hi", [P, KT, T], F32R)
        xt_lo = sb("xt_lo", [P, KT, T], F32R)
        qk = sb("qk", [P, 2, 2, T])
        ez = sb("ez", [P, 2, T])
        z1 = sb("z1", [P, 2, T])
        phi_raw = sb("phi_raw", [P, 2, 2, T])
        phi = sb("phi", [P, 2, 2, T])
        v_ext = sb("v_ext", [P, VB, TT, 2, HD + 2])
        rmax = sb("rmax", [P, 4])
        sc = sb("sc", [P, 4, BS])
        pexp = sb("pexp", [P, 4, BS])
        rsum = sb("rsum", [P, 4])
        rinv = sb("rinv", [P, 4])
        prob = sb("prob", [P, 4, BS])
        pt = sb("pt", [P, 2, 2, TT, P])
        at = sb("at", [P, 2, T + P])
        den = sb("den", [P, TT])
        rden = sb("rden", [P, 2, TT])
        num = sb("num", [P, 2, TT, HD])
        o = sb("o", [P, 2, TT, HD])
        ot = sb("ot", [P, 2, T])

        qk_ps = [ps(f"qk_ps{i}", [P, 2, T]) for i in range(2)]
        v_ps = ps("v_ps", [P, 512])
        sc_ps = ps("sc_ps", [P, 512])
        at_ps = ps("at_ps", [P, 512])
        num_ps = ps("num_ps", [P, 512])
        lo_ps = ps("lo_ps", [P, 512])
        wo_ps = ps("wo_ps", [P, TT, D])

        consts_loaded = sem("consts_loaded")
        stage_loaded = [sem(f"stage_loaded{i}") for i in range(2)]
        wo_loaded = sem("wo_loaded")
        xln_loaded = sem("xln_loaded")
        xres_loaded = sem("xres_loaded")
        y_stored = sem("y_stored")
        mem_zeroed = sem("mem_zeroed")
        masks_ready = sem("masks_ready")
        w_hi_ready = sem("w_hi_ready")
        w_lo_ready = sem("w_lo_ready")
        ln_stats = sem("ln_stats")
        ln_mv = sem("ln_mv")
        ln_var = sem("ln_var")
        ln_rstd = sem("ln_rstd")
        xn_ready = sem("xn_ready")
        xt_done = sem("xt_done")
        xt_hi_ready = sem("xt_hi_ready")
        xt_lo_ready = sem("xt_lo_ready")
        qk_done = sem("qk_done")
        v_done = sem("v_done")
        sc_done = sem("sc_done")
        at_done = sem("at_done")
        pt_done = sem("pt_done")
        num_done = sem("num_done")
        loc_done = sem("loc_done")
        ot_done = sem("ot_done")
        wo_done = sem("wo_done")
        qk_copied = sem("qk_copied")
        e_ready = sem("e_ready")
        p_exp = sem("p_exp")
        pt_ready = sem("pt_ready")
        num_scaled = sem("num_scaled")
        v_ready = sem("v_ready")
        z1_ready = sem("z1_ready")
        phi_joined = sem("phi_joined")
        phi_ready = sem("phi_ready")
        max_ready = sem("max_ready")
        sc_ready = sem("sc_ready")
        sum_ready = sem("sum_ready")
        inv_ready = sem("inv_ready")
        prob_ready = sem("prob_ready")
        at_ready = sem("at_ready")
        den_ready = sem("den_ready")
        rden_ready = sem("rden_ready")
        ot_ready = sem("ot_ready")
        o_ready = sem("o_ready")
        y_sum = sem("y_sum")
        y_ready = sem("y_ready")

        block = ctx.enter_context(nc.Block())

        def run(eng, boot, step):
            boot(eng)
            for c in range(LAG):
                step(0, c)
            with eng.Fori(0, B - 1) as i:
                for c in range(LAG, LAG + H):
                    step(i, c)
            for c in range(LAG, H + LAG):
                step(B - 1, c)

        def live(i, n):
            return not isinstance(i, int) or 0 <= H * i + n < B * H

        @block.sync
        def _(sp):
            sp.dma_start(x_ln[:], x_in[0].rearrange("(t p) d -> p t d", p=P)).then_inc(xln_loaded, 16)
            sp.dma_start(phi_s[:], io["phi_scale"].rearrange("h o k -> k (h o)"),
                         allow_slow_non_contiguous=True).then_inc(consts_loaded, 16)
            sp.dma_start(phi_b[:], io["phi_bias"].rearrange("h o k -> k (h o)"),
                         allow_slow_non_contiguous=True).then_inc(consts_loaded, 16)
            sp.dma_start(bo_bc[:], io["bo"].rearrange("(a n) -> a n", a=1).broadcast_to([P, D]))\
              .then_inc(consts_loaded, 16)
            for m in range(12):
                if m >= 2:
                    sp.wait_ge(w_lo_ready, m - 1)
                g, w = m // 3, io["W" + "qkv"[m % 3]]
                sp.dma_start(w_stage[:, m % 2], w.rearrange("(k p) n -> p k n", p=P)[:, :, g * 512:(g + 1) * 512])\
                  .then_inc(stage_loaded[m % 2], 16)
                if m == 5:
                    sp.dma_start(wo[:], io["Wo"].rearrange("(h p) n -> p h n", p=P)).then_inc(wo_loaded, 16)

            for b in range(B):
                if b + 1 < B:
                    sp.wait_ge(xn_ready, b + 1)
                    sp.dma_start(x_ln[:], x_in[b + 1].rearrange("(t p) d -> p t d", p=P)).then_inc(xln_loaded, 16)
                if b:
                    sp.wait_ge(y_sum, b)
                    sp.wait_ge(y_stored, 16 * b)
                sp.dma_start(x_res[:], x_in[b].rearrange("(t p) d -> p t d", p=P)).then_inc(xres_loaded, 16)
                sp.wait_ge(y_ready, b + 1)
                sp.dma_start(x_out[b].rearrange("(t p) d -> p t d", p=P), y[:]).then_inc(y_stored, 16)
            sp.wait_ge(y_stored, 16 * B)

        @block.gpsimd
        def _(pool):
            pool.memset(ident[:], 0.0).then_inc(mem_zeroed, 1)
            pool.memset(ones[:], 1.0).then_inc(mem_zeroed, 1)
            pool.memset(half[:], -0.5).then_inc(mem_zeroed, 1)
            pool.memset(at_mask[:], 1.0).then_inc(mem_zeroed, 1)
            pool.memset(pt[:], 0.0).then_inc(mem_zeroed, 1)
            for par in range(VB):
                for h2 in range(2):
                    pool.memset(v_ext[:, par, :, h2, HD:HD + 1], 1.0).then_inc(mem_zeroed, 1)
                    pool.memset(v_ext[:, par, :, h2, HD + 1:HD + 2], 0.0).then_inc(mem_zeroed, 1)
            pool.wait_ge(mem_zeroed, 5 + 4 * VB)
            pool.memset(at_mask[BS:P, 0:BS], 0.0).then_inc(masks_ready, 1)
            pool.memset(at_mask[BS:P, T:T + BS], 0.0).then_inc(masks_ready, 1)
            pool.wait_ge(masks_ready, 2)
            pool.affine_select(out=ident[:], in_=ident[:], compare_op=ALU.not_equal, fill=1.0, base=0,
                               pattern=[[-1, P]], channel_multiplier=1).then_inc(masks_ready, 1)

            def power(i, k):
                need(pool, ln_var, i, 1, k)
                pool.tensor_tensor(rstd[:], var_eps[:], half[:], ALU.pow).then_inc(ln_rstd, 1)

            pool.wait_ge(mem_zeroed, 3)
            power(0, 1)
            with pool.Fori(0, B - 1) as i:
                power(i, 2)

        @block.tensor
        def _(pe):
            def product(out, hi_l, lo_l, hi_r, lo_r, start=True):
                last = None
                for k in range(KT):
                    for m, (l, r) in enumerate(((hi_l, hi_r), (hi_l, lo_r), (lo_l, hi_r))):
                        last = nc.tensor.matmul(out, l(k), r(k), start=start and k == 0 and m == 0,
                                                stop=k == KT - 1 and m == 2)
                return last

            def transpose_xn(i, k, bank):
                need(pe, xn_ready, i, 1, k)
                for kt in range(KT):
                    for t in range(TT):
                        last = nc.tensor.transpose(bank[:, kt, t * P:(t + 1) * P], xn[:, t, kt * P:(kt + 1) * P],
                                                   ident[:])
                last.then_inc(xt_done, 1)

            def step(i, c):
                h = c % H
                if live(i, c):
                    if h == 0:
                        need(pe, xt_lo_ready, i, 1, c // H + 1)
                    if h % 4 == 0:
                        pe.wait_ge(w_lo_ready, 3 * (h // 4 + 1))
                    need(pe, e_ready, i, H, c - 1)
                    for j in range(2):
                        last = product(qk_ps[c % 2][:, j],
                                       lambda k: w_hi[j][:, k, h * HD:(h + 1) * HD],
                                       lambda k: w_lo[j][:, k, h * HD:(h + 1) * HD],
                                       lambda k: xt_hi[:, k], lambda k: xt_lo[:, k])
                    last.then_inc(qk_done, 1)
                if live(i, c) and h % 2 == 0:
                    need(pe, v_ready, i, H // 2, c // 2)
                    need(pe, pt_ready, i, H // 2, c // 2 - 1)
                    for t in range(TT):
                        last = product(v_ps[:, t * 256:(t + 1) * 256],
                                       lambda k: xt_hi[:, k, t * P:(t + 1) * P],
                                       lambda k: xt_lo[:, k, t * P:(t + 1) * P],
                                       lambda k: w_hi[2][:, k, h * HD:(h + 2) * HD],
                                       lambda k: w_lo[2][:, k, h * HD:(h + 2) * HD])
                    last.then_inc(v_done, 1)
                if live(i, c + 1) and h == H - 1:
                    need(pe, e_ready, i, H, c)
                    transpose_xn(i, c // H + 2, qk_ps[0])
                n = c - 1
                if live(i, n):
                    need(pe, qk_copied, i, H, n + 1)
                    if n % 2 == 0:
                        need(pe, sc_ready, i, H // 2, n // 2)
                    for b in range(T // BS):
                        s0 = (n % 2) * 2 * BS + (b % 2) * BS
                        last = nc.tensor.matmul(sc_ps[(b // 2) * BS:(b // 2 + 1) * BS, s0:s0 + BS],
                                                qk[:, n % 2, 0, b * BS:(b + 1) * BS],
                                                qk[:, n % 2, 1, b * BS:(b + 1) * BS], start=True, stop=True)
                    last.then_inc(sc_done, 1)
                n = c - 2
                if live(i, n):
                    need(pe, phi_ready, i, H, n + 1)
                    need(pe, at_ready, i, H, n)
                    nc.tensor.matmul(at_ps[:, 0:T], phi[:, n % 2, 1, 0:P], phi[:, n % 2, 0, :],
                                     start=True, stop=True)
                    nc.tensor.matmul(at_ps[:, T:T + P], phi[:, n % 2, 1, P:T], phi[:, n % 2, 0, P:T],
                                     start=True, stop=True).then_inc(at_done, 1)
                if c % 2 == 1 and live(i, c - 3):
                    need(pe, prob_ready, i, H // 2, (c - 3) // 2 + 1)
                    if live(i, c - 1):
                        need(pe, v_ready, i, H // 2, (c - 1) // 2 + 1)
                    for h2 in range(2):
                        last = nc.tensor.transpose(v_ps[:, h2 * P:(h2 + 1) * P], prob[:, 2 * h2:2 * h2 + 2, :],
                                                   ident[:])
                    last.then_inc(pt_done, 1)
                n = c - 3
                if live(i, n):
                    need(pe, at_ready, i, H, n + 1)
                    need(pe, v_ready, i, H // 2, n // 2 + 1)
                    need(pe, num_scaled, i, H, n)
                    v = v_ext[:, (n // 2) % VB]
                    nc.tensor.matmul(num_ps[:, 0:HD + 2], at[:, n % 2, 0:P], v[:, 0, n % 2, :], start=True, stop=True)
                    nc.tensor.matmul(num_ps[:, HD + 2:2 * HD + 4], at[:, n % 2, P:T], v[:, 0, n % 2, :],
                                     start=True, stop=False)
                    nc.tensor.matmul(num_ps[:, HD + 2:2 * HD + 4], at[:, n % 2, T:T + P], v[:, 1, n % 2, :],
                                     start=False, stop=True).then_inc(num_done, 1)
                n = c - 5
                if live(i, n):
                    need(pe, o_ready, i, H, n + 1)
                    for t in range(TT):
                        last = nc.tensor.transpose(lo_ps[:, T + t * P:T + (t + 1) * P], o[:, n % 2, t, :], ident[:])
                    last.then_inc(ot_done, 1)
                n = c - 6
                if live(i, n):
                    need(pe, ot_ready, i, H, n + 1)
                    if n % H == 0:
                        pe.wait_ge(wo_loaded, 16)
                        need(pe, y_sum, i, 1, n // H)
                    for t in range(TT):
                        last = nc.tensor.matmul(wo_ps[:, t], ot[:, n % 2, t * P:(t + 1) * P], wo[:, n % H],
                                                start=n % H == 0 and t == 0, stop=n % H == H - 1,
                                                skip_group_check=True)
                    last.then_inc(wo_done, 1)
                n = c - 4
                if live(i, n):
                    need(pe, pt_ready, i, H // 2, n // 2 + 1)
                    need(pe, v_ready, i, H // 2, n // 2 + 1)
                    need(pe, ot_ready, i, H, n)
                    for t in range(TT):
                        last = nc.tensor.matmul(lo_ps[:, t * P:(t + 1) * P], pt[:, (n // 2) % 2, n % 2, t],
                                                v_ext[:, (n // 2) % VB, t, n % 2, 0:HD], start=True, stop=True)
                    last.then_inc(loc_done, 1)

            def boot(eng):
                eng.wait_ge(masks_ready, 3)
                transpose_xn(0, 1, qk_ps[0])

            run(pe, boot, step)

        @block.scalar
        def _(act):
            def split_weights(g):
                for m in range(3 * g, 3 * g + 3):
                    act.wait_ge(stage_loaded[m % 2], 16 * (m // 2 + 1))
                    nc.scalar.copy(w_hi[m % 3][:, :, g * 512:(g + 1) * 512], w_stage[:, m % 2]).then_inc(w_hi_ready, 1)

            def split_xt(i, k, n):
                need(act, xt_done, i, 1, k)
                need(act, qk_done, i, H, n)
                need(act, v_done, i, H // 2, n // 2)
                nc.scalar.copy(xt_hi[:], qk_ps[0][:]).then_inc(xt_hi_ready, 1)

            def step(i, c):
                h = c % H
                if isinstance(i, int) and i == 0 and c in (1, 3, 5):
                    split_weights((c + 1) // 2)
                if live(i, c):
                    need(act, qk_done, i, H, c + 1)
                    need(act, sc_done, i, H, c - 1)
                    nc.scalar.copy(qk[:, c % 2], qk_ps[c % 2][:]).then_inc(qk_copied, 1)
                    need(act, phi_joined, i, H, c)
                    nc.scalar.activation(ez[:], qk_ps[c % 2][:], ACT.Exp, bias=phi_b[:, h:h + 1],
                                         scale=phi_s[:, h:h + 1]).then_inc(e_ready, 1)
                if live(i, c + 1) and h == H - 1:
                    split_xt(i, c // H + 2, c + 1)
                if c % 2 == 0 and live(i, c - 2):
                    need(act, sc_ready, i, H // 2, c // 2)
                    need(act, prob_ready, i, H // 2, c // 2 - 1)
                    nc.scalar.activation(pexp[:], sc[:], ACT.Exp, scale=SCALING).then_inc(p_exp, 1)
                if c % 2 == 1 and live(i, c - 3):
                    p = (c - 3) // 2
                    need(act, pt_done, i, H // 2, p + 1)
                    need(act, loc_done, i, H, 2 * p - 2)
                    src = v_ps[:, 0:2 * P].rearrange("p (h t c) -> p h t c", h=2, t=2)
                    for r in range(2):
                        q = slice(r * BS, (r + 1) * BS)
                        last = nc.scalar.copy(pt[q, p % 2, :, :, r * BS:(r + 1) * BS], src[q])
                    last.then_inc(pt_ready, 1)
                n = c - 3
                if live(i, n):
                    need(act, rden_ready, i, H, n + 1)
                    need(act, o_ready, i, H, n - 1)
                    for t in range(TT):
                        last = nc.scalar.activation(num[:, n % 2, t], num_ps[:, t * (HD + 2):t * (HD + 2) + HD],
                                                    ACT.Copy, scale=rden[:, n % 2, t:t + 1])
                    last.then_inc(num_scaled, 1)

            def boot(eng):
                split_weights(0)
                split_xt(0, 1, 0)
                act.wait_ge(consts_loaded, 48)

            run(act, boot, step)

        @block.vector
        def _(dve):
            def split_weights(g):
                for m in range(3 * g, 3 * g + 3):
                    dve.wait_ge(w_hi_ready, m + 1)
                    cols = slice(g * 512, (g + 1) * 512)
                    nc.vector.tensor_tensor(w_lo[m % 3][:, :, cols], w_stage[:, m % 2],
                                            w_hi[m % 3][:, :, cols].bitcast(F32), ALU.subtract).then_inc(w_lo_ready, 1)

            def layer_norm(i, k):
                need(dve, xln_loaded, i, 16, 16 * k)
                for t in range(TT):
                    nc.vector.bn_stats(stats[:, t], x_ln[:, t]).then_inc(ln_stats, 1)
                need(dve, ln_stats, i, TT, TT * k)
                nc.vector.tensor_copy(stats_count[:], stats[:, :, 0])
                for t in range(TT):
                    nc.vector.bn_aggr(mv[:, t], stats[:, t]).then_inc(ln_mv, 1)
                need(dve, ln_mv, i, TT, TT * k)
                nc.vector.tensor_scalar(var_eps[:], mv[:, :, 1], LN_EPS, None, ALU.add).then_inc(ln_var, 1)
                need(dve, ln_rstd, i, 1, k)
                need(dve, xt_done, i, 1, k - 1)
                for t in range(TT):
                    last = nc.vector.tensor_scalar(xn[:, t], x_ln[:, t], mv[:, t, 0:1], rstd[:, t:t + 1],
                                                   ALU.subtract, ALU.mult)
                last.then_inc(xn_ready, 1)

            def split_xt(i, k):
                need(dve, xt_hi_ready, i, 1, k)
                nc.vector.tensor_tensor(xt_lo[:], qk_ps[0][:], xt_hi[:].bitcast(F32), ALU.subtract)\
                  .then_inc(xt_lo_ready, 1)

            def step(i, c):
                h = c % H
                if isinstance(i, int) and i == 0 and c in (1, 3, 5):
                    split_weights((c + 1) // 2)
                if live(i, c) and h % 2 == 0:
                    p = c // 2
                    need(dve, v_done, i, H // 2, p + 1)
                    need(dve, loc_done, i, H, 2 * (p - VB + 1))
                    need(dve, num_done, i, H, 2 * (p - VB + 1))
                    nc.vector.tensor_copy(v_ext[:, p % VB, :, :, 0:HD],
                                          v_ps[:].rearrange("p (t h d) -> p t h d", t=TT, h=2)).then_inc(v_ready, 1)
                if live(i, c):
                    need(dve, qk_copied, i, H, c + 1)
                    nc.vector.tensor_scalar(z1[:], qk[:, c % 2], phi_s[:, h:h + 1], phi_b1[:, h:h + 1],
                                            ALU.mult, ALU.add).then_inc(z1_ready, 1)
                    need(dve, e_ready, i, H, c + 1)
                    need(dve, z1_ready, i, H, c + 1)
                    nc.vector.scalar_tensor_tensor(phi_raw[:, c % 2], ez[:], 1.0, z1[:], ALU.min, ALU.max)\
                      .then_inc(phi_joined, 1)
                    need(dve, phi_joined, i, H, c + 1)
                    need(dve, at_done, i, H, c - 1)
                    nc.vector.tensor_scalar(phi[:, c % 2], phi_raw[:, c % 2], PHI_TOP, None, ALU.min)\
                      .then_inc(phi_ready, 1)
                if live(i, c + 1) and h == H - 1:
                    split_xt(i, c // H + 2)
                if c % 2 == 0 and live(i, c - 2):
                    p = (c - 2) // 2
                    need(dve, sc_done, i, H, c)
                    src = sc_ps[:, 0:4 * BS].rearrange("p (g s) -> p g s", g=4)
                    nc.vector.reduce_max(rmax[:], src, AX_X).then_inc(max_ready, 1)
                    need(dve, max_ready, i, H // 2, p + 1)
                    need(dve, p_exp, i, H // 2, p)
                    nc.vector.tensor_tensor(sc[:], src, rmax[:].unsqueeze(2).broadcast_to([P, 4, BS]), ALU.subtract)\
                      .then_inc(sc_ready, 1)
                n = c - 2
                if live(i, n):
                    need(dve, at_done, i, H, n + 1)
                    need(dve, num_done, i, H, n - 1)
                    nc.vector.tensor_tensor(at[:, n % 2], at_ps[:, 0:T + P], at_mask[:], ALU.mult).then_inc(at_ready, 1)
                n = c - 3
                if live(i, n):
                    need(dve, num_done, i, H, n + 1)
                    nc.vector.tensor_scalar(den[:], num_ps[:, HD:HD + 2 + HD + 1:HD + 2], DEN_EPS, None, ALU.max)\
                      .then_inc(den_ready, 1)
                    need(dve, den_ready, i, H, n + 1)
                    need(dve, num_scaled, i, H, n - 1)
                    nc.vector.reciprocal(rden[:, n % 2], den[:]).then_inc(rden_ready, 1)
                n = c - 5
                if live(i, n):
                    need(dve, ot_done, i, H, n + 1)
                    need(dve, wo_done, i, H, n - 1)
                    nc.vector.tensor_copy(ot[:, n % 2], lo_ps[:, T:2 * T]).then_inc(ot_ready, 1)
                n = c - 6
                if live(i, n) and n % H == H - 1:
                    k = n // H + 1
                    need(dve, wo_done, i, H, n + 1)
                    need(dve, xres_loaded, i, 16, 16 * k)
                    nc.vector.tensor_tensor(y[:], wo_ps[:], x_res[:], ALU.add).then_inc(y_sum, 1)
                    need(dve, y_sum, i, 1, k)
                    nc.vector.tensor_tensor(y[:], y[:], bo_bc[:].unsqueeze(1).broadcast_to([P, TT, D]), ALU.add)\
                      .then_inc(y_ready, 1)
                n = c - 4
                if live(i, n):
                    need(dve, loc_done, i, H, n + 1)
                    need(dve, num_scaled, i, H, n + 1)
                    need(dve, ot_done, i, H, n - 1)
                    nc.vector.tensor_tensor(o[:, n % 2], lo_ps[:, 0:T].rearrange("p (t d) -> p t d", t=TT),
                                            num[:, n % 2], ALU.add).then_inc(o_ready, 1)
                if c % 2 == 0 and live(i, c - 2):
                    p = (c - 2) // 2
                    need(dve, p_exp, i, H // 2, p + 1)
                    nc.vector.reduce_sum(rsum[:], pexp[:], AX_X).then_inc(sum_ready, 1)
                    need(dve, sum_ready, i, H // 2, p + 1)
                    nc.vector.reciprocal(rinv[:], rsum[:]).then_inc(inv_ready, 1)
                    need(dve, inv_ready, i, H // 2, p + 1)
                    need(dve, pt_done, i, H // 2, p)
                    nc.vector.tensor_tensor(prob[:], pexp[:], rinv[:].unsqueeze(2).broadcast_to([P, 4, BS]), ALU.mult)\
                      .then_inc(prob_ready, 1)
                if h == 10 and live(i, c - h + H):
                    layer_norm(i, c // H + 2)

            def boot(eng):
                layer_norm(0, 1)
                split_weights(0)
                dve.wait_ge(consts_loaded, 48)
                nc.vector.tensor_scalar(phi_b1[:], phi_b[:], 1.0, None, ALU.add).then_inc(masks_ready, 1)
                dve.wait_ge(masks_ready, 4)
                dve.wait_ge(mem_zeroed, 5 + 4 * VB)
                split_xt(0, 1)

            run(dve, boot, step)


FI = 704
IT = -(-FI // P)
FR = FI - (IT - 1) * P
G = 512
GT = G // P
NG = B * T // G
TURN = 2 * IT


def rows(t):
    return P if t < IT - 1 else FR


class FfnWeights:

    def __init__(self, nc, ctx):
        def sb(name, shape, dt=F32):
            return ctx.enter_context(nc.sbuf_tensor("f_" + name, shape, dt))

        self.gate_hi = sb("gate_hi", [P, KT, FI], F32R)
        self.gate_lo = sb("gate_lo", [P, KT, FI], F32R)
        self.up_hi = sb("up_hi", [P, KT, FI], F32R)
        self.up_lo = sb("up_lo", [P, KT, FI], F32R)
        self.down_hi = sb("down_hi", [P, IT, D], F32R)
        self.down_lo = sb("down_lo", [P, IT, D], F32R)
        self.gate_s = sb("gate_s", [P, IT])
        self.up_s = sb("up_s", [P, IT])
        self.down_s = sb("down_s", [P, D])
        self.ident = sb("ident", [P, P])


def prepare_ffn(nc, io, fw):
    with ExitStack() as ctx:
        def sb(name, shape, dt=F32):
            return ctx.enter_context(nc.sbuf_tensor("p_" + name, shape, dt))

        def sem(name):
            return ctx.enter_context(nc.semaphore("p_" + name))

        gate = sb("gate", [P, IT, D])
        up = sb("up", [P, IT, D])
        down = sb("down", [P, KT, FI])
        t_ps = [ctx.enter_context(nc.psum_tensor(f"p_t_ps{i}", [P, 512], F32)) for i in range(4)]
        gate_loaded, up_loaded, down_loaded = sem("gate_loaded"), sem("up_loaded"), sem("down_loaded")
        scales_loaded = sem("scales_loaded")
        ident_ready = sem("ident_ready")
        t_done, hi_ready, lo_ready = sem("t_done"), sem("hi_ready"), sem("lo_ready")
        NB = len(t_ps)

        pieces = []
        for nat, hi, lo, loaded in ((gate, fw.gate_hi, fw.gate_lo, gate_loaded), (up, fw.up_hi, fw.up_lo, up_loaded)):
            for k in range(KT):
                for t0, t1 in ((0, 4), (4, IT)):
                    ins = [(nat[0:rows(t), t, k * P:(k + 1) * P], (t - t0) * P, rows(t), P) for t in range(t0, t1)]
                    end = min(t1 * P, FI)
                    pieces.append((loaded, 32, ins, hi[:, k, t0 * P:end], lo[:, k, t0 * P:end], P, end - t0 * P))
        for t in range(IT):
            ins = [(down[:, k, t * P:t * P + rows(t)], k * P, P, rows(t)) for k in range(KT)]
            pieces.append((down_loaded, 16, ins, fw.down_hi[0:rows(t), t], fw.down_lo[0:rows(t), t], rows(t), D))

        block = ctx.enter_context(nc.Block())

        @block.sync
        def _(sp):
            cut = (IT - 1) * P
            for w, dst, loaded in ((io["f_gate_w"], gate, gate_loaded), (io["f_up_w"], up, up_loaded)):
                sp.dma_start(dst[:, 0:IT - 1], w[0:cut].rearrange("(t p) d -> p t d", p=P)).then_inc(loaded, 16)
                sp.dma_start(dst[0:FR, IT - 1], w[cut:FI]).then_inc(loaded, 16)
            sp.dma_start(down[:], io["f_down_w"].rearrange("(k p) n -> p k n", p=P)).then_inc(down_loaded, 16)
            for s, dst in ((io["f_gate_s"], fw.gate_s), (io["f_up_s"], fw.up_s)):
                sp.dma_start(dst[:, 0:IT - 1], s[0:cut].rearrange("(t p) -> p t", p=P),
                             allow_slow_non_contiguous=True).then_inc(scales_loaded, 16)
                sp.dma_start(dst[0:FR, IT - 1:IT], s[cut:FI].rearrange("(p a) -> p a", a=1))\
                  .then_inc(scales_loaded, 16)
            sp.dma_start(fw.down_s[:], io["f_down_s"].rearrange("(a n) -> a n", a=1).broadcast_to([P, D]))\
              .then_inc(scales_loaded, 16)
            sp.wait_ge(scales_loaded, 80)

        @block.gpsimd
        def _(pool):
            pool.memset(fw.ident[:], 0.0).then_inc(ident_ready, 1)
            pool.wait_ge(ident_ready, 1)
            pool.affine_select(out=fw.ident[:], in_=fw.ident[:], compare_op=ALU.not_equal, fill=1.0, base=0,
                               pattern=[[-1, P]], channel_multiplier=1).then_inc(ident_ready, 1)

        @block.tensor
        def _(pe):
            pe.wait_ge(ident_ready, 2)
            for m, (loaded, count, ins, hi, lo, r, cols) in enumerate(pieces):
                pe.wait_ge(loaded, count)
                if m >= NB:
                    pe.wait_ge(lo_ready, m - NB + 1)
                for src, at, kin, kout in ins:
                    last = nc.tensor.transpose(t_ps[m % NB][0:kout, at:at + kin], src, fw.ident[0:kin, 0:kin])
                last.then_inc(t_done, 1)

        @block.scalar
        def _(act):
            for m, (loaded, count, ins, hi, lo, r, cols) in enumerate(pieces):
                act.wait_ge(t_done, m + 1)
                nc.scalar.copy(hi, t_ps[m % NB][0:r, 0:cols]).then_inc(hi_ready, 1)

        @block.vector
        def _(dve):
            for m, (loaded, count, ins, hi, lo, r, cols) in enumerate(pieces):
                dve.wait_ge(hi_ready, m + 1)
                nc.vector.tensor_tensor(lo, t_ps[m % NB][0:r, 0:cols], hi.bitcast(F32), ALU.subtract)\
                  .then_inc(lo_ready, 1)


def ffn(nc, name, fw, x_in, x_out):
    LAG = 6
    with ExitStack() as ctx:
        def sb(n, shape, dt=F32):
            return ctx.enter_context(nc.sbuf_tensor(name + n, shape, dt))

        def ps(n, shape):
            return ctx.enter_context(nc.psum_tensor(name + n, shape, F32))

        def sem(n):
            return ctx.enter_context(nc.semaphore(name + n))

        x = sb("x", [P, 2, GT, D])
        y = sb("y", [P, 2, GT, D])
        xn = sb("xn", [P, GT, D])
        stats = sb("stats", [P, GT, 6])
        stats_count = sb("stats_count", [P, GT])
        mv = sb("mv", [P, GT, 2])
        var_eps = sb("var_eps", [P, GT])
        half = sb("half", [P, GT])
        rstd = sb("rstd", [P, GT])
        xt_hi = sb("xt_hi", [P, 2, KT, G], F32R)
        xt_lo = sb("xt_lo", [P, 2, KT, G], F32R)
        act_g = sb("act_g", [P, 2, G])
        hid = sb("hid", [P, 2, G])
        hid_hi = sb("hid_hi", [P, 2, G], F32R)
        hid_lo = sb("hid_lo", [P, 2, G], F32R)

        gate_ps = [ps(f"gate_ps{i}", [P, G]) for i in range(2)]
        up_ps = [ps(f"up_ps{i}", [P, G]) for i in range(2)]
        xt_ps = [ps(f"xt_ps{k}", [P, G]) for k in range(KT)]
        down_ps = [ps(f"down_ps{i}", [P, 2, D]) for i in range(2)]

        x_loaded = [sem(f"x_loaded{i}") for i in range(2)]
        y_stored = [sem(f"y_stored{i}") for i in range(2)]
        half_ready = sem("half_ready")
        ln_stats, ln_mv, ln_var, ln_rstd = sem("ln_stats"), sem("ln_mv"), sem("ln_var"), sem("ln_rstd")
        xn_ready, xt_done, xt_hi_ready, xt_lo_ready = sem("xn_ready"), sem("xt_done"), sem("xt_hi_ready"), sem("xt_lo_ready")
        gate_up_done, silu_ready, hid_ready = sem("gate_up_done"), sem("silu_ready"), sem("hid_ready")
        hid_hi_ready, hid_lo_ready, down_done = sem("hid_hi_ready"), sem("hid_lo_ready"), sem("down_done")
        y_scaled, y_ready = sem("y_scaled"), sem("y_ready")

        block = ctx.enter_context(nc.Block())
        TURNS = NG // 2

        def run(eng, boot, step):
            boot(eng)
            for c in range(LAG):
                step(0, c)
            with eng.Fori(0, TURNS - 1) as i:
                for c in range(LAG, LAG + TURN):
                    step(i, c)
            for c in range(LAG, TURN + LAG):
                step(TURNS - 1, c)

        def live(i, n):
            return not isinstance(i, int) or 0 <= TURN * i + n < IT * NG

        def tokens(x_dram, g):
            return x_dram.rearrange("b t d -> (b t) d")[g * G:(g + 1) * G].rearrange("(t p) d -> p t d", p=P)

        @block.sync
        def _(sp):
            sp.dma_start(x[:, 0], tokens(x_in, 0)).then_inc(x_loaded[0], 16)
            for g in range(NG):
                if g + 1 < NG:
                    if g >= 1:
                        sp.wait_ge(y_ready, g)
                        sp.wait_ge(y_stored[(g + 1) % 2], 16 * ((g + 1) // 2))
                    sp.dma_start(x[:, (g + 1) % 2], tokens(x_in, g + 1)).then_inc(x_loaded[(g + 1) % 2], 16)
                sp.wait_ge(y_ready, g + 1)
                sp.dma_start(tokens(x_out, g), y[:, g % 2]).then_inc(y_stored[g % 2], 16)
            for s in y_stored:
                sp.wait_ge(s, 16 * (NG // 2))

        @block.gpsimd
        def _(pool):
            pool.memset(half[:], -0.5).then_inc(half_ready, 1)
            pool.wait_ge(half_ready, 1)

            def power(i, k):
                need(pool, ln_var, i, 1, k)
                pool.tensor_tensor(rstd[:], var_eps[:], half[:], ALU.pow).then_inc(ln_rstd, 1)

            power(0, 1)
            with pool.Fori(0, NG - 1) as i:
                power(i, 2)

        @block.tensor
        def _(pe):
            def transpose_xn(i, k):
                need(pe, xn_ready, i, 2, k)
                need(pe, xt_lo_ready, i, 2, k - 1)
                for kt in range(KT):
                    for t in range(GT):
                        last = nc.tensor.transpose(xt_ps[kt][:, t * P:(t + 1) * P], xn[:, t, kt * P:(kt + 1) * P],
                                                   fw.ident[:])
                last.then_inc(xt_done, 1)

            def step(i, c):
                t = c % IT
                if t == IT - 1 and live(i, c - t + IT):
                    transpose_xn(i, c // IT + 2)
                if live(i, c):
                    g = (c // IT) % 2
                    cols = slice(t * P, t * P + rows(t))
                    if t == 0:
                        need(pe, xt_lo_ready, i, 2, c // IT + 1)
                    need(pe, hid_ready, i, TURN, c - 1)
                    for out, w_hi, w_lo in ((gate_ps, fw.gate_hi, fw.gate_lo), (up_ps, fw.up_hi, fw.up_lo)):
                        for k in range(KT):
                            for m, (l, r) in enumerate(((w_hi, xt_hi), (w_hi, xt_lo), (w_lo, xt_hi))):
                                last = nc.tensor.matmul(out[c % 2][0:rows(t)], l[:, k, cols], r[:, g, k],
                                                        start=k == 0 and m == 0, stop=k == KT - 1 and m == 2)
                    last.then_inc(gate_up_done, 1)
                n = c - 2
                if live(i, n):
                    u = n % IT
                    need(pe, hid_lo_ready, i, TURN, n + 1)
                    if u == 0:
                        need(pe, y_scaled, i, 2, n // IT)
                    for j in range(GT):
                        for m, (l, r) in enumerate(((hid_hi, fw.down_hi), (hid_hi, fw.down_lo), (hid_lo, fw.down_hi))):
                            last = nc.tensor.matmul(down_ps[j // 2][:, j % 2], l[0:rows(u), n % 2, j * P:(j + 1) * P],
                                                    r[0:rows(u), u], start=u == 0 and m == 0 and j % 2 == 0,
                                                    stop=u == IT - 1 and m == 2, skip_group_check=True)
                    last.then_inc(down_done, 1)

            def boot(eng):
                transpose_xn(0, 1)

            run(pe, boot, step)

        @block.scalar
        def _(act):
            def split_xt(i, k, par):
                need(act, xt_done, i, 2, k)
                need(act, gate_up_done, i, TURN, (k - 2) * IT)
                for kt in range(KT):
                    last = nc.scalar.copy(xt_hi[:, par, kt], xt_ps[kt][:])
                last.then_inc(xt_hi_ready, 1)

            def step(i, c):
                t = c % IT
                if t == IT - 1 and live(i, c - t + IT):
                    split_xt(i, c // IT + 2, (c // IT + 1) % 2)
                if live(i, c):
                    need(act, gate_up_done, i, TURN, c + 1)
                    need(act, hid_ready, i, TURN, c - 1)
                    nc.scalar.activation(act_g[0:rows(t), c % 2], gate_ps[c % 2][0:rows(t)], ACT.Silu,
                                         scale=fw.gate_s[0:rows(t), t:t + 1]).then_inc(silu_ready, 1)
                n = c - 1
                if live(i, n):
                    need(act, hid_ready, i, TURN, n + 1)
                    need(act, down_done, i, TURN, n - 1)
                    nc.scalar.copy(hid_hi[0:rows(n % IT), n % 2], hid[0:rows(n % IT), n % 2]).then_inc(hid_hi_ready, 1)

            def boot(eng):
                split_xt(0, 1, 0)

            run(act, boot, step)

        @block.vector
        def _(dve):
            def layer_norm(i, k, par):
                need(dve, x_loaded[par], i, 16, 16 * ((k + 1) // 2))
                for t in range(GT):
                    nc.vector.bn_stats(stats[:, t], x[:, par, t]).then_inc(ln_stats, 1)
                need(dve, ln_stats, i, 2 * GT, GT * k)
                nc.vector.tensor_copy(stats_count[:], stats[:, :, 0])
                for t in range(GT):
                    nc.vector.bn_aggr(mv[:, t], stats[:, t]).then_inc(ln_mv, 1)
                need(dve, ln_mv, i, 2 * GT, GT * k)
                nc.vector.tensor_scalar(var_eps[:], mv[:, :, 1], LN_EPS, None, ALU.add).then_inc(ln_var, 1)
                need(dve, ln_rstd, i, 2, k)
                need(dve, xt_done, i, 2, k - 1)
                for t in range(GT):
                    last = nc.vector.tensor_scalar(xn[:, t], x[:, par, t], mv[:, t, 0:1], rstd[:, t:t + 1],
                                                   ALU.subtract, ALU.mult)
                last.then_inc(xn_ready, 1)

            def split_xt(i, k, par):
                need(dve, xt_hi_ready, i, 2, k)
                for kt in range(KT):
                    last = nc.vector.tensor_tensor(xt_lo[:, par, kt], xt_ps[kt][:], xt_hi[:, par, kt].bitcast(F32),
                                                   ALU.subtract)
                last.then_inc(xt_lo_ready, 1)

            def step(i, c):
                t = c % IT
                if t == IT - 1 and live(i, c - t + IT):
                    split_xt(i, c // IT + 2, (c // IT + 1) % 2)
                if live(i, c):
                    need(dve, silu_ready, i, TURN, c + 1)
                    need(dve, hid_lo_ready, i, TURN, c - 1)
                    nc.vector.scalar_tensor_tensor(hid[0:rows(t), c % 2], up_ps[c % 2][0:rows(t)],
                                                   fw.up_s[0:rows(t), t:t + 1], act_g[0:rows(t), c % 2],
                                                   ALU.mult, ALU.mult).then_inc(hid_ready, 1)
                n = c - 1
                if live(i, n):
                    r = rows(n % IT)
                    need(dve, hid_hi_ready, i, TURN, n + 1)
                    nc.vector.tensor_tensor(hid_lo[0:r, n % 2], hid[0:r, n % 2], hid_hi[0:r, n % 2].bitcast(F32),
                                            ALU.subtract).then_inc(hid_lo_ready, 1)
                n = c - 2
                if live(i, n) and n % IT == IT - 1:
                    k = n // IT + 1
                    par = (n // IT) % 2
                    need(dve, down_done, i, TURN, n + 1)
                    for j in range(2):
                        last = nc.vector.tensor_tensor(y[:, par, 2 * j:2 * j + 2], down_ps[j][:],
                                                       fw.down_s[:].unsqueeze(1).broadcast_to([P, 2, D]), ALU.mult)
                    last.then_inc(y_scaled, 1)
                    need(dve, y_scaled, i, 2, k)
                    nc.vector.tensor_tensor(y[:, par], y[:, par], x[:, par], ALU.add).then_inc(y_ready, 1)
                if t == 3 and live(i, c - t + IT):
                    layer_norm(i, c // IT + 2, (c // IT + 1) % 2)

            def boot(eng):
                layer_norm(0, 1, 0)
                split_xt(0, 1, 0)

            run(dve, boot, step)


BH = 16
DK = 8
DV = 16
VH = DV // DK
KD = BH * DK
VD = BH * DV
LR = 16
B_EPS = 1e-5
GATE_NORM = 16.0


def attention_b(nc, io, fw, x_in, x_out):
    LAG = 7
    TURN = 4
    TURNS = (B - 1 - LAG) // TURN
    with ExitStack() as ctx:
        def sb(n, shape, dt=F32):
            return ctx.enter_context(nc.sbuf_tensor("b_" + n, shape, dt))

        def ps(n, shape):
            return ctx.enter_context(nc.psum_tensor("b_" + n, shape, F32))

        def sem(n):
            return ctx.enter_context(nc.semaphore("b_" + n))

        CQ, CK, CV, CG, CR, CN = 0, KD, 2 * KD, 2 * KD + VD, 2 * KD + 2 * VD, 2 * KD + 2 * VD + LR
        kv = sb("kv", [P, 4, DV, T])
        state = sb("state", [P, 2, DV, T])
        w_hi = sb("w_hi", [P, KT, CN], F32R)
        w_lo = sb("w_lo", [P, KT, CN], F32R)
        wo_hi = sb("wo_hi", [P, VH, D], F32R)
        wo_lo = sb("wo_lo", [P, VH, D], F32R)
        gk2 = sb("gk2", [LR, KD])
        bgk2 = sb("bgk2", [P, 1])
        norm_w = sb("norm_w", [P, VH])
        one = sb("one", [P, 1])
        head_of = sb("head_of", [P, BH])
        sum_keys = sb("sum_keys", [P, DK, BH, DK])
        mean_vals = sb("mean_vals", [P, BH, DK])
        x_ln = sb("x_ln", [P, TT, D])
        x_res = sb("x_res", [P, TT, D])
        y = sb("y", [P, TT, D])
        xn = sb("xn", [P, TT, D])
        stats = sb("stats", [P, TT, 6])
        stats_count = sb("stats_count", [P, TT])
        mv = sb("mv", [P, TT, 2])
        var_eps = sb("var_eps", [P, TT])
        half = sb("half", [P, T])
        rstd = sb("rstd", [P, TT])
        xt_hi = sb("xt_hi", [P, KT, T], F32R)
        xt_lo = sb("xt_lo", [P, KT, T], F32R)
        q = sb("q", [P, 4, T])
        k_ = sb("k", [P, 4, T])
        v = sb("v", [P, VH, T])
        gk1 = sb("gk1", [LR, T])
        z = sb("z", [P, T])
        z_abs = sb("z_abs", [P, T])
        e_abs = sb("e_abs", [P, T])
        ln1 = sb("ln1", [P, T])
        log_sig = sb("log_sig", [P, T])
        decay = sb("decay", [P, 4, T])
        eg = sb("eg", [P, VH, T])
        swish = sb("swish", [P, 4, VH, T])
        o_sq = sb("o_sq", [P, VH, T])
        ms = sb("ms", [P, T])
        rms = sb("rms", [P, T])
        on = sb("on", [P, VH, T])
        o_hi = sb("o_hi", [P, VH, T], F32R)
        o_lo = sb("o_lo", [P, VH, T], F32R)
        w_stage = kv[:, 0].rearrange("p v t -> p (v t)")[:, 0:KT * CN].rearrange("p (k n) -> p k n", k=KT)
        wo_stage = kv[:, 1, 0:VH, :]

        def weight_parts(w):
            gates = w_stage[:, :, CG:CR].rearrange("p k (h a v) -> p k h a v", h=BH, a=VH)
            parts = [(w_stage[:, :, 0:CG], w[:, :, 0:CG]), (w_stage[:, :, CR:CN], w[:, :, CR:CN])]
            for a in range(VH):
                parts.append((gates[:, :, :, a], w[:, :, CG + a * P:CG + (a + 1) * P]
                              .rearrange("p k (h v) -> p k h v", h=BH)))
            return parts

        xt_ps, kq_ps, v_ps, g_ps, gk_ps = (ps(n, [P, 2, T]) for n in ("xt_ps", "kq_ps", "v_ps", "g_ps", "gk_ps"))
        o_ps, ms_ps, y_ps = (ps(n, [P, 2, T]) for n in ("o_ps", "ms_ps", "y_ps"))

        w_loaded, consts_loaded, xln_loaded, xres_loaded = (sem(n) for n in
                                                            ("w_loaded", "consts_loaded", "xln_loaded", "xres_loaded"))
        v_stored, y_stored = sem("v_stored"), sem("y_stored")
        v_spread = [sem(f"v_spread{i}") for i in range(4)]
        consts_set, masks_set, sel_set = sem("consts_set"), sem("masks_set"), sem("sel_set")
        w_hi_ready, w_lo_ready = sem("w_hi_ready"), sem("w_lo_ready")
        ln_stats, ln_mv, ln_var, ln_rstd, xn_ready = (sem(n) for n in
                                                      ("ln_stats", "ln_mv", "ln_var", "ln_rstd", "xn_ready"))
        xt_done, xt_hi_ready, xt_lo_ready = sem("xt_done"), sem("xt_hi_ready"), sem("xt_lo_ready")
        gk1_done, kq_done, v_done, g_done, gk2_done = (sem(n) for n in
                                                       ("gk1_done", "kq_done", "v_done", "g_done", "gk2_done"))
        o_done, ms_done, y_done = sem("o_done"), sem("ms_done"), sem("y_done")
        gk1_ready, k_ready, q_ready, v_ready, eg_ready = (sem(n) for n in
                                                          ("gk1_ready", "k_ready", "q_ready", "v_ready", "eg_ready"))
        z_ready, abs_ready, e_ready, ln_ready, ls_ready, decay_ready = (
            sem(n) for n in ("z_ready", "abs_ready", "e_ready", "ln_ready", "ls_ready", "decay_ready"))
        eg1_ready, sig_ready, swish_ready = sem("eg1_ready"), sem("sig_ready"), sem("swish_ready")
        kv_ready, state_ready, qs_ready = sem("kv_ready"), sem("state_ready"), sem("qs_ready")
        sq_ready, ms_ready, rms_ready, on_ready, og_ready, o_hi_ready, o_lo_ready, y_ready = (
            sem(n) for n in ("sq_ready", "ms_ready", "rms_ready", "on_ready", "og_ready", "o_hi_ready", "o_lo_ready",
                             "y_ready"))

        v_dram = nc.dram_tensor("b_values", (B, VD, T), F32, kind="Internal").ap()
        block = ctx.enter_context(nc.Block())

        def run(eng, boot, step):
            boot(eng)
            for c in range(LAG):
                step(0, c)
            with eng.Fori(0, TURNS) as i:
                for c in range(LAG, LAG + TURN):
                    step(i, c)
            for c in range(LAG, B - TURN * TURNS + 3):
                step(TURNS, c)

        def live(i, n):
            return not isinstance(i, int) or 0 <= TURN * i + n < B

        @block.sync
        def _(sp):
            def tiles(x_dram, b):
                return x_dram[b].rearrange("(t p) d -> p t d", p=P)

            sp.dma_start(x_ln[:], tiles(x_in, 0)).then_inc(xln_loaded, 16)
            for n, c0, c1 in (("Wq", CQ, CK), ("Wk", CK, CV), ("Wv", CV, CG), ("Wg", CG, CR), ("Wgk1", CR, CN)):
                sp.dma_start(w_stage[:, :, c0:c1], io["b_" + n].rearrange("(k p) n -> p k n", p=P)).then_inc(w_loaded, 16)
            for h in range(BH):
                at = slice(h * DK, (h + 1) * DK)
                sp.dma_start(wo_stage[at], io["b_Wo"][h * DV:(h + 1) * DV].rearrange("(a v) n -> v a n", a=VH))\
                  .then_inc(w_loaded, 16)
                sp.dma_start(norm_w[at], io["b_norm_w"].rearrange("(a v) -> v a", a=VH),
                             allow_slow_non_contiguous=True).then_inc(consts_loaded, 16)
            sp.dma_start(gk2[:], io["b_Wgk2"]).then_inc(consts_loaded, 16)
            sp.dma_start(bgk2[:], io["b_bgk2"].rearrange("(p a) -> p a", a=1)).then_inc(consts_loaded, 16)
            sp.wait_ge(w_lo_ready, 5)
            for c in range(B + 3):
                if c + 1 < B:
                    sp.wait_ge(xn_ready, c + 1)
                    sp.dma_start(x_ln[:], tiles(x_in, c + 1)).then_inc(xln_loaded, 16)
                if c < B:
                    sp.wait_ge(v_ready, c + 1)
                    sp.dma_start(v_dram[c].rearrange("(a p) t -> p a t", p=P), v[:]).then_inc(v_stored, 16)
                    sp.wait_ge(v_stored, 16 * (c + 1))
                    if c >= 4:
                        sp.wait_ge(state_ready, DV * (c - 3))
                    for h in range(BH):
                        src = v_dram[c, h * DV:(h + 1) * DV].rearrange("(a v) t -> a (v t)", a=1)
                        sp.dma_start(kv[h * DK:(h + 1) * DK, c % 4].rearrange("p v t -> p (v t)"),
                                     src.broadcast_to([DK, DV * T])).then_inc(v_spread[c % 4], 16)
                n = c - 3
                if n >= 0:
                    if n >= 1:
                        sp.wait_ge(y_ready, n)
                        sp.wait_ge(y_stored, 16 * n)
                    sp.dma_start(x_res[:], tiles(x_in, n)).then_inc(xres_loaded, 16)
                    sp.wait_ge(y_ready, n + 1)
                    sp.dma_start(tiles(x_out, n), y[:]).then_inc(y_stored, 16)
            sp.wait_ge(y_stored, 16 * B)

        @block.gpsimd
        def _(pool):
            pool.memset(half[:], -0.5).then_inc(consts_set, 1)
            pool.memset(one[:], 1.0).then_inc(consts_set, 1)
            pool.memset(head_of[:], 1.0).then_inc(consts_set, 1)
            pool.wait_ge(consts_set, 3)
            pool.affine_select(out=head_of[:], in_=head_of[:], compare_op=ALU.is_ge, fill=0.0, base=0,
                               pattern=[[-DK, BH]], channel_multiplier=1).then_inc(masks_set, 1)
            pool.wait_ge(masks_set, 1)
            pool.affine_select(out=head_of[:], in_=head_of[:], compare_op=ALU.is_ge, fill=0.0, base=DK - 1,
                               pattern=[[DK, BH]], channel_multiplier=-1).then_inc(masks_set, 1)

            def power(i, k):
                need(pool, ln_var, i, TURN, k)
                pool.tensor_tensor(rstd[:], var_eps[:], half[:, 0:TT], ALU.pow).then_inc(ln_rstd, 1)

            def step(i, c):
                n = c - 1
                if live(i, n):
                    need(pool, k_ready, i, TURN, n + 1)
                    need(pool, v_spread[n % 4], i, 16 * BH, 16 * BH * (n // 4 + 1))
                    pool.tensor_tensor(kv[:, n % 4], kv[:, n % 4], k_[:, n % 4].unsqueeze(1).broadcast_to([P, DV, T]),
                                       ALU.mult).then_inc(kv_ready, 1)
                if live(i, c + 1):
                    power(i, c + 2)
                n = c - 3
                if live(i, n):
                    need(pool, ms_ready, i, TURN, n + 1)
                    need(pool, on_ready, i, TURN, n)
                    pool.tensor_tensor(rms[:], ms[:], half[:], ALU.pow).then_inc(rms_ready, 1)
                n = c - 2
                if live(i, n):
                    need(pool, state_ready, i, DV * TURN, DV * (n + 1))
                    need(pool, q_ready, i, TURN, n + 1)
                    pool.tensor_tensor(state[:, n % 2], state[:, n % 2],
                                       q[:, n % 4].unsqueeze(1).broadcast_to([P, DV, T]), ALU.mult).then_inc(qs_ready, 1)

            def boot(eng):
                power(0, 1)

            run(pool, boot, step)

        @block.tensor
        def _(pe):
            def project(out, c0, m=P):
                for k in range(KT):
                    for j, (l, r) in enumerate(((w_hi, xt_hi), (w_hi, xt_lo), (w_lo, xt_hi))):
                        last = nc.tensor.matmul(out, l[:, k, c0:c0 + m], r[:, k], start=k == 0 and j == 0,
                                                stop=k == KT - 1 and j == 2)
                return last

            def transpose_xn(i, k):
                need(pe, xn_ready, i, TURN, k)
                need(pe, xt_lo_ready, i, TURN, k - 1)
                for kt in range(KT):
                    for t in range(TT):
                        last = nc.tensor.transpose(xt_ps[:, kt, t * P:(t + 1) * P], xn[:, t, kt * P:(kt + 1) * P],
                                                   fw.ident[:])
                last.then_inc(xt_done, 1)

            def step(i, c):
                if live(i, c):
                    need(pe, xt_lo_ready, i, TURN, c + 1)
                    need(pe, decay_ready, i, TURN, c)
                    need(pe, k_ready, i, TURN, c)
                    need(pe, q_ready, i, TURN, c)
                    need(pe, v_ready, i, TURN, c)
                    need(pe, swish_ready, i, TURN, c)
                    project(gk_ps[0:LR, 0], CR, LR).then_inc(gk1_done, 1)
                    project(kq_ps[:, 1], CQ)
                    project(kq_ps[:, 0], CK).then_inc(kq_done, 1)
                    for a in range(VH):
                        last = project(v_ps[:, a], CV + a * P)
                    last.then_inc(v_done, 1)
                    need(pe, gk1_ready, i, TURN, c + 1)
                    nc.tensor.matmul(gk_ps[:, 1], gk2[:], gk1[:], start=True, stop=True).then_inc(gk2_done, 1)
                    for a in range(VH):
                        last = project(g_ps[:, a], CG + a * P)
                    last.then_inc(g_done, 1)
                n = c - 3
                if live(i, n):
                    need(pe, qs_ready, i, TURN, n + 1)
                    need(pe, on_ready, i, TURN, n)
                    for m in range(DV):
                        last = nc.tensor.matmul(o_ps[:, m // DK], sum_keys[:, m % DK], state[:, n % 2, m],
                                                start=m % DK == 0, stop=m % DK == DK - 1)
                    last.then_inc(o_done, 1)
                if live(i, c + 1):
                    transpose_xn(i, c + 2)
                if live(i, n):
                    need(pe, sq_ready, i, TURN, n + 1)
                    need(pe, ms_ready, i, TURN, n)
                    for a in range(VH):
                        last = nc.tensor.matmul(ms_ps[:, 0], mean_vals[:], o_sq[:, a], start=a == 0, stop=a == VH - 1)
                    last.then_inc(ms_done, 1)
                    need(pe, o_lo_ready, i, TURN, n + 1)
                    need(pe, y_ready, i, TURN, n)
                    for t in range(TT):
                        rows_t = slice(t * P, (t + 1) * P)
                        for a in range(VH):
                            for m, (l, r) in enumerate(((o_hi, wo_hi), (o_hi, wo_lo), (o_lo, wo_hi))):
                                last = nc.tensor.matmul(y_ps[:, t], l[:, a, rows_t], r[:, a], start=a == 0 and m == 0,
                                                        stop=a == VH - 1 and m == 2)
                    last.then_inc(y_done, 1)

            def boot(eng):
                pe.wait_ge(sel_set, 3)
                pe.wait_ge(consts_loaded, 16 * (BH + 2))
                pe.wait_ge(w_lo_ready, 5)
                transpose_xn(0, 1)

            run(pe, boot, step)

        @block.scalar
        def _(act):
            def split_xt(i, k):
                need(act, xt_done, i, TURN, k)
                need(act, g_done, i, TURN, k - 1)
                nc.scalar.copy(xt_hi[:], xt_ps[:]).then_inc(xt_hi_ready, 1)

            def step(i, c):
                if live(i, c):
                    split_xt(i, c + 1)
                    need(act, gk1_done, i, TURN, c + 1)
                    nc.scalar.copy(gk1[:], gk_ps[0:LR, 0]).then_inc(gk1_ready, 1)
                    need(act, kq_done, i, TURN, c + 1)
                    need(act, kv_ready, i, TURN, c - 3)
                    nc.scalar.copy(k_[:, c % 4], kq_ps[:, 0]).then_inc(k_ready, 1)
                    need(act, qs_ready, i, TURN, c - 3)
                    nc.scalar.mul(q[:, c % 4], kq_ps[:, 1], float(DK) ** -0.5).then_inc(q_ready, 1)
                    need(act, v_done, i, TURN, c + 1)
                    need(act, v_stored, i, 16 * TURN, 16 * c)
                    nc.scalar.copy(v[:], v_ps[:]).then_inc(v_ready, 1)
                    need(act, gk2_done, i, TURN, c + 1)
                    need(act, ls_ready, i, TURN, c)
                    nc.scalar.activation(z[:], gk_ps[:, 1], ACT.Identity, bias=bgk2[:]).then_inc(z_ready, 1)
                    need(act, g_done, i, TURN, c + 1)
                    need(act, swish_ready, i, TURN, c)
                    nc.scalar.activation(eg[:], g_ps[:], ACT.Exp, scale=-1.0).then_inc(eg_ready, 1)
                n = c - 3
                if live(i, n):
                    need(act, o_done, i, TURN, n + 1)
                    nc.scalar.activation(o_sq[:], o_ps[:], ACT.Square).then_inc(sq_ready, 1)
                if live(i, c):
                    need(act, abs_ready, i, TURN, c + 1)
                    nc.scalar.activation(e_abs[:], z_abs[:], ACT.Exp, scale=-1.0).then_inc(e_ready, 1)
                    need(act, e_ready, i, TURN, c + 1)
                    nc.scalar.activation(ln1[:], e_abs[:], ACT.Ln, bias=one[:]).then_inc(ln_ready, 1)
                    need(act, ls_ready, i, TURN, c + 1)
                    need(act, state_ready, i, DV * TURN, DV * (c - 3))
                    nc.scalar.activation(decay[:, c % 4], log_sig[:], ACT.Exp, scale=1.0 / GATE_NORM)\
                      .then_inc(decay_ready, 1)
                n = c - 3
                if live(i, n):
                    need(act, og_ready, i, TURN, n + 1)
                    nc.scalar.copy(o_hi[:], on[:]).then_inc(o_hi_ready, 1)

            def boot(eng):
                act.wait_ge(w_loaded, 16 * (5 + BH))
                for staged, hi in weight_parts(w_hi):
                    nc.scalar.copy(hi, staged).then_inc(w_hi_ready, 1)
                nc.scalar.copy(wo_hi[:], wo_stage).then_inc(w_hi_ready, 1)
                act.wait_ge(consts_set, 3)
                act.wait_ge(consts_loaded, 16 * (BH + 2))

            run(act, boot, step)

        @block.vector
        def _(dve):
            def layer_norm(i, k):
                need(dve, xln_loaded, i, 16 * TURN, 16 * k)
                for t in range(TT):
                    nc.vector.bn_stats(stats[:, t], x_ln[:, t]).then_inc(ln_stats, 1)
                need(dve, ln_stats, i, TT * TURN, TT * k)
                nc.vector.tensor_copy(stats_count[:], stats[:, :, 0])
                for t in range(TT):
                    nc.vector.bn_aggr(mv[:, t], stats[:, t]).then_inc(ln_mv, 1)
                need(dve, ln_mv, i, TT * TURN, TT * k)
                nc.vector.tensor_scalar(var_eps[:], mv[:, :, 1], LN_EPS, None, ALU.add).then_inc(ln_var, 1)

            def normalise(i, k):
                need(dve, ln_rstd, i, TURN, k)
                need(dve, xt_done, i, TURN, k - 1)
                for t in range(TT):
                    last = nc.vector.tensor_scalar(xn[:, t], x_ln[:, t], mv[:, t, 0:1], rstd[:, t:t + 1],
                                                   ALU.subtract, ALU.mult)
                last.then_inc(xn_ready, 1)

            def step(i, c):
                if live(i, c):
                    need(dve, xt_hi_ready, i, TURN, c + 1)
                    nc.vector.tensor_tensor(xt_lo[:], xt_ps[:], xt_hi[:].bitcast(F32), ALU.subtract)\
                      .then_inc(xt_lo_ready, 1)
                if live(i, c + 1):
                    layer_norm(i, c + 2)
                n = c - 2
                if live(i, n):
                    need(dve, kv_ready, i, TURN, n + 1)
                    need(dve, decay_ready, i, TURN, n + 1)
                    need(dve, o_done, i, TURN, n - 1)
                    for m in range(DV):
                        nc.vector.tensor_tensor_scan(state[:, n % 2, m], decay[:, n % 4], kv[:, n % 4, m], 0.0,
                                                     ALU.mult, ALU.add).then_inc(state_ready, 1)
                if live(i, c + 1):
                    normalise(i, c + 2)
                n = c - 3
                if live(i, n):
                    need(dve, ms_done, i, TURN, n + 1)
                    nc.vector.tensor_scalar(ms[:], ms_ps[:, 0], B_EPS, None, ALU.add).then_inc(ms_ready, 1)
                if live(i, c):
                    need(dve, z_ready, i, TURN, c + 1)
                    nc.vector.scalar_tensor_tensor(z_abs[:], z[:], -1.0, z[:], ALU.mult, ALU.max).then_inc(abs_ready, 1)
                    need(dve, eg_ready, i, TURN, c + 1)
                    nc.vector.tensor_scalar(eg[:], eg[:], 1.0, None, ALU.add).then_inc(eg1_ready, 1)
                    need(dve, eg1_ready, i, TURN, c + 1)
                    nc.vector.reciprocal(eg[:], eg[:]).then_inc(sig_ready, 1)
                    need(dve, ln_ready, i, TURN, c + 1)
                    nc.vector.scalar_tensor_tensor(log_sig[:], z[:], 0.0, ln1[:], ALU.min, ALU.subtract)\
                      .then_inc(ls_ready, 1)
                    need(dve, sig_ready, i, TURN, c + 1)
                    nc.vector.tensor_tensor(swish[:, c % 4], g_ps[:], eg[:], ALU.mult).then_inc(swish_ready, 1)
                n = c - 3
                if live(i, n):
                    need(dve, rms_ready, i, TURN, n + 1)
                    need(dve, o_lo_ready, i, TURN, n)
                    for a in range(VH):
                        last = nc.vector.scalar_tensor_tensor(on[:, a], o_ps[:, a], norm_w[:, a:a + 1], rms[:],
                                                              ALU.mult, ALU.mult)
                    last.then_inc(on_ready, 1)
                    need(dve, on_ready, i, TURN, n + 1)
                    nc.vector.tensor_tensor(on[:], on[:], swish[:, n % 4], ALU.mult).then_inc(og_ready, 1)
                    need(dve, o_hi_ready, i, TURN, n + 1)
                    nc.vector.tensor_tensor(o_lo[:], on[:], o_hi[:].bitcast(F32), ALU.subtract).then_inc(o_lo_ready, 1)
                    need(dve, y_done, i, TURN, n + 1)
                    need(dve, xres_loaded, i, 16 * TURN, 16 * (n + 1))
                    nc.vector.tensor_tensor(y[:], y_ps[:], x_res[:], ALU.add).then_inc(y_ready, 1)

            def boot(eng):
                dve.wait_ge(masks_set, 2)
                nc.vector.memset(sum_keys[:], 0.0).then_inc(sel_set, 1)
                nc.vector.tensor_scalar(mean_vals[:], head_of[:].unsqueeze(2).broadcast_to([P, BH, DK]), 1.0 / DV, None,
                                        ALU.mult).then_inc(sel_set, 1)
                dve.wait_ge(sel_set, 2)
                for m in range(DK):
                    last = nc.vector.tensor_copy(sum_keys[:, m, :, m], head_of[:])
                last.then_inc(sel_set, 1)
                dve.wait_ge(w_hi_ready, 5)
                for (staged, lo), (_, hi) in zip(weight_parts(w_lo), weight_parts(w_hi)):
                    nc.vector.tensor_tensor(lo, staged, hi.bitcast(F32), ALU.subtract).then_inc(w_lo_ready, 1)
                nc.vector.tensor_tensor(wo_lo[:], wo_stage, wo_hi[:].bitcast(F32), ALU.subtract).then_inc(w_lo_ready, 1)
                dve.wait_ge(consts_loaded, 16 * (BH + 2))
                layer_norm(0, 1)
                normalise(0, 1)

            run(dve, boot, step)


def build(nc, io, x_in, out, stages=4):
    x1 = nc.dram_tensor("x1", (B, T, D), F32, kind="Internal").ap() if stages > 1 else out
    x2 = nc.dram_tensor("x2", (B, T, D), F32, kind="Internal").ap() if stages > 2 else out
    x3 = nc.dram_tensor("x3", (B, T, D), F32, kind="Internal").ap() if stages > 3 else out
    attention_a(nc, io, x_in, x1)
    if stages > 1:
        with ExitStack() as ctx:
            fw = FfnWeights(nc, ctx)
            prepare_ffn(nc, io, fw)
            ffn(nc, "f1_", fw, x1, x2)
            if stages > 2:
                attention_b(nc, io, fw, x2, x3)
            if stages > 3:
                ffn(nc, "f2_", fw, x3, out)


_PRE = {"L0_attn_a_": "", "L0_attn_b_": "b_", "L0_ffn_": "f_"}


def kernel(**inputs):
    import numpy as _np
    import concourse.bacc as _bacc
    from concourse import mybir as _mybir
    from concourse.bass_utils import run_bass_kernel_spmd as _run

    nc = _bacc.Bacc("TRN2", target_bir_lowering=False, num_devices=1)
    arrays, io = {}, {}
    for name, array in inputs.items():
        a = _np.ascontiguousarray(array)
        arrays[f"in_{name}_dram"] = a
        short = name
        for long, pre in _PRE.items():
            if name.startswith(long):
                short = pre + name[len(long):]
        io[short] = nc.dram_tensor(f"in_{name}_dram", a.shape, _mybir.dt.from_np(a.dtype), kind="ExternalInput").ap()
    out = nc.dram_tensor("out_0_dram", (B, T, D), _mybir.dt.float32, kind="ExternalOutput").ap()
    build(nc, io, io["x"], out, stages=4)
    r = _run(nc, [arrays], core_ids=[0])
    return r.results[0]["out_0_dram"]
```

```python
from contextlib import ExitStack

import concourse.bass as bass
from concourse import mybir

F32 = mybir.dt.float32
F32R = mybir.dt.float32r
ALU = mybir.AluOpType
ACT = mybir.ActivationFunctionType
AX_X = mybir.AxisListType.X

P = 128
B = 16
T = 256
D = 256
TT = T // P
KT = D // P
H = 16
HD = 128
BS = 64
SCALING = float(HD) ** -0.5
LN_EPS = 1e-5
DEN_EPS = 1e-6
PHI_TOP = 10.0
VB = 4
LAG = 8


def value(i, rate, k):
    if isinstance(i, int):
        v = i * rate + k
        return v if v > 0 else None
    assert k > 0
    return i * rate + k


def need(eng, sem, i, rate, k):
    v = value(i, rate, k)
    if v is not None:
        eng.wait_ge(sem, v)


def attention_a(nc, io, x_in, x_out):
    with ExitStack() as ctx:
        def sb(name, shape, dt=F32):
            return ctx.enter_context(nc.sbuf_tensor("a_" + name, shape, dt))

        def ps(name, shape):
            return ctx.enter_context(nc.psum_tensor("a_" + name, shape, F32))

        def sem(name):
            return ctx.enter_context(nc.semaphore("a_" + name))

        w_hi = [sb(f"w{n}_hi", [P, KT, H * HD], F32R) for n in "qkv"]
        w_lo = [sb(f"w{n}_lo", [P, KT, H * HD], F32R) for n in "qkv"]
        wo_hi = sb("wo_hi", [P, H, D], F32R)
        wo_lo = sb("wo_lo", [P, H, D], F32R)
        w_stage = sb("w_stage", [P, 2, KT, 4 * HD])
        phi_s = sb("phi_s", [P, H])
        phi_b = sb("phi_b", [P, H])
        phi_b1 = sb("phi_b1", [P, H])
        bo_bc = sb("bo_bc", [P, D])
        ident = sb("ident", [P, P])
        ones = sb("ones", [P, P])
        at_mask = sb("at_mask", [P, T + P])
        x_ln = sb("x_ln", [P, TT, D])
        x_res = sb("x_res", [P, TT, D])
        y = sb("y", [P, TT, D])
        xn = sb("xn", [P, TT, D])
        stats = sb("stats", [P, TT, 6])
        stats_count = sb("stats_count", [P, TT])
        mv = sb("mv", [P, TT, 2])
        var_eps = sb("var_eps", [P, TT])
        half = sb("half", [P, TT])
        rstd = sb("rstd", [P, TT])
        xt_hi = sb("xt_hi", [P, KT, T], F32R)
        xt_lo = sb("xt_lo", [P, KT, T], F32R)
        qk = sb("qk", [P, 2, 2, T])
        ez = sb("ez", [P, 2, 2, T])
        z1 = sb("z1", [P, 2, 2, T])
        phi_raw = sb("phi_raw", [P, 2, T])
        phi_hi = sb("phi_hi", [P, 2, 2, T], F32R)
        phi_lo = sb("phi_lo", [P, 2, 2, T], F32R)
        v_ext = sb("v_ext", [P, VB, TT, 2, HD + 2])
        rmax = sb("rmax", [P, 4])
        sc = sb("sc", [P, 4, BS])
        pexp = sb("pexp", [P, 4, BS])
        rsum = sb("rsum", [P, 4])
        rinv = sb("rinv", [P, 4])
        prob = sb("prob", [P, 4, BS])
        pt = sb("pt", [P, 2, 2, TT, P])
        at = sb("at", [P, 2, T + P])
        den = sb("den", [P, TT])
        rden = sb("rden", [P, 2, TT])
        num = sb("num", [P, 2, TT, HD])
        o = sb("o", [P, 2, TT, HD])
        ot_hi = sb("ot_hi", [P, 2, T], F32R)
        ot_lo = sb("ot_lo", [P, 2, T], F32R)

        qk_ps = [ps(f"qk_ps{i}", [P, 2, T]) for i in range(2)]
        v_ps = ps("v_ps", [P, 512])
        sc_ps = ps("sc_ps", [P, 512])
        at_ps = ps("at_ps", [P, 512])
        num_ps = ps("num_ps", [P, 512])
        lo_ps = ps("lo_ps", [P, 512])
        wo_ps = ps("wo_ps", [P, TT, D])

        consts_loaded = sem("consts_loaded")
        stage_loaded = [sem(f"stage_loaded{i}") for i in range(2)]
        xln_loaded = sem("xln_loaded")
        xres_loaded = sem("xres_loaded")
        y_stored = sem("y_stored")
        mem_zeroed = sem("mem_zeroed")
        masks_ready = sem("masks_ready")
        w_hi_ready = sem("w_hi_ready")
        w_lo_ready = sem("w_lo_ready")
        ln_stats = sem("ln_stats")
        ln_mv = sem("ln_mv")
        ln_var = sem("ln_var")
        ln_rstd = sem("ln_rstd")
        xn_ready = sem("xn_ready")
        xt_done = sem("xt_done")
        xt_hi_ready = sem("xt_hi_ready")
        xt_lo_ready = sem("xt_lo_ready")
        qk_done = sem("qk_done")
        v_done = sem("v_done")
        sc_done = sem("sc_done")
        at_done = sem("at_done")
        pt_done = sem("pt_done")
        num_done = sem("num_done")
        loc_done = sem("loc_done")
        ot_done = sem("ot_done")
        wo_done = sem("wo_done")
        qk_copied = sem("qk_copied")
        e_ready = sem("e_ready")
        p_exp = sem("p_exp")
        pt_ready = sem("pt_ready")
        num_scaled = sem("num_scaled")
        v_ready = sem("v_ready")
        z1_ready = sem("z1_ready")
        phi_joined = sem("phi_joined")
        phi_hi_ready = sem("phi_hi_ready")
        phi_ready = sem("phi_ready")
        max_ready = sem("max_ready")
        sc_ready = sem("sc_ready")
        sum_ready = sem("sum_ready")
        inv_ready = sem("inv_ready")
        prob_ready = sem("prob_ready")
        at_ready = sem("at_ready")
        den_ready = sem("den_ready")
        rden_ready = sem("rden_ready")
        ot_hi_ready = sem("ot_hi_ready")
        ot_ready = sem("ot_ready")
        o_ready = sem("o_ready")
        y_sum = sem("y_sum")
        y_ready = sem("y_ready")

        def wo_chunk(slot):
            return w_stage[:, slot].rearrange("p k n -> p (k n)").rearrange("p (h n) -> p h n", h=4)

        def chunk(m, w, w_o):
            g = m // 4
            if m % 4 < 3:
                return w_stage[:, m % 2], w[m % 4][:, :, g * 512:(g + 1) * 512]
            return wo_chunk(m % 2), w_o[:, 4 * g:4 * g + 4]

        CHUNKS_AT = ((4,), (5,), (6,), (7,), (8, 9), (10, 11), (12, 13), (14, 15))
        block = ctx.enter_context(nc.Block())

        def run(eng, boot, step):
            boot(eng)
            for c in range(LAG):
                step(0, c)
            with eng.Fori(0, B - 1) as i:
                for c in range(LAG, LAG + H):
                    step(i, c)
            for c in range(LAG, H + LAG):
                step(B - 1, c)

        def live(i, n):
            return not isinstance(i, int) or 0 <= H * i + n < B * H

        @block.sync
        def _(sp):
            sp.dma_start(x_ln[:], x_in[0].rearrange("(t p) d -> p t d", p=P)).then_inc(xln_loaded, 16)
            sp.dma_start(phi_s[:], io["phi_scale"].rearrange("h o k -> k (h o)"),
                         allow_slow_non_contiguous=True).then_inc(consts_loaded, 16)
            sp.dma_start(phi_b[:], io["phi_bias"].rearrange("h o k -> k (h o)"),
                         allow_slow_non_contiguous=True).then_inc(consts_loaded, 16)
            sp.dma_start(bo_bc[:], io["bo"].rearrange("(a n) -> a n", a=1).broadcast_to([P, D]))\
              .then_inc(consts_loaded, 16)
            for m in range(16):
                if m >= 2:
                    sp.wait_ge(w_lo_ready, m - 1)
                g = m // 4
                if m % 4 < 3:
                    src = io["W" + "qkv"[m % 4]].rearrange("(k p) n -> p k n", p=P)[:, :, g * 512:(g + 1) * 512]
                    dst = w_stage[:, m % 2]
                else:
                    src = io["Wo"].rearrange("(h p) n -> p h n", p=P)[:, 4 * g:4 * g + 4]
                    dst = wo_chunk(m % 2)
                sp.dma_start(dst, src).then_inc(stage_loaded[m % 2], 16)

            for b in range(B):
                if b + 1 < B:
                    sp.wait_ge(xn_ready, b + 1)
                    sp.dma_start(x_ln[:], x_in[b + 1].rearrange("(t p) d -> p t d", p=P)).then_inc(xln_loaded, 16)
                if b:
                    sp.wait_ge(y_sum, b)
                    sp.wait_ge(y_stored, 16 * b)
                sp.dma_start(x_res[:], x_in[b].rearrange("(t p) d -> p t d", p=P)).then_inc(xres_loaded, 16)
                sp.wait_ge(y_ready, b + 1)
                sp.dma_start(x_out[b].rearrange("(t p) d -> p t d", p=P), y[:]).then_inc(y_stored, 16)
            sp.wait_ge(y_stored, 16 * B)

        @block.gpsimd
        def _(pool):
            pool.memset(ident[:], 0.0).then_inc(mem_zeroed, 1)
            pool.memset(ones[:], 1.0).then_inc(mem_zeroed, 1)
            pool.memset(half[:], -0.5).then_inc(mem_zeroed, 1)
            pool.memset(at_mask[:], 1.0).then_inc(mem_zeroed, 1)
            pool.memset(pt[:], 0.0).then_inc(mem_zeroed, 1)
            for par in range(VB):
                for h2 in range(2):
                    pool.memset(v_ext[:, par, :, h2, HD:HD + 1], 1.0).then_inc(mem_zeroed, 1)
                    pool.memset(v_ext[:, par, :, h2, HD + 1:HD + 2], 0.0).then_inc(mem_zeroed, 1)
            pool.wait_ge(mem_zeroed, 5 + 4 * VB)
            pool.memset(at_mask[BS:P, 0:BS], 0.0).then_inc(masks_ready, 1)
            pool.memset(at_mask[BS:P, T:T + BS], 0.0).then_inc(masks_ready, 1)
            pool.wait_ge(masks_ready, 2)
            pool.affine_select(out=ident[:], in_=ident[:], compare_op=ALU.not_equal, fill=1.0, base=0,
                               pattern=[[-1, P]], channel_multiplier=1).then_inc(masks_ready, 1)

            def power(i, k):
                need(pool, ln_var, i, 1, k)
                pool.tensor_tensor(rstd[:], var_eps[:], half[:], ALU.pow).then_inc(ln_rstd, 1)

            pool.wait_ge(mem_zeroed, 3)
            power(0, 1)
            with pool.Fori(0, B - 1) as i:
                power(i, 2)

        @block.tensor
        def _(pe):
            def product(out, hi_l, lo_l, hi_r, lo_r, start=True):
                last = None
                for k in range(KT):
                    for m, (l, r) in enumerate(((hi_l, hi_r), (hi_l, lo_r), (lo_l, hi_r))):
                        last = nc.tensor.matmul(out, l(k), r(k), start=start and k == 0 and m == 0,
                                                stop=k == KT - 1 and m == 2)
                return last

            def transpose_xn(i, k, bank):
                need(pe, xn_ready, i, 1, k)
                for kt in range(KT):
                    for t in range(TT):
                        last = nc.tensor.transpose(bank[:, kt, t * P:(t + 1) * P], xn[:, t, kt * P:(kt + 1) * P],
                                                   ident[:])
                last.then_inc(xt_done, 1)

            def transpose_o(i, n):
                need(pe, o_ready, i, H, n + 1)
                for t in range(TT):
                    last = nc.tensor.transpose(lo_ps[:, T + t * P:T + (t + 1) * P], o[:, n % 2, t, :], ident[:])
                last.then_inc(ot_done, 1)

            def step(i, c):
                h = c % H
                if live(i, c):
                    if h == 0:
                        need(pe, xt_lo_ready, i, 1, c // H + 1)
                    if h % 4 == 0:
                        pe.wait_ge(w_lo_ready, h + 2)
                    need(pe, z1_ready, i, H, c - 1)
                    for j in range(2):
                        last = product(qk_ps[c % 2][:, j],
                                       lambda k: w_hi[j][:, k, h * HD:(h + 1) * HD],
                                       lambda k: w_lo[j][:, k, h * HD:(h + 1) * HD],
                                       lambda k: xt_hi[:, k], lambda k: xt_lo[:, k])
                    last.then_inc(qk_done, 1)
                if live(i, c) and h % 2 == 0:
                    need(pe, v_ready, i, H // 2, c // 2)
                    need(pe, pt_ready, i, H // 2, c // 2 - 1)
                    if h % 4 == 0:
                        pe.wait_ge(w_lo_ready, h + 3)
                    for t in range(TT):
                        last = product(v_ps[:, t * 256:(t + 1) * 256],
                                       lambda k: xt_hi[:, k, t * P:(t + 1) * P],
                                       lambda k: xt_lo[:, k, t * P:(t + 1) * P],
                                       lambda k: w_hi[2][:, k, h * HD:(h + 2) * HD],
                                       lambda k: w_lo[2][:, k, h * HD:(h + 2) * HD])
                    last.then_inc(v_done, 1)
                if c % 2 == 0 and live(i, c - 5):
                    transpose_o(i, c - 5)
                if live(i, c + 1) and h == H - 1:
                    need(pe, z1_ready, i, H, c)
                    transpose_xn(i, c // H + 2, qk_ps[0])
                n = c - 1
                if live(i, n):
                    need(pe, qk_copied, i, H, n + 1)
                    if n % 2 == 0:
                        need(pe, sc_ready, i, H // 2, n // 2)
                    for b in range(T // BS):
                        s0 = (n % 2) * 2 * BS + (b % 2) * BS
                        last = nc.tensor.matmul(sc_ps[(b // 2) * BS:(b // 2 + 1) * BS, s0:s0 + BS],
                                                qk[:, n % 2, 0, b * BS:(b + 1) * BS],
                                                qk[:, n % 2, 1, b * BS:(b + 1) * BS], start=True, stop=True)
                    last.then_inc(sc_done, 1)
                n = c - 2
                if live(i, n):
                    need(pe, phi_ready, i, H, n + 1)
                    need(pe, at_ready, i, H, n)
                    for out, keys, queries in ((slice(0, T), slice(0, P), slice(0, T)),
                                               (slice(T, T + P), slice(P, T), slice(P, T))):
                        for m, (l, r) in enumerate(((phi_hi, phi_hi), (phi_hi, phi_lo), (phi_lo, phi_hi))):
                            last = nc.tensor.matmul(at_ps[:, out], l[:, n % 2, 1, keys], r[:, n % 2, 0, queries],
                                                    start=m == 0, stop=m == 2)
                    last.then_inc(at_done, 1)
                if c % 2 == 1 and live(i, c - 5):
                    transpose_o(i, c - 5)
                if c % 2 == 1 and live(i, c - 3):
                    need(pe, prob_ready, i, H // 2, (c - 3) // 2 + 1)
                    if live(i, c - 1):
                        need(pe, v_ready, i, H // 2, (c - 1) // 2 + 1)
                    for h2 in range(2):
                        last = nc.tensor.transpose(v_ps[:, h2 * P:(h2 + 1) * P], prob[:, 2 * h2:2 * h2 + 2, :],
                                                   ident[:])
                    last.then_inc(pt_done, 1)
                n = c - 3
                if live(i, n):
                    need(pe, at_ready, i, H, n + 1)
                    need(pe, v_ready, i, H // 2, n // 2 + 1)
                    need(pe, num_scaled, i, H, n)
                    v = v_ext[:, (n // 2) % VB]
                    nc.tensor.matmul(num_ps[:, 0:HD + 2], at[:, n % 2, 0:P], v[:, 0, n % 2, :], start=True, stop=True)
                    nc.tensor.matmul(num_ps[:, HD + 2:2 * HD + 4], at[:, n % 2, P:T], v[:, 0, n % 2, :],
                                     start=True, stop=False)
                    nc.tensor.matmul(num_ps[:, HD + 2:2 * HD + 4], at[:, n % 2, T:T + P], v[:, 1, n % 2, :],
                                     start=False, stop=True).then_inc(num_done, 1)
                n = c - 6
                if live(i, n):
                    need(pe, ot_ready, i, H, n + 1)
                    if n % H == 0:
                        need(pe, y_sum, i, 1, n // H)
                    if n % 4 == 0:
                        pe.wait_ge(w_lo_ready, n % H + 4)
                    for t in range(TT):
                        for m, (l, r) in enumerate(((ot_hi, wo_hi), (ot_hi, wo_lo), (ot_lo, wo_hi))):
                            last = nc.tensor.matmul(wo_ps[:, t], l[:, n % 2, t * P:(t + 1) * P], r[:, n % H],
                                                    start=n % H == 0 and t == 0 and m == 0,
                                                    stop=n % H == H - 1 and m == 2, skip_group_check=True)
                    last.then_inc(wo_done, 1)
                n = c - 4
                if live(i, n):
                    need(pe, pt_ready, i, H // 2, n // 2 + 1)
                    need(pe, v_ready, i, H // 2, n // 2 + 1)
                    need(pe, ot_ready, i, H, n)
                    for t in range(TT):
                        last = nc.tensor.matmul(lo_ps[:, t * P:(t + 1) * P], pt[:, (n // 2) % 2, n % 2, t],
                                                v_ext[:, (n // 2) % VB, t, n % 2, 0:HD], start=True, stop=True)
                    last.then_inc(loc_done, 1)

            def boot(eng):
                eng.wait_ge(masks_ready, 3)
                transpose_xn(0, 1, qk_ps[0])

            run(pe, boot, step)

        @block.scalar
        def _(act):
            def split_weights(chunks):
                for m in chunks:
                    staged, hi = chunk(m, w_hi, wo_hi)
                    act.wait_ge(stage_loaded[m % 2], 16 * (m // 2 + 1))
                    nc.scalar.copy(hi, staged).then_inc(w_hi_ready, 1)

            def split_xt(i, k, n):
                need(act, xt_done, i, 1, k)
                need(act, qk_done, i, H, n)
                need(act, v_done, i, H // 2, n // 2)
                nc.scalar.copy(xt_hi[:], qk_ps[0][:]).then_inc(xt_hi_ready, 1)

            def step(i, c):
                h = c % H
                if isinstance(i, int) and i == 0:
                    split_weights(CHUNKS_AT[c])
                if live(i, c):
                    need(act, qk_done, i, H, c + 1)
                    need(act, sc_done, i, H, c - 1)
                    nc.scalar.copy(qk[:, c % 2], qk_ps[c % 2][:]).then_inc(qk_copied, 1)
                    need(act, phi_joined, i, H, c - 1)
                    nc.scalar.activation(ez[:, c % 2], qk_ps[c % 2][:], ACT.Exp, bias=phi_b[:, h:h + 1],
                                         scale=phi_s[:, h:h + 1]).then_inc(e_ready, 1)
                n = c - 5
                if live(i, n):
                    need(act, ot_done, i, H, n + 1)
                    need(act, wo_done, i, H, n - 1)
                    nc.scalar.copy(ot_hi[:, n % 2], lo_ps[:, T:2 * T]).then_inc(ot_hi_ready, 1)
                if live(i, c):
                    nc.scalar.activation(z1[:, c % 2], qk_ps[c % 2][:], ACT.Identity, bias=phi_b1[:, h:h + 1],
                                         scale=phi_s[:, h:h + 1]).then_inc(z1_ready, 1)
                if live(i, c + 1) and h == H - 1:
                    split_xt(i, c // H + 2, c + 1)
                if live(i, c) and h % 2 == 0:
                    p = c // 2
                    need(act, v_done, i, H // 2, p + 1)
                    need(act, loc_done, i, H, 2 * (p - VB + 1))
                    need(act, num_done, i, H, 2 * (p - VB + 1))
                    nc.scalar.copy(v_ext[:, p % VB, :, :, 0:HD],
                                   v_ps[:].rearrange("p (t h d) -> p t h d", t=TT, h=2)).then_inc(v_ready, 1)
                if c % 2 == 0 and live(i, c - 2):
                    need(act, sc_ready, i, H // 2, c // 2)
                    need(act, prob_ready, i, H // 2, c // 2 - 1)
                    nc.scalar.activation(pexp[:], sc[:], ACT.Exp, scale=SCALING).then_inc(p_exp, 1)
                if c % 2 == 1 and live(i, c - 3):
                    p = (c - 3) // 2
                    need(act, pt_done, i, H // 2, p + 1)
                    need(act, loc_done, i, H, 2 * p - 2)
                    src = v_ps[:, 0:2 * P].rearrange("p (h t c) -> p h t c", h=2, t=2)
                    for r in range(2):
                        q = slice(r * BS, (r + 1) * BS)
                        last = nc.scalar.copy(pt[q, p % 2, :, :, r * BS:(r + 1) * BS], src[q])
                    last.then_inc(pt_ready, 1)
                n = c - 3
                if live(i, n):
                    need(act, rden_ready, i, H, n + 1)
                    need(act, o_ready, i, H, n - 1)
                    for t in range(TT):
                        last = nc.scalar.activation(num[:, n % 2, t], num_ps[:, t * (HD + 2):t * (HD + 2) + HD],
                                                    ACT.Copy, scale=rden[:, n % 2, t:t + 1])
                    last.then_inc(num_scaled, 1)

            def boot(eng):
                act.wait_ge(mem_zeroed, 5 + 4 * VB)
                split_weights(range(4))
                split_xt(0, 1, 0)
                act.wait_ge(masks_ready, 4)

            run(act, boot, step)

        @block.vector
        def _(dve):
            def split_weights(chunks):
                for m in chunks:
                    staged, lo = chunk(m, w_lo, wo_lo)
                    dve.wait_ge(w_hi_ready, m + 1)
                    nc.vector.tensor_tensor(lo, staged, chunk(m, w_hi, wo_hi)[1].bitcast(F32), ALU.subtract)\
                      .then_inc(w_lo_ready, 1)

            def layer_norm(i, k):
                need(dve, xln_loaded, i, 16, 16 * k)
                for t in range(TT):
                    nc.vector.bn_stats(stats[:, t], x_ln[:, t]).then_inc(ln_stats, 1)
                need(dve, ln_stats, i, TT, TT * k)
                nc.vector.tensor_copy(stats_count[:], stats[:, :, 0])
                for t in range(TT):
                    nc.vector.bn_aggr(mv[:, t], stats[:, t]).then_inc(ln_mv, 1)
                need(dve, ln_mv, i, TT, TT * k)
                nc.vector.tensor_scalar(var_eps[:], mv[:, :, 1], LN_EPS, None, ALU.add).then_inc(ln_var, 1)

            def normalise(i, k):
                need(dve, ln_rstd, i, 1, k)
                need(dve, xt_done, i, 1, k - 1)
                for t in range(TT):
                    last = nc.vector.tensor_scalar(xn[:, t], x_ln[:, t], mv[:, t, 0:1], rstd[:, t:t + 1],
                                                   ALU.subtract, ALU.mult)
                last.then_inc(xn_ready, 1)

            def split_xt(i, k):
                need(dve, xt_hi_ready, i, 1, k)
                nc.vector.tensor_tensor(xt_lo[:], qk_ps[0][:], xt_hi[:].bitcast(F32), ALU.subtract)\
                  .then_inc(xt_lo_ready, 1)

            def step(i, c):
                h = c % H
                if isinstance(i, int) and i == 0:
                    split_weights(CHUNKS_AT[c])
                n = c - 5
                if live(i, n):
                    need(dve, loc_done, i, H, n + 1)
                    need(dve, num_scaled, i, H, n + 1)
                    need(dve, ot_done, i, H, n - 1)
                    nc.vector.tensor_tensor(o[:, n % 2], lo_ps[:, 0:T].rearrange("p (t d) -> p t d", t=TT),
                                            num[:, n % 2], ALU.add).then_inc(o_ready, 1)
                n = c - 1
                if live(i, n):
                    need(dve, e_ready, i, H, n + 1)
                    need(dve, z1_ready, i, H, n + 1)
                    need(dve, phi_ready, i, H, n)
                    nc.vector.scalar_tensor_tensor(phi_raw[:], ez[:, n % 2], 1.0, z1[:, n % 2], ALU.min, ALU.max)\
                      .then_inc(phi_joined, 1)
                    need(dve, phi_joined, i, H, n + 1)
                    need(dve, at_done, i, H, n - 1)
                    nc.vector.tensor_scalar(phi_hi[:, n % 2], phi_raw[:], PHI_TOP, None, ALU.min)\
                      .then_inc(phi_hi_ready, 1)
                    need(dve, phi_hi_ready, i, H, n + 1)
                    nc.vector.scalar_tensor_tensor(phi_lo[:, n % 2], phi_raw[:], PHI_TOP, phi_hi[:, n % 2].bitcast(F32),
                                                   ALU.min, ALU.subtract).then_inc(phi_ready, 1)
                if live(i, c + 1) and h == H - 1:
                    split_xt(i, c // H + 2)
                n = c - 5
                if live(i, n):
                    need(dve, ot_hi_ready, i, H, n + 1)
                    nc.vector.tensor_tensor(ot_lo[:, n % 2], lo_ps[:, T:2 * T], ot_hi[:, n % 2].bitcast(F32),
                                            ALU.subtract).then_inc(ot_ready, 1)
                if c % 2 == 0 and live(i, c - 2):
                    p = (c - 2) // 2
                    need(dve, sc_done, i, H, c)
                    src = sc_ps[:, 0:4 * BS].rearrange("p (g s) -> p g s", g=4)
                    nc.vector.reduce_max(rmax[:], src, AX_X).then_inc(max_ready, 1)
                    need(dve, max_ready, i, H // 2, p + 1)
                    need(dve, p_exp, i, H // 2, p)
                    nc.vector.tensor_tensor(sc[:], src, rmax[:].unsqueeze(2).broadcast_to([P, 4, BS]), ALU.subtract)\
                      .then_inc(sc_ready, 1)
                n = c - 2
                if live(i, n):
                    need(dve, at_done, i, H, n + 1)
                    need(dve, num_done, i, H, n - 1)
                    nc.vector.tensor_tensor(at[:, n % 2], at_ps[:, 0:T + P], at_mask[:], ALU.mult).then_inc(at_ready, 1)
                n = c - 3
                if live(i, n):
                    need(dve, num_done, i, H, n + 1)
                    nc.vector.tensor_scalar(den[:], num_ps[:, HD:HD + 2 + HD + 1:HD + 2], DEN_EPS, None, ALU.max)\
                      .then_inc(den_ready, 1)
                    need(dve, den_ready, i, H, n + 1)
                    need(dve, num_scaled, i, H, n - 1)
                    nc.vector.reciprocal(rden[:, n % 2], den[:]).then_inc(rden_ready, 1)
                n = c - 6
                if live(i, n) and n % H == H - 1:
                    k = n // H + 1
                    need(dve, wo_done, i, H, n + 1)
                    need(dve, xres_loaded, i, 16, 16 * k)
                    nc.vector.tensor_tensor(y[:], wo_ps[:], x_res[:], ALU.add).then_inc(y_sum, 1)
                    need(dve, y_sum, i, 1, k)
                    nc.vector.tensor_tensor(y[:], y[:], bo_bc[:].unsqueeze(1).broadcast_to([P, TT, D]), ALU.add)\
                      .then_inc(y_ready, 1)
                if c % 2 == 0 and live(i, c - 2):
                    p = (c - 2) // 2
                    need(dve, p_exp, i, H // 2, p + 1)
                    nc.vector.reduce_sum(rsum[:], pexp[:], AX_X).then_inc(sum_ready, 1)
                    need(dve, sum_ready, i, H // 2, p + 1)
                    nc.vector.reciprocal(rinv[:], rsum[:]).then_inc(inv_ready, 1)
                    need(dve, inv_ready, i, H // 2, p + 1)
                    need(dve, pt_done, i, H // 2, p)
                    nc.vector.tensor_tensor(prob[:], pexp[:], rinv[:].unsqueeze(2).broadcast_to([P, 4, BS]), ALU.mult)\
                      .then_inc(prob_ready, 1)
                if h == 9 and live(i, c - h + H):
                    layer_norm(i, c // H + 2)
                if h == 11 and live(i, c - h + H):
                    normalise(i, c // H + 2)

            def boot(eng):
                layer_norm(0, 1)
                normalise(0, 1)
                split_weights(range(4))
                dve.wait_ge(consts_loaded, 48)
                nc.vector.tensor_scalar(phi_b1[:], phi_b[:], 1.0, None, ALU.add).then_inc(masks_ready, 1)
                dve.wait_ge(masks_ready, 4)
                dve.wait_ge(mem_zeroed, 5 + 4 * VB)
                split_xt(0, 1)

            run(dve, boot, step)


FI = 704
IT = -(-FI // P)
FR = FI - (IT - 1) * P
G = 512
GT = G // P
NG = B * T // G
TURN = 2 * IT


def rows(t):
    return P if t < IT - 1 else FR


class FfnWeights:

    def __init__(self, nc, ctx):
        def sb(name, shape, dt=F32):
            return ctx.enter_context(nc.sbuf_tensor("f_" + name, shape, dt))

        self.gate_hi = sb("gate_hi", [P, KT, FI], F32R)
        self.gate_lo = sb("gate_lo", [P, KT, FI], F32R)
        self.up_hi = sb("up_hi", [P, KT, FI], F32R)
        self.up_lo = sb("up_lo", [P, KT, FI], F32R)
        self.down_hi = sb("down_hi", [P, IT, D], F32R)
        self.down_lo = sb("down_lo", [P, IT, D], F32R)
        self.gate_s = sb("gate_s", [P, IT])
        self.up_s = sb("up_s", [P, IT])
        self.down_s = sb("down_s", [P, D])
        self.ident = sb("ident", [P, P])
        self.nc, self.ctx, self.sems = nc, ctx, {}

    def sem(self, name):
        if name not in self.sems:
            self.sems[name] = self.ctx.enter_context(self.nc.semaphore("f_" + name))
        return self.sems[name]


def prepare_ffn(nc, io, fw):
    with ExitStack() as ctx:
        def sb(name, shape, dt=F32):
            return ctx.enter_context(nc.sbuf_tensor("p_" + name, shape, dt))

        def sem(name):
            return ctx.enter_context(nc.semaphore("p_" + name))

        gate = sb("gate", [P, IT, D])
        up = sb("up", [P, IT, D])
        down = sb("down", [P, KT, FI])
        t_ps = [ctx.enter_context(nc.psum_tensor(f"p_t_ps{i}", [P, 512], F32)) for i in range(4)]
        gate_loaded, up_loaded, down_loaded = sem("gate_loaded"), sem("up_loaded"), sem("down_loaded")
        scales_loaded = sem("scales_loaded")
        ident_ready = sem("ident_ready")
        t_done, hi_ready, lo_ready = sem("t_done"), sem("hi_ready"), sem("lo_ready")
        NB = len(t_ps)

        pieces = []
        for nat, hi, lo, loaded in ((gate, fw.gate_hi, fw.gate_lo, gate_loaded), (up, fw.up_hi, fw.up_lo, up_loaded)):
            for k in range(KT):
                for t0, t1 in ((0, 4), (4, IT)):
                    ins = [(nat[0:rows(t), t, k * P:(k + 1) * P], (t - t0) * P, rows(t), P) for t in range(t0, t1)]
                    end = min(t1 * P, FI)
                    pieces.append((loaded, 32, ins, hi[:, k, t0 * P:end], lo[:, k, t0 * P:end], P, end - t0 * P))
        for t in range(IT):
            ins = [(down[:, k, t * P:t * P + rows(t)], k * P, P, rows(t)) for k in range(KT)]
            pieces.append((down_loaded, 16, ins, fw.down_hi[0:rows(t), t], fw.down_lo[0:rows(t), t], rows(t), D))

        block = ctx.enter_context(nc.Block())

        @block.sync
        def _(sp):
            cut = (IT - 1) * P
            for w, dst, loaded in ((io["f_gate_w"], gate, gate_loaded), (io["f_up_w"], up, up_loaded)):
                sp.dma_start(dst[:, 0:IT - 1], w[0:cut].rearrange("(t p) d -> p t d", p=P)).then_inc(loaded, 16)
                sp.dma_start(dst[0:FR, IT - 1], w[cut:FI]).then_inc(loaded, 16)
            sp.dma_start(down[:], io["f_down_w"].rearrange("(k p) n -> p k n", p=P)).then_inc(down_loaded, 16)
            for s, dst in ((io["f_gate_s"], fw.gate_s), (io["f_up_s"], fw.up_s)):
                sp.dma_start(dst[:, 0:IT - 1], s[0:cut].rearrange("(t p) -> p t", p=P),
                             allow_slow_non_contiguous=True).then_inc(scales_loaded, 16)
                sp.dma_start(dst[0:FR, IT - 1:IT], s[cut:FI].rearrange("(p a) -> p a", a=1))\
                  .then_inc(scales_loaded, 16)
            sp.dma_start(fw.down_s[:], io["f_down_s"].rearrange("(a n) -> a n", a=1).broadcast_to([P, D]))\
              .then_inc(scales_loaded, 16)
            sp.wait_ge(scales_loaded, 80)

        @block.gpsimd
        def _(pool):
            pool.memset(fw.ident[:], 0.0).then_inc(ident_ready, 1)
            pool.wait_ge(ident_ready, 1)
            pool.affine_select(out=fw.ident[:], in_=fw.ident[:], compare_op=ALU.not_equal, fill=1.0, base=0,
                               pattern=[[-1, P]], channel_multiplier=1).then_inc(ident_ready, 1)

        @block.tensor
        def _(pe):
            pe.wait_ge(ident_ready, 2)
            for m, (loaded, count, ins, hi, lo, r, cols) in enumerate(pieces):
                pe.wait_ge(loaded, count)
                if m >= NB:
                    pe.wait_ge(lo_ready, m - NB + 1)
                for src, at, kin, kout in ins:
                    last = nc.tensor.transpose(t_ps[m % NB][0:kout, at:at + kin], src, fw.ident[0:kin, 0:kin])
                last.then_inc(t_done, 1)

        @block.scalar
        def _(act):
            for m, (loaded, count, ins, hi, lo, r, cols) in enumerate(pieces):
                act.wait_ge(t_done, m + 1)
                nc.scalar.copy(hi, t_ps[m % NB][0:r, 0:cols]).then_inc(hi_ready, 1)

        @block.vector
        def _(dve):
            for m, (loaded, count, ins, hi, lo, r, cols) in enumerate(pieces):
                dve.wait_ge(hi_ready, m + 1)
                nc.vector.tensor_tensor(lo, t_ps[m % NB][0:r, 0:cols], hi.bitcast(F32), ALU.subtract)\
                  .then_inc(lo_ready, 1)


def ffn(nc, name, fw, x_in, x_out):
    LAG = 6
    with ExitStack() as ctx:
        def sb(n, shape, dt=F32):
            return ctx.enter_context(nc.sbuf_tensor(name + n, shape, dt))

        def ps(n, shape):
            return ctx.enter_context(nc.psum_tensor(name + n, shape, F32))

        sem = fw.sem

        x = sb("x", [P, 2, GT, D])
        y = sb("y", [P, 2, GT, D])
        xn = sb("xn", [P, GT, D])
        stats = sb("stats", [P, GT, 6])
        stats_count = sb("stats_count", [P, GT])
        mv = sb("mv", [P, GT, 2])
        var_eps = sb("var_eps", [P, GT])
        half = sb("half", [P, GT])
        rstd = sb("rstd", [P, GT])
        xt_hi = sb("xt_hi", [P, 2, KT, G], F32R)
        xt_lo = sb("xt_lo", [P, 2, KT, G], F32R)
        act_g = sb("act_g", [P, 2, G])
        hid = sb("hid", [P, 2, G])
        hid_hi = sb("hid_hi", [P, 2, G], F32R)
        hid_lo = sb("hid_lo", [P, 2, G], F32R)

        gate_ps = [ps(f"gate_ps{i}", [P, G]) for i in range(2)]
        up_ps = [ps(f"up_ps{i}", [P, G]) for i in range(2)]
        xt_ps = [ps(f"xt_ps{k}", [P, G]) for k in range(KT)]
        down_ps = [ps(f"down_ps{i}", [P, 2, D]) for i in range(2)]

        x_loaded = [sem(f"x_loaded{i}") for i in range(2)]
        y_stored = [sem(f"y_stored{i}") for i in range(2)]
        half_ready = sem("half_ready")
        ln_stats, ln_mv, ln_var, ln_rstd = sem("ln_stats"), sem("ln_mv"), sem("ln_var"), sem("ln_rstd")
        xn_ready, xt_done, xt_hi_ready, xt_lo_ready = sem("xn_ready"), sem("xt_done"), sem("xt_hi_ready"), sem("xt_lo_ready")
        gate_up_done, silu_ready, hid_ready = sem("gate_up_done"), sem("silu_ready"), sem("hid_ready")
        hid_hi_ready, hid_lo_ready, down_done = sem("hid_hi_ready"), sem("hid_lo_ready"), sem("down_done")
        y_scaled, y_ready = sem("y_scaled"), sem("y_ready")

        block = ctx.enter_context(nc.Block())
        TURNS = NG // 2

        def run(eng, boot, step):
            boot(eng)
            for c in range(LAG):
                step(0, c)
            with eng.Fori(0, TURNS - 1) as i:
                for c in range(LAG, LAG + TURN):
                    step(i, c)
            for c in range(LAG, TURN + LAG):
                step(TURNS - 1, c)

        def live(i, n):
            return not isinstance(i, int) or 0 <= TURN * i + n < IT * NG

        def tokens(x_dram, g):
            return x_dram.rearrange("b t d -> (b t) d")[g * G:(g + 1) * G].rearrange("(t p) d -> p t d", p=P)

        @block.sync
        def _(sp):
            sp.dma_start(x[:, 0], tokens(x_in, 0)).then_inc(x_loaded[0], 16)
            for g in range(NG):
                if g + 1 < NG:
                    if g >= 1:
                        sp.wait_ge(y_ready, g)
                        if g >= 2:
                            sp.wait_ge(y_stored[g % 2], 16 * (g // 2))
                    sp.dma_start(x[:, (g + 1) % 2], tokens(x_in, g + 1)).then_inc(x_loaded[(g + 1) % 2], 16)
                sp.wait_ge(y_ready, g + 1)
                sp.dma_start(tokens(x_out, g), y[:, g % 2]).then_inc(y_stored[g % 2], 16)
            for s in y_stored:
                sp.wait_ge(s, 16 * (NG // 2))

        @block.gpsimd
        def _(pool):
            pool.memset(half[:], -0.5).then_inc(half_ready, 1)
            pool.wait_ge(half_ready, 1)

            def power(i, k):
                need(pool, ln_var, i, 1, k)
                pool.tensor_tensor(rstd[:], var_eps[:], half[:], ALU.pow).then_inc(ln_rstd, 1)

            power(0, 1)
            with pool.Fori(0, NG - 1) as i:
                power(i, 2)

        @block.tensor
        def _(pe):
            def transpose_xn(i, k):
                need(pe, xn_ready, i, 2, k)
                need(pe, xt_lo_ready, i, 2, k - 1)
                for kt in range(KT):
                    for t in range(GT):
                        last = nc.tensor.transpose(xt_ps[kt][:, t * P:(t + 1) * P], xn[:, t, kt * P:(kt + 1) * P],
                                                   fw.ident[:])
                last.then_inc(xt_done, 1)

            def step(i, c):
                t = c % IT
                if live(i, c):
                    g = (c // IT) % 2
                    cols = slice(t * P, t * P + rows(t))
                    if t == 0:
                        need(pe, xt_lo_ready, i, 2, c // IT + 1)
                    need(pe, hid_ready, i, TURN, c - 1)
                    for out, w_hi, w_lo in ((gate_ps, fw.gate_hi, fw.gate_lo), (up_ps, fw.up_hi, fw.up_lo)):
                        for k in range(KT):
                            for m, (l, r) in enumerate(((w_hi, xt_hi), (w_hi, xt_lo), (w_lo, xt_hi))):
                                last = nc.tensor.matmul(out[c % 2][0:rows(t)], l[:, k, cols], r[:, g, k],
                                                        start=k == 0 and m == 0, stop=k == KT - 1 and m == 2)
                    last.then_inc(gate_up_done, 1)
                if t == IT - 1 and live(i, c - t + IT):
                    transpose_xn(i, c // IT + 2)
                n = c - 2
                if live(i, n):
                    u = n % IT
                    need(pe, hid_lo_ready, i, TURN, n + 1)
                    if u == 0:
                        need(pe, y_scaled, i, 2, n // IT)
                    for j in range(GT):
                        for m, (l, r) in enumerate(((hid_hi, fw.down_hi), (hid_hi, fw.down_lo), (hid_lo, fw.down_hi))):
                            last = nc.tensor.matmul(down_ps[j // 2][:, j % 2], l[0:rows(u), n % 2, j * P:(j + 1) * P],
                                                    r[0:rows(u), u], start=u == 0 and m == 0 and j % 2 == 0,
                                                    stop=u == IT - 1 and m == 2, skip_group_check=True)
                    last.then_inc(down_done, 1)

            def boot(eng):
                transpose_xn(0, 1)

            run(pe, boot, step)

        @block.scalar
        def _(act):
            def split_xt(i, k, par):
                need(act, xt_done, i, 2, k)
                need(act, gate_up_done, i, TURN, (k - 2) * IT)
                for kt in range(KT):
                    last = nc.scalar.copy(xt_hi[:, par, kt], xt_ps[kt][:])
                last.then_inc(xt_hi_ready, 1)

            def step(i, c):
                t = c % IT
                if t == IT - 1 and live(i, c - t + IT):
                    split_xt(i, c // IT + 2, (c // IT + 1) % 2)
                if live(i, c):
                    need(act, gate_up_done, i, TURN, c + 1)
                    need(act, hid_ready, i, TURN, c - 1)
                    nc.scalar.activation(act_g[0:rows(t), c % 2], gate_ps[c % 2][0:rows(t)], ACT.Silu,
                                         scale=fw.gate_s[0:rows(t), t:t + 1]).then_inc(silu_ready, 1)
                n = c - 1
                if live(i, n):
                    need(act, hid_ready, i, TURN, n + 1)
                    need(act, down_done, i, TURN, n - 1)
                    nc.scalar.copy(hid_hi[0:rows(n % IT), n % 2], hid[0:rows(n % IT), n % 2]).then_inc(hid_hi_ready, 1)

            def boot(eng):
                split_xt(0, 1, 0)

            run(act, boot, step)

        @block.vector
        def _(dve):
            def layer_norm(i, k, par):
                need(dve, x_loaded[par], i, 16, 16 * ((k + 1) // 2))
                for t in range(GT):
                    nc.vector.bn_stats(stats[:, t], x[:, par, t]).then_inc(ln_stats, 1)
                need(dve, ln_stats, i, 2 * GT, GT * k)
                nc.vector.tensor_copy(stats_count[:], stats[:, :, 0])
                for t in range(GT):
                    nc.vector.bn_aggr(mv[:, t], stats[:, t]).then_inc(ln_mv, 1)
                need(dve, ln_mv, i, 2 * GT, GT * k)
                nc.vector.tensor_scalar(var_eps[:], mv[:, :, 1], LN_EPS, None, ALU.add).then_inc(ln_var, 1)

            def normalise(i, k, par):
                need(dve, ln_rstd, i, 2, k)
                need(dve, xt_done, i, 2, k - 1)
                for t in range(GT):
                    last = nc.vector.tensor_scalar(xn[:, t], x[:, par, t], mv[:, t, 0:1], rstd[:, t:t + 1],
                                                   ALU.subtract, ALU.mult)
                last.then_inc(xn_ready, 1)

            def split_xt(i, k, par):
                need(dve, xt_hi_ready, i, 2, k)
                for kt in range(KT):
                    last = nc.vector.tensor_tensor(xt_lo[:, par, kt], xt_ps[kt][:], xt_hi[:, par, kt].bitcast(F32),
                                                   ALU.subtract)
                last.then_inc(xt_lo_ready, 1)

            def step(i, c):
                t = c % IT
                if t == IT - 1 and live(i, c - t + IT):
                    split_xt(i, c // IT + 2, (c // IT + 1) % 2)
                if live(i, c):
                    need(dve, silu_ready, i, TURN, c + 1)
                    need(dve, hid_lo_ready, i, TURN, c - 1)
                    nc.vector.scalar_tensor_tensor(hid[0:rows(t), c % 2], up_ps[c % 2][0:rows(t)],
                                                   fw.up_s[0:rows(t), t:t + 1], act_g[0:rows(t), c % 2],
                                                   ALU.mult, ALU.mult).then_inc(hid_ready, 1)
                n = c - 1
                if live(i, n):
                    r = rows(n % IT)
                    need(dve, hid_hi_ready, i, TURN, n + 1)
                    nc.vector.tensor_tensor(hid_lo[0:r, n % 2], hid[0:r, n % 2], hid_hi[0:r, n % 2].bitcast(F32),
                                            ALU.subtract).then_inc(hid_lo_ready, 1)
                n = c - 2
                if live(i, n) and n % IT == IT - 1:
                    k = n // IT + 1
                    par = (n // IT) % 2
                    need(dve, down_done, i, TURN, n + 1)
                    for j in range(2):
                        last = nc.vector.tensor_tensor(y[:, par, 2 * j:2 * j + 2], down_ps[j][:],
                                                       fw.down_s[:].unsqueeze(1).broadcast_to([P, 2, D]), ALU.mult)
                    last.then_inc(y_scaled, 1)
                    need(dve, y_scaled, i, 2, k)
                    nc.vector.tensor_tensor(y[:, par], y[:, par], x[:, par], ALU.add).then_inc(y_ready, 1)
                if t == 3 and live(i, c - t + IT):
                    layer_norm(i, c // IT + 2, (c // IT + 1) % 2)
                if t == 4 and live(i, c - t + IT):
                    normalise(i, c // IT + 2, (c // IT + 1) % 2)

            def boot(eng):
                layer_norm(0, 1, 0)
                normalise(0, 1, 0)
                split_xt(0, 1, 0)

            run(dve, boot, step)


BH = 16
DK = 8
DV = 16
VH = DV // DK
KD = BH * DK
VD = BH * DV
LR = 16
B_EPS = 1e-5
GATE_NORM = 16.0


def attention_b(nc, io, fw, x_in, x_out):
    LAG = 7
    TURN = 4
    TURNS = (B - 1 - LAG) // TURN
    with ExitStack() as ctx:
        def sb(n, shape, dt=F32):
            return ctx.enter_context(nc.sbuf_tensor("b_" + n, shape, dt))

        def ps(n, shape):
            return ctx.enter_context(nc.psum_tensor("b_" + n, shape, F32))

        def sem(n):
            return ctx.enter_context(nc.semaphore("b_" + n))

        CQ, CK, CV, CG, CR, CN = 0, KD, 2 * KD, 2 * KD + VD, 2 * KD + 2 * VD, 2 * KD + 2 * VD + LR
        kv = sb("kv", [P, 4, DV, T])
        state = sb("state", [P, 2, DV, T])
        w_hi = sb("w_hi", [P, KT, CN], F32R)
        w_lo = sb("w_lo", [P, KT, CN], F32R)
        wo_hi = sb("wo_hi", [P, VH, D], F32R)
        wo_lo = sb("wo_lo", [P, VH, D], F32R)
        gk2 = sb("gk2", [LR, KD])
        bgk2 = sb("bgk2", [P, 1])
        norm_w = sb("norm_w", [P, VH])
        one = sb("one", [P, 1])
        head_of = sb("head_of", [P, BH])
        sum_keys = sb("sum_keys", [P, DK, BH, DK])
        mean_vals = sb("mean_vals", [P, BH, DK])
        x_ln = sb("x_ln", [P, TT, D])
        x_res = sb("x_res", [P, TT, D])
        y = sb("y", [P, TT, D])
        xn = sb("xn", [P, TT, D])
        stats = sb("stats", [P, TT, 6])
        stats_count = sb("stats_count", [P, TT])
        mv = sb("mv", [P, TT, 2])
        var_eps = sb("var_eps", [P, TT])
        half = sb("half", [P, TT])
        rstd = sb("rstd", [P, TT])
        xt_hi = sb("xt_hi", [P, KT, T], F32R)
        xt_lo = sb("xt_lo", [P, KT, T], F32R)
        q = sb("q", [P, 4, T])
        k_ = sb("k", [P, 4, T])
        v = sb("v", [P, VH, T])
        gk1 = sb("gk1", [LR, T])
        z = sb("z", [P, 2, T])
        z_abs = sb("z_abs", [P, T])
        log_sig = sb("log_sig", [P, T])
        decay = sb("decay", [P, 2, T])
        swish = sb("swish", [P, 4, VH, T])
        o_sq = sb("o_sq", [P, VH, T])
        o = sb("o", [P, VH, T])
        ms = sb("ms", [P, T])
        ln_ms = sb("ln_ms", [P, T])
        rms0 = sb("rms0", [P, T])
        rms_sq = sb("rms_sq", [P, T])
        rms = sb("rms", [P, T])
        eps = sb("eps", [P, 1])
        on = sb("on", [P, VH, T])
        o_hi = sb("o_hi", [P, VH, T], F32R)
        o_lo = sb("o_lo", [P, VH, T], F32R)
        w_stage = kv[:, 0].rearrange("p v t -> p (v t)")[:, 0:KT * CN].rearrange("p (k n) -> p k n", k=KT)
        wo_stage = kv[:, 1, 0:VH, :]

        def weight_parts(w):
            gates = w_stage[:, :, CG:CR].rearrange("p k (h a v) -> p k h a v", h=BH, a=VH)
            parts = [(w_stage[:, :, 0:CG], w[:, :, 0:CG]), (w_stage[:, :, CR:CN], w[:, :, CR:CN])]
            for a in range(VH):
                parts.append((gates[:, :, :, a], w[:, :, CG + a * P:CG + (a + 1) * P]
                              .rearrange("p k (h v) -> p k h v", h=BH)))
            return parts

        xt_ps, kq_ps, v_ps, g_ps, gk_ps = (ps(n, [P, 2, T]) for n in ("xt_ps", "kq_ps", "v_ps", "g_ps", "gk_ps"))
        o_ps, ms_ps, y_ps = (ps(n, [P, 2, T]) for n in ("o_ps", "ms_ps", "y_ps"))

        w_loaded, consts_loaded, xln_loaded, xres_loaded = (sem(n) for n in
                                                            ("w_loaded", "consts_loaded", "xln_loaded", "xres_loaded"))
        v_stored, y_stored = sem("v_stored"), sem("y_stored")
        wo_scaled = sem("wo_scaled")
        v_spread = [sem(f"v_spread{i}") for i in range(4)]
        consts_set, masks_set, sel_set = sem("consts_set"), sem("masks_set"), sem("sel_set")
        w_hi_ready, w_lo_ready = sem("w_hi_ready"), sem("w_lo_ready")
        ln_stats, ln_mv, ln_var, ln_rstd, xn_ready = (sem(n) for n in
                                                      ("ln_stats", "ln_mv", "ln_var", "ln_rstd", "xn_ready"))
        xt_done, xt_hi_ready, xt_lo_ready = sem("xt_done"), sem("xt_hi_ready"), sem("xt_lo_ready")
        gk1_done, kq_done, v_done, g_done, gk2_done = (sem(n) for n in
                                                       ("gk1_done", "kq_done", "v_done", "g_done", "gk2_done"))
        o_done, ms_done, y_done = sem("o_done"), sem("ms_done"), sem("y_done")
        gk1_ready, k_ready, q_ready, v_ready = (sem(n) for n in ("gk1_ready", "k_ready", "q_ready", "v_ready"))
        z_ready, abs_ready, e_ready, ln_ready, ls_ready, decay_ready = (
            sem(n) for n in ("z_ready", "abs_ready", "e_ready", "ln_ready", "ls_ready", "decay_ready"))
        swish_ready, o_ready = sem("swish_ready"), sem("o_ready")
        kv_ready, state_ready, qs_ready = sem("kv_ready"), sem("state_ready"), sem("qs_ready")
        ln_ms_ready, rms0_ready, rms_sq_ready, rms_err_ready = (
            sem(n) for n in ("ln_ms_ready", "rms0_ready", "rms_sq_ready", "rms_err_ready"))
        sq_ready, ms_ready, rms_ready, on_ready, og_ready, o_hi_ready, o_lo_ready, y_ready = (
            sem(n) for n in ("sq_ready", "ms_ready", "rms_ready", "on_ready", "og_ready", "o_hi_ready", "o_lo_ready",
                             "y_ready"))

        v_dram = nc.dram_tensor("b_values", (B, VD, T), F32, kind="Internal").ap()
        block = ctx.enter_context(nc.Block())

        def run(eng, boot, step):
            boot(eng)
            for c in range(LAG):
                step(0, c)
            with eng.Fori(0, TURNS) as i:
                for c in range(LAG, LAG + TURN):
                    step(i, c)
            for c in range(LAG, B - TURN * TURNS + 5):
                step(TURNS, c)

        def live(i, n):
            return not isinstance(i, int) or 0 <= TURN * i + n < B

        @block.sync
        def _(sp):
            def tiles(x_dram, b):
                return x_dram[b].rearrange("(t p) d -> p t d", p=P)

            sp.dma_start(x_ln[:], tiles(x_in, 0)).then_inc(xln_loaded, 16)
            for n, c0, c1 in (("Wq", CQ, CK), ("Wk", CK, CV), ("Wv", CV, CG), ("Wg", CG, CR), ("Wgk1", CR, CN)):
                sp.dma_start(w_stage[:, :, c0:c1], io["b_" + n].rearrange("(k p) n -> p k n", p=P)).then_inc(w_loaded, 16)
            for h in range(BH):
                at = slice(h * DK, (h + 1) * DK)
                sp.dma_start(wo_stage[at], io["b_Wo"][h * DV:(h + 1) * DV].rearrange("(a v) n -> v a n", a=VH))\
                  .then_inc(w_loaded, 16)
                sp.dma_start(norm_w[at], io["b_norm_w"].rearrange("(a v) -> v a", a=VH),
                             allow_slow_non_contiguous=True).then_inc(consts_loaded, 16)
            sp.dma_start(gk2[:], io["b_Wgk2"]).then_inc(consts_loaded, 16)
            sp.dma_start(bgk2[:], io["b_bgk2"].rearrange("(p a) -> p a", a=1)).then_inc(consts_loaded, 16)
            sp.wait_ge(w_lo_ready, 5)
            sp.wait_ge(xn_ready, 1)
            sp.dma_start(x_ln[:], tiles(x_in, 1)).then_inc(xln_loaded, 16)
            for c in range(B + 5):
                if c < B:
                    sp.wait_ge(v_ready, c + 1)
                    sp.dma_start(v_dram[c].rearrange("(a p) t -> p a t", p=P), v[:]).then_inc(v_stored, 16)
                    sp.wait_ge(v_stored, 16 * (c + 1))
                    if c >= 4:
                        sp.wait_ge(state_ready, DV * (c - 3))
                    for h in range(BH):
                        src = v_dram[c, h * DV:(h + 1) * DV].rearrange("(a v) t -> a (v t)", a=1)
                        sp.dma_start(kv[h * DK:(h + 1) * DK, c % 4].rearrange("p v t -> p (v t)"),
                                     src.broadcast_to([DK, DV * T])).then_inc(v_spread[c % 4], 16)
                n = c - 5
                if n >= 0:
                    sp.wait_ge(y_ready, n + 1)
                    sp.dma_start(tiles(x_out, n), y[:]).then_inc(y_stored, 16)
                if 0 <= n + 1 < B:
                    sp.dma_start(x_res[:], tiles(x_in, n + 1)).then_inc(xres_loaded, 16)
                if c + 2 < B:
                    sp.wait_ge(xn_ready, c + 2)
                    sp.dma_start(x_ln[:], tiles(x_in, c + 2)).then_inc(xln_loaded, 16)
            sp.wait_ge(y_stored, 16 * B)

        @block.gpsimd
        def _(pool):
            pool.memset(half[:], -0.5).then_inc(consts_set, 1)
            pool.memset(one[:], 1.0).then_inc(consts_set, 1)
            pool.memset(eps[:], B_EPS).then_inc(consts_set, 1)
            pool.memset(head_of[:], 1.0).then_inc(consts_set, 1)
            pool.wait_ge(consts_set, 4)
            pool.affine_select(out=head_of[:], in_=head_of[:], compare_op=ALU.is_ge, fill=0.0, base=0,
                               pattern=[[-DK, BH]], channel_multiplier=1).then_inc(masks_set, 1)
            pool.wait_ge(masks_set, 1)
            pool.affine_select(out=head_of[:], in_=head_of[:], compare_op=ALU.is_ge, fill=0.0, base=DK - 1,
                               pattern=[[DK, BH]], channel_multiplier=-1).then_inc(masks_set, 1)

            def power(i, k):
                need(pool, ln_var, i, TURN, k)
                pool.tensor_tensor(rstd[:], var_eps[:], half[:], ALU.pow).then_inc(ln_rstd, 1)

            def step(i, c):
                if live(i, c + 1):
                    power(i, c + 2)
                n = c - 2
                if live(i, n):
                    need(pool, q_ready, i, TURN, n + 1)
                    for j in range(2):
                        vs = slice(j * DK, (j + 1) * DK)
                        need(pool, state_ready, i, DV * TURN, DV * n + DK * (j + 1))
                        pool.tensor_tensor(state[:, n % 2, vs], state[:, n % 2, vs],
                                           q[:, n % 4].unsqueeze(1).broadcast_to([P, DK, T]), ALU.mult)\
                            .then_inc(qs_ready, 1)

            def boot(eng):
                for used in fw.sems.values():
                    pool.sem_clear(used)
                power(0, 1)

            run(pool, boot, step)

        @block.tensor
        def _(pe):
            def project(out, c0, m=P):
                for k in range(KT):
                    for j, (l, r) in enumerate(((w_hi, xt_hi), (w_hi, xt_lo), (w_lo, xt_hi))):
                        last = nc.tensor.matmul(out, l[:, k, c0:c0 + m], r[:, k], start=k == 0 and j == 0,
                                                stop=k == KT - 1 and j == 2)
                return last

            def transpose_xn(i, k):
                need(pe, xn_ready, i, TURN, k)
                need(pe, xt_lo_ready, i, TURN, k - 1)
                for kt in range(KT):
                    for t in range(TT):
                        last = nc.tensor.transpose(xt_ps[:, kt, t * P:(t + 1) * P], xn[:, t, kt * P:(kt + 1) * P],
                                                   fw.ident[:])
                last.then_inc(xt_done, 1)

            def step(i, c):
                if live(i, c):
                    need(pe, xt_lo_ready, i, TURN, c + 1)
                    need(pe, abs_ready, i, TURN, c)
                    need(pe, q_ready, i, TURN, c)
                    need(pe, v_ready, i, TURN, c)
                    project(gk_ps[0:LR, 0], CR, LR).then_inc(gk1_done, 1)
                    project(kq_ps[:, 1], CQ)
                    project(kq_ps[:, 0], CK).then_inc(kq_done, 1)
                    need(pe, gk1_ready, i, TURN, c + 1)
                    nc.tensor.matmul(gk_ps[:, 1], gk2[:], gk1[:], start=True, stop=True).then_inc(gk2_done, 1)
                    for a in range(VH):
                        last = project(v_ps[:, a], CV + a * P)
                    last.then_inc(v_done, 1)
                    need(pe, swish_ready, i, TURN, c)
                    for a in range(VH):
                        last = project(g_ps[:, a], CG + a * P)
                    last.then_inc(g_done, 1)
                n = c - 5
                if live(i, n):
                    need(pe, o_lo_ready, i, TURN, n + 1)
                    need(pe, y_ready, i, TURN, n)
                    for t in range(TT):
                        rows_t = slice(t * P, (t + 1) * P)
                        for a in range(VH):
                            for m, (l, r) in enumerate(((o_hi, wo_hi), (o_hi, wo_lo), (o_lo, wo_hi))):
                                last = nc.tensor.matmul(y_ps[:, t], l[:, a, rows_t], r[:, a], start=a == 0 and m == 0,
                                                        stop=a == VH - 1 and m == 2)
                    last.then_inc(y_done, 1)
                n = c - 3
                if live(i, n):
                    need(pe, o_ready, i, TURN, n)
                    for m in range(DV):
                        if m % DK == 0:
                            need(pe, qs_ready, i, 2 * TURN, 2 * n + m // DK + 1)
                        last = nc.tensor.matmul(o_ps[:, m // DK], sum_keys[:, m % DK], state[:, n % 2, m],
                                                start=m % DK == 0, stop=m % DK == DK - 1)
                    last.then_inc(o_done, 1)
                if live(i, c + 1):
                    transpose_xn(i, c + 2)
                if live(i, n):
                    need(pe, sq_ready, i, TURN, n + 1)
                    need(pe, ln_ms_ready, i, TURN, n)
                    for a in range(VH):
                        last = nc.tensor.matmul(ms_ps[:, 0], mean_vals[:], o_sq[:, a], start=a == 0, stop=a == VH - 1)
                    last.then_inc(ms_done, 1)

            def boot(eng):
                pe.wait_ge(sel_set, 3)
                pe.wait_ge(consts_loaded, 16 * (BH + 2))
                pe.wait_ge(w_lo_ready, 5)
                transpose_xn(0, 1)

            run(pe, boot, step)

        @block.scalar
        def _(act):
            def split_xt(i, k):
                need(act, xt_done, i, TURN, k)
                need(act, g_done, i, TURN, k - 1)
                nc.scalar.copy(xt_hi[:], xt_ps[:]).then_inc(xt_hi_ready, 1)

            def step(i, c):
                if live(i, c - 1):
                    need(act, g_done, i, TURN, c)
                    need(act, og_ready, i, TURN, c - 4)
                    nc.scalar.activation(swish[:, (c - 1) % 4], g_ps[:], ACT.Silu).then_inc(swish_ready, 1)
                if live(i, c):
                    need(act, gk1_done, i, TURN, c + 1)
                    nc.scalar.copy(gk1[:], gk_ps[0:LR, 0]).then_inc(gk1_ready, 1)
                    need(act, kq_done, i, TURN, c + 1)
                    need(act, kv_ready, i, TURN, c - 3)
                    nc.scalar.copy(k_[:, c % 4], kq_ps[:, 0]).then_inc(k_ready, 1)
                    need(act, qs_ready, i, 2 * TURN, 2 * (c - 3))
                    nc.scalar.mul(q[:, c % 4], kq_ps[:, 1], float(DK) ** -0.5).then_inc(q_ready, 1)
                    need(act, gk2_done, i, TURN, c + 1)
                    nc.scalar.activation(z[:, c % 2], gk_ps[:, 1], ACT.Identity, bias=bgk2[:]).then_inc(z_ready, 1)
                    need(act, ls_ready, i, TURN, c)
                    nc.scalar.activation(z_abs[:], gk_ps[:, 1], ACT.Abs, bias=bgk2[:]).then_inc(abs_ready, 1)
                    need(act, v_done, i, TURN, c + 1)
                    need(act, v_stored, i, 16 * TURN, 16 * c)
                    nc.scalar.copy(v[:], v_ps[:]).then_inc(v_ready, 1)
                    need(act, abs_ready, i, TURN, c + 1)
                    nc.scalar.activation(z_abs[:], z_abs[:], ACT.Exp, scale=-1.0).then_inc(e_ready, 1)
                if live(i, c - 1):
                    need(act, ls_ready, i, TURN, c)
                    need(act, state_ready, i, DV * TURN, DV * (c - 2))
                    nc.scalar.activation(decay[:, (c - 1) % 2], log_sig[:], ACT.Exp, scale=1.0 / GATE_NORM)\
                      .then_inc(decay_ready, 1)
                n = c - 4
                if live(i, n):
                    need(act, ln_ms_ready, i, TURN, n + 1)
                    need(act, rms_ready, i, TURN, n)
                    nc.scalar.activation(rms0[:], ln_ms[:], ACT.Exp, scale=-0.5).then_inc(rms0_ready, 1)
                if live(i, c):
                    need(act, e_ready, i, TURN, c + 1)
                    nc.scalar.activation(z_abs[:], z_abs[:], ACT.Ln, bias=one[:]).then_inc(ln_ready, 1)
                if live(i, n):
                    need(act, og_ready, i, TURN, n + 1)
                    need(act, y_done, i, TURN, n)
                    nc.scalar.copy(o_hi[:], on[:]).then_inc(o_hi_ready, 1)
                n = c - 3
                if live(i, n):
                    need(act, o_done, i, TURN, n + 1)
                    nc.scalar.activation(o_sq[:], o_ps[:], ACT.Square).then_inc(sq_ready, 1)
                    need(act, on_ready, i, TURN, n)
                    nc.scalar.copy(o[:], o_ps[:]).then_inc(o_ready, 1)
                if live(i, c + 1):
                    split_xt(i, c + 2)
                if live(i, n):
                    need(act, ms_done, i, TURN, n + 1)
                    need(act, rms_ready, i, TURN, n)
                    nc.scalar.activation(ms[:], ms_ps[:, 0], ACT.Identity, bias=eps[:]).then_inc(ms_ready, 1)
                    need(act, rms0_ready, i, TURN, n)
                    nc.scalar.activation(ln_ms[:], ms_ps[:, 0], ACT.Ln, bias=eps[:]).then_inc(ln_ms_ready, 1)

            def boot(eng):
                act.wait_ge(w_loaded, 16 * (5 + BH))
                act.wait_ge(consts_loaded, 16 * (BH + 2))
                for staged, hi in weight_parts(w_hi):
                    nc.scalar.copy(hi, staged).then_inc(w_hi_ready, 1)
                for a in range(VH):
                    nc.scalar.mul(wo_stage[:, a], wo_stage[:, a], norm_w[:, a:a + 1]).then_inc(wo_scaled, 1)
                act.wait_ge(wo_scaled, VH)
                nc.scalar.copy(wo_hi[:], wo_stage).then_inc(w_hi_ready, 1)
                act.wait_ge(consts_set, 4)
                split_xt(0, 1)

            run(act, boot, step)

        @block.vector
        def _(dve):
            def layer_norm(i, k):
                need(dve, xln_loaded, i, 16 * TURN, 16 * k)
                for t in range(TT):
                    nc.vector.bn_stats(stats[:, t], x_ln[:, t]).then_inc(ln_stats, 1)
                need(dve, ln_stats, i, TT * TURN, TT * k)
                nc.vector.tensor_copy(stats_count[:], stats[:, :, 0])
                for t in range(TT):
                    nc.vector.bn_aggr(mv[:, t], stats[:, t]).then_inc(ln_mv, 1)
                need(dve, ln_mv, i, TT * TURN, TT * k)
                nc.vector.tensor_scalar(var_eps[:], mv[:, :, 1], LN_EPS, None, ALU.add).then_inc(ln_var, 1)

            def normalise(i, k):
                need(dve, ln_rstd, i, TURN, k)
                need(dve, xt_done, i, TURN, k - 1)
                for t in range(TT):
                    last = nc.vector.tensor_scalar(xn[:, t], x_ln[:, t], mv[:, t, 0:1], rstd[:, t:t + 1],
                                                   ALU.subtract, ALU.mult)
                last.then_inc(xn_ready, 1)

            def split_xt(i, k):
                need(dve, xt_hi_ready, i, TURN, k)
                nc.vector.tensor_tensor(xt_lo[:], xt_ps[:], xt_hi[:].bitcast(F32), ALU.subtract).then_inc(xt_lo_ready, 1)

            def step(i, c):
                if live(i, c + 1):
                    layer_norm(i, c + 2)
                if live(i, c - 1):
                    need(dve, ln_ready, i, TURN, c)
                    need(dve, decay_ready, i, TURN, c - 1)
                    nc.vector.scalar_tensor_tensor(log_sig[:], z[:, (c - 1) % 2], 0.0, z_abs[:], ALU.min, ALU.subtract)\
                      .then_inc(ls_ready, 1)
                n = c - 2
                if live(i, n):
                    need(dve, k_ready, i, TURN, n + 1)
                    need(dve, v_spread[n % 4], i, 16 * BH, 16 * BH * (n // 4 + 1))
                    nc.vector.tensor_tensor(kv[:, n % 4], kv[:, n % 4], k_[:, n % 4].unsqueeze(1).broadcast_to([P, DV, T]),
                                            ALU.mult).then_inc(kv_ready, 1)
                n = c - 4
                if live(i, n):
                    need(dve, rms0_ready, i, TURN, n + 1)
                    nc.vector.tensor_tensor(rms_sq[:], rms0[:], rms0[:], ALU.mult).then_inc(rms_sq_ready, 1)
                    need(dve, rms_sq_ready, i, TURN, n + 1)
                    need(dve, ms_ready, i, TURN, n + 1)
                    nc.vector.scalar_tensor_tensor(rms_sq[:], ms[:], -0.5, rms_sq[:], ALU.mult, ALU.mult)\
                      .then_inc(rms_err_ready, 1)
                    need(dve, rms_err_ready, i, TURN, n + 1)
                    nc.vector.scalar_tensor_tensor(rms[:], rms_sq[:], 1.5, rms0[:], ALU.add, ALU.mult)\
                      .then_inc(rms_ready, 1)
                    need(dve, rms_ready, i, TURN, n + 1)
                    need(dve, o_ready, i, TURN, n + 1)
                    nc.vector.tensor_tensor(on[:], o[:], rms[:].unsqueeze(1).broadcast_to([P, VH, T]), ALU.mult)\
                      .then_inc(on_ready, 1)
                    need(dve, on_ready, i, TURN, n + 1)
                    need(dve, swish_ready, i, TURN, n + 1)
                    nc.vector.tensor_tensor(on[:], on[:], swish[:, n % 4], ALU.mult).then_inc(og_ready, 1)
                n = c - 5
                if live(i, n):
                    need(dve, y_done, i, TURN, n + 1)
                    need(dve, xres_loaded, i, 16 * TURN, 16 * (n + 1))
                    need(dve, y_stored, i, 16 * TURN, 16 * n)
                    nc.vector.tensor_tensor(y[:], y_ps[:], x_res[:], ALU.add).then_inc(y_ready, 1)
                if live(i, c + 1):
                    normalise(i, c + 2)
                n = c - 2
                if live(i, n):
                    need(dve, kv_ready, i, TURN, n + 1)
                    need(dve, decay_ready, i, TURN, n + 1)
                    need(dve, o_done, i, TURN, n - 1)
                    for m in range(DV):
                        nc.vector.tensor_tensor_scan(state[:, n % 2, m], decay[:, n % 2], kv[:, n % 4, m], 0.0,
                                                     ALU.mult, ALU.add).then_inc(state_ready, 1)
                n = c - 4
                if live(i, n):
                    need(dve, o_hi_ready, i, TURN, n + 1)
                    nc.vector.tensor_tensor(o_lo[:], on[:], o_hi[:].bitcast(F32), ALU.subtract).then_inc(o_lo_ready, 1)
                if live(i, c + 1):
                    split_xt(i, c + 2)

            def boot(eng):
                dve.wait_ge(masks_set, 2)
                nc.vector.memset(sum_keys[:], 0.0).then_inc(sel_set, 1)
                nc.vector.tensor_scalar(mean_vals[:], head_of[:].unsqueeze(2).broadcast_to([P, BH, DK]), 1.0 / DV, None,
                                        ALU.mult).then_inc(sel_set, 1)
                dve.wait_ge(sel_set, 2)
                for m in range(DK):
                    last = nc.vector.tensor_copy(sum_keys[:, m, :, m], head_of[:])
                last.then_inc(sel_set, 1)
                dve.wait_ge(w_hi_ready, 5)
                for (staged, lo), (_, hi) in zip(weight_parts(w_lo), weight_parts(w_hi)):
                    nc.vector.tensor_tensor(lo, staged, hi.bitcast(F32), ALU.subtract).then_inc(w_lo_ready, 1)
                nc.vector.tensor_tensor(wo_lo[:], wo_stage, wo_hi[:].bitcast(F32), ALU.subtract).then_inc(w_lo_ready, 1)
                dve.wait_ge(consts_loaded, 16 * (BH + 2))
                layer_norm(0, 1)
                normalise(0, 1)
                split_xt(0, 1)

            run(dve, boot, step)


def build(nc, io, x_in, out, stages=4):
    x1 = nc.dram_tensor("x1", (B, T, D), F32, kind="Internal").ap() if stages > 1 else out
    x2 = nc.dram_tensor("x2", (B, T, D), F32, kind="Internal").ap() if stages > 2 else out
    x3 = nc.dram_tensor("x3", (B, T, D), F32, kind="Internal").ap() if stages > 3 else out
    attention_a(nc, io, x_in, x1)
    if stages > 1:
        with ExitStack() as ctx:
            fw = FfnWeights(nc, ctx)
            prepare_ffn(nc, io, fw)
            ffn(nc, "f1_", fw, x1, x2)
            if stages > 2:
                attention_b(nc, io, fw, x2, x3)
            if stages > 3:
                ffn(nc, "f2_", fw, x3, out)


_PRE = {"L0_attn_a_": "", "L0_attn_b_": "b_", "L0_ffn_": "f_"}


def kernel(**inputs):
    import numpy as _np
    import concourse.bacc as _bacc
    from concourse import mybir as _mybir
    from concourse.bass_utils import run_bass_kernel_spmd as _run

    nc = _bacc.Bacc("TRN2", target_bir_lowering=False, num_devices=1)
    arrays, io = {}, {}
    for name, array in inputs.items():
        a = _np.ascontiguousarray(array)
        arrays[f"in_{name}_dram"] = a
        short = name
        for long, pre in _PRE.items():
            if name.startswith(long):
                short = pre + name[len(long):]
        io[short] = nc.dram_tensor(f"in_{name}_dram", a.shape, _mybir.dt.from_np(a.dtype), kind="ExternalInput").ap()
    out = nc.dram_tensor("out_0_dram", (B, T, D), _mybir.dt.float32, kind="ExternalOutput").ap()
    build(nc, io, io["x"], out, stages=4)
    r = _run(nc, [arrays], core_ids=[0])
    return r.results[0]["out_0_dram"]
```

```python
from contextlib import ExitStack

import concourse.bass as bass
from concourse import mybir

F32 = mybir.dt.float32
F32R = mybir.dt.float32r
ALU = mybir.AluOpType
ACT = mybir.ActivationFunctionType
AX_X = mybir.AxisListType.X

P = 128
B = 16
T = 256
D = 256
TT = T // P
KT = D // P
H = 16
HD = 128
BS = 64
SCALING = float(HD) ** -0.5
LN_EPS = 1e-5
DEN_EPS = 1e-6
PHI_TOP = 10.0
VB = 4
SLOTS = 3
LAG = 8


def value(i, rate, k):
    if isinstance(i, int):
        v = i * rate + k
        return v if v > 0 else None
    assert k > 0
    return i * rate + k


def need(eng, sem, i, rate, k):
    v = value(i, rate, k)
    if v is not None:
        eng.wait_ge(sem, v)


def attention_a(nc, io, x_in, x_out):
    with ExitStack() as ctx:
        def sb(name, shape, dt=F32):
            return ctx.enter_context(nc.sbuf_tensor("a_" + name, shape, dt))

        def ps(name, shape):
            return ctx.enter_context(nc.psum_tensor("a_" + name, shape, F32))

        def sem(name):
            return ctx.enter_context(nc.semaphore("a_" + name))

        w_hi = [sb(f"w{n}_hi", [P, KT, H * HD], F32R) for n in "qkv"]
        w_lo = [sb(f"w{n}_lo", [P, KT, H * HD], F32R) for n in "qkv"]
        wo_hi = sb("wo_hi", [P, H, D], F32R)
        wo_lo = sb("wo_lo", [P, H, D], F32R)
        w_stage = sb("w_stage", [P, SLOTS, KT, 4 * HD])
        phi_s = sb("phi_s", [P, H])
        phi_b = sb("phi_b", [P, H])
        phi_b1 = sb("phi_b1", [P, H])
        bo_bc = sb("bo_bc", [P, D])
        ident = sb("ident", [P, P])
        at_mask = sb("at_mask", [P, T + P])
        x_ln = sb("x_ln", [P, TT, D])
        x_res = sb("x_res", [P, TT, D])
        y = sb("y", [P, TT, D])
        xn = sb("xn", [P, TT, D])
        stats = sb("stats", [P, TT, 6])
        stats_count = sb("stats_count", [P, TT])
        mv = sb("mv", [P, TT, 2])
        var_eps = sb("var_eps", [P, TT])
        half = sb("half", [P, TT])
        rstd = sb("rstd", [P, TT])
        xt_hi = sb("xt_hi", [P, KT, T], F32R)
        xt_lo = sb("xt_lo", [P, KT, T], F32R)
        qk = sb("qk", [P, 2, 2, T])
        ez = sb("ez", [P, 2, 2, T])
        z1 = sb("z1", [P, 2, 2, T])
        phi_raw = sb("phi_raw", [P, 2, T])
        phi_hi = sb("phi_hi", [P, 2, 2, T], F32R)
        phi_lo = sb("phi_lo", [P, 2, 2, T], F32R)
        v_ext = sb("v_ext", [P, VB, TT, 2, HD + 2])
        rmax = sb("rmax", [P, 4])
        sc = sb("sc", [P, 4, BS])
        pexp = sb("pexp", [P, 4, BS])
        rsum = sb("rsum", [P, 4])
        rinv = sb("rinv", [P, 4])
        prob = sb("prob", [P, 4, BS])
        pt = sb("pt", [P, 2, 2, TT, P])
        at = sb("at", [P, 2, T + P])
        den = sb("den", [P, TT])
        rden = sb("rden", [P, 2, TT])
        num = sb("num", [P, 2, TT, HD])
        o = sb("o", [P, 2, TT, HD])
        ot_hi = sb("ot_hi", [P, 2, T], F32R)
        ot_lo = sb("ot_lo", [P, 2, T], F32R)

        qk_ps = [ps(f"qk_ps{i}", [P, 2, T]) for i in range(2)]
        v_ps = ps("v_ps", [P, 512])
        sc_ps = ps("sc_ps", [P, 512])
        at_ps = ps("at_ps", [P, 512])
        num_ps = ps("num_ps", [P, 512])
        lo_ps = ps("lo_ps", [P, 512])
        wo_ps = ps("wo_ps", [P, TT, D])

        consts_loaded = sem("consts_loaded")
        stage_loaded = [sem(f"stage_loaded{i}") for i in range(SLOTS)]
        xln_loaded = sem("xln_loaded")
        xres_loaded = sem("xres_loaded")
        y_stored = sem("y_stored")
        mem_zeroed = sem("mem_zeroed")
        masks_ready = sem("masks_ready")
        w_hi_ready = sem("w_hi_ready")
        w_lo_ready = sem("w_lo_ready")
        ln_stats = sem("ln_stats")
        ln_mv = sem("ln_mv")
        ln_var = sem("ln_var")
        ln_rstd = sem("ln_rstd")
        xn_ready = sem("xn_ready")
        xt_done = sem("xt_done")
        xt_hi_ready = sem("xt_hi_ready")
        xt_lo_ready = sem("xt_lo_ready")
        qk_done = sem("qk_done")
        v_done = sem("v_done")
        sc_done = sem("sc_done")
        at_done = sem("at_done")
        pt_done = sem("pt_done")
        num_done = sem("num_done")
        loc_done = sem("loc_done")
        ot_done = sem("ot_done")
        wo_done = sem("wo_done")
        qk_copied = sem("qk_copied")
        e_ready = sem("e_ready")
        p_exp = sem("p_exp")
        pt_ready = sem("pt_ready")
        num_scaled = sem("num_scaled")
        v_ready = sem("v_ready")
        z1_ready = sem("z1_ready")
        phi_joined = sem("phi_joined")
        phi_hi_ready = sem("phi_hi_ready")
        phi_ready = sem("phi_ready")
        max_ready = sem("max_ready")
        sc_ready = sem("sc_ready")
        sum_ready = sem("sum_ready")
        inv_ready = sem("inv_ready")
        prob_ready = sem("prob_ready")
        at_ready = sem("at_ready")
        den_ready = sem("den_ready")
        rden_ready = sem("rden_ready")
        ot_hi_ready = sem("ot_hi_ready")
        ot_ready = sem("ot_ready")
        o_ready = sem("o_ready")
        y_sum = sem("y_sum")
        y_ready = sem("y_ready")

        def wo_chunk(slot):
            return w_stage[:, slot].rearrange("p k n -> p (k n)").rearrange("p (h n) -> p h n", h=4)

        def chunk(m, w, w_o):
            g = m // 4
            if m % 4 < 3:
                return w_stage[:, m % SLOTS], w[m % 4][:, :, g * 512:(g + 1) * 512]
            return wo_chunk(m % SLOTS), w_o[:, 4 * g:4 * g + 4]

        CHUNKS_AT = ((4,), (5,), (6,), (7,), (8, 9), (10, 11), (12, 13), (14, 15))
        block = ctx.enter_context(nc.Block())

        def run(eng, boot, step):
            boot(eng)
            for c in range(LAG):
                step(0, c)
            with eng.Fori(0, B - 1) as i:
                for c in range(LAG, LAG + H):
                    step(i, c)
            for c in range(LAG, H + LAG):
                step(B - 1, c)

        def live(i, n):
            return not isinstance(i, int) or 0 <= H * i + n < B * H

        @block.sync
        def _(sp):
            sp.dma_start(x_ln[:], x_in[0].rearrange("(t p) d -> p t d", p=P)).then_inc(xln_loaded, 16)
            for m in range(16):
                if m >= SLOTS:
                    sp.wait_ge(w_lo_ready, m - SLOTS + 1)
                g = m // 4
                if m % 4 < 3:
                    src = io["W" + "qkv"[m % 4]].rearrange("(k p) n -> p k n", p=P)[:, :, g * 512:(g + 1) * 512]
                    dst = w_stage[:, m % SLOTS]
                else:
                    src = io["Wo"].rearrange("(h p) n -> p h n", p=P)[:, 4 * g:4 * g + 4]
                    dst = wo_chunk(m % SLOTS)
                sp.dma_start(dst, src).then_inc(stage_loaded[m % SLOTS], 16)
                if m == 1:
                    sp.dma_start(phi_s[:], io["phi_scale"].rearrange("h o k -> k (h o)"),
                                 allow_slow_non_contiguous=True).then_inc(consts_loaded, 16)
                    sp.dma_start(phi_b[:], io["phi_bias"].rearrange("h o k -> k (h o)"),
                                 allow_slow_non_contiguous=True).then_inc(consts_loaded, 16)
                    sp.dma_start(bo_bc[:], io["bo"].rearrange("(a n) -> a n", a=1).broadcast_to([P, D]))\
                      .then_inc(consts_loaded, 16)

            for b in range(B):
                if b + 1 < B:
                    sp.wait_ge(xn_ready, b + 1)
                    sp.dma_start(x_ln[:], x_in[b + 1].rearrange("(t p) d -> p t d", p=P)).then_inc(xln_loaded, 16)
                if b:
                    sp.wait_ge(y_sum, b)
                    sp.wait_ge(y_stored, 16 * b)
                sp.dma_start(x_res[:], x_in[b].rearrange("(t p) d -> p t d", p=P)).then_inc(xres_loaded, 16)
                sp.wait_ge(y_ready, b + 1)
                sp.dma_start(x_out[b].rearrange("(t p) d -> p t d", p=P), y[:]).then_inc(y_stored, 16)
            sp.wait_ge(y_stored, 16 * B)

        @block.gpsimd
        def _(pool):
            pool.memset(ident[:], 0.0).then_inc(mem_zeroed, 1)
            pool.memset(half[:], -0.5).then_inc(mem_zeroed, 1)
            pool.memset(at_mask[:], 1.0).then_inc(mem_zeroed, 1)
            pool.memset(pt[:], 0.0).then_inc(mem_zeroed, 1)
            for par in range(VB):
                for h2 in range(2):
                    pool.memset(v_ext[:, par, :, h2, HD:HD + 1], 1.0).then_inc(mem_zeroed, 1)
                    pool.memset(v_ext[:, par, :, h2, HD + 1:HD + 2], 0.0).then_inc(mem_zeroed, 1)
            pool.wait_ge(mem_zeroed, 4 + 4 * VB)
            pool.memset(at_mask[BS:P, 0:BS], 0.0).then_inc(masks_ready, 1)
            pool.memset(at_mask[BS:P, T:T + BS], 0.0).then_inc(masks_ready, 1)
            pool.wait_ge(masks_ready, 2)
            pool.affine_select(out=ident[:], in_=ident[:], compare_op=ALU.not_equal, fill=1.0, base=0,
                               pattern=[[-1, P]], channel_multiplier=1).then_inc(masks_ready, 1)

            def power(i, k):
                need(pool, ln_var, i, 1, k)
                pool.tensor_tensor(rstd[:], var_eps[:], half[:], ALU.pow).then_inc(ln_rstd, 1)

            power(0, 1)
            with pool.Fori(0, B - 1) as i:
                power(i, 2)

        @block.tensor
        def _(pe):
            def product(out, hi_l, lo_l, hi_r, lo_r, start=True):
                last = None
                for k in range(KT):
                    for m, (l, r) in enumerate(((hi_l, hi_r), (hi_l, lo_r), (lo_l, hi_r))):
                        last = nc.tensor.matmul(out, l(k), r(k), start=start and k == 0 and m == 0,
                                                stop=k == KT - 1 and m == 2)
                return last

            def transpose_xn(i, k, bank):
                need(pe, xn_ready, i, 1, k)
                for kt in range(KT):
                    for t in range(TT):
                        last = nc.tensor.transpose(bank[:, kt, t * P:(t + 1) * P], xn[:, t, kt * P:(kt + 1) * P],
                                                   ident[:])
                last.then_inc(xt_done, 1)

            def transpose_o(i, n):
                need(pe, o_ready, i, H, n + 1)
                for t in range(TT):
                    last = nc.tensor.transpose(lo_ps[:, T + t * P:T + (t + 1) * P], o[:, n % 2, t, :], ident[:])
                last.then_inc(ot_done, 1)

            def step(i, c):
                h = c % H
                if live(i, c):
                    if h == 0:
                        need(pe, xt_lo_ready, i, 1, c // H + 1)
                    if h % 4 == 0:
                        pe.wait_ge(w_lo_ready, h + 2)
                    need(pe, z1_ready, i, H, c - 1)
                    for j in range(2):
                        last = product(qk_ps[c % 2][:, j],
                                       lambda k: w_hi[j][:, k, h * HD:(h + 1) * HD],
                                       lambda k: w_lo[j][:, k, h * HD:(h + 1) * HD],
                                       lambda k: xt_hi[:, k], lambda k: xt_lo[:, k])
                    last.then_inc(qk_done, 1)
                if live(i, c) and h % 2 == 0:
                    need(pe, v_ready, i, H // 2, c // 2)
                    need(pe, pt_ready, i, H // 2, c // 2 - 1)
                    if h % 4 == 0:
                        pe.wait_ge(w_lo_ready, h + 3)
                    for t in range(TT):
                        last = product(v_ps[:, t * 256:(t + 1) * 256],
                                       lambda k: xt_hi[:, k, t * P:(t + 1) * P],
                                       lambda k: xt_lo[:, k, t * P:(t + 1) * P],
                                       lambda k: w_hi[2][:, k, h * HD:(h + 2) * HD],
                                       lambda k: w_lo[2][:, k, h * HD:(h + 2) * HD])
                    last.then_inc(v_done, 1)
                if c % 2 == 0 and live(i, c - 5):
                    transpose_o(i, c - 5)
                if live(i, c + 1) and h == H - 1:
                    need(pe, z1_ready, i, H, c)
                    transpose_xn(i, c // H + 2, qk_ps[0])
                n = c - 1
                if live(i, n):
                    need(pe, qk_copied, i, H, n + 1)
                    if n % 2 == 0:
                        need(pe, sc_ready, i, H // 2, n // 2)
                    for b in range(T // BS):
                        s0 = (n % 2) * 2 * BS + (b % 2) * BS
                        last = nc.tensor.matmul(sc_ps[(b // 2) * BS:(b // 2 + 1) * BS, s0:s0 + BS],
                                                qk[:, n % 2, 0, b * BS:(b + 1) * BS],
                                                qk[:, n % 2, 1, b * BS:(b + 1) * BS], start=True, stop=True)
                    last.then_inc(sc_done, 1)
                n = c - 2
                if live(i, n):
                    need(pe, phi_ready, i, H, n + 1)
                    need(pe, at_ready, i, H, n)
                    for out, keys, queries in ((slice(0, T), slice(0, P), slice(0, T)),
                                               (slice(T, T + P), slice(P, T), slice(P, T))):
                        for m, (l, r) in enumerate(((phi_hi, phi_hi), (phi_hi, phi_lo), (phi_lo, phi_hi))):
                            last = nc.tensor.matmul(at_ps[:, out], l[:, n % 2, 1, keys], r[:, n % 2, 0, queries],
                                                    start=m == 0, stop=m == 2)
                    last.then_inc(at_done, 1)
                if c % 2 == 1 and live(i, c - 5):
                    transpose_o(i, c - 5)
                if c % 2 == 1 and live(i, c - 3):
                    need(pe, prob_ready, i, H // 2, (c - 3) // 2 + 1)
                    if live(i, c - 1):
                        need(pe, v_ready, i, H // 2, (c - 1) // 2 + 1)
                    for h2 in range(2):
                        last = nc.tensor.transpose(v_ps[:, h2 * P:(h2 + 1) * P], prob[:, 2 * h2:2 * h2 + 2, :],
                                                   ident[:])
                    last.then_inc(pt_done, 1)
                n = c - 3
                if live(i, n):
                    need(pe, at_ready, i, H, n + 1)
                    need(pe, v_ready, i, H // 2, n // 2 + 1)
                    need(pe, num_scaled, i, H, n)
                    v = v_ext[:, (n // 2) % VB]
                    nc.tensor.matmul(num_ps[:, 0:HD + 2], at[:, n % 2, 0:P], v[:, 0, n % 2, :], start=True, stop=True)
                    nc.tensor.matmul(num_ps[:, HD + 2:2 * HD + 4], at[:, n % 2, P:T], v[:, 0, n % 2, :],
                                     start=True, stop=False)
                    nc.tensor.matmul(num_ps[:, HD + 2:2 * HD + 4], at[:, n % 2, T:T + P], v[:, 1, n % 2, :],
                                     start=False, stop=True).then_inc(num_done, 1)
                n = c - 6
                if live(i, n):
                    need(pe, ot_ready, i, H, n + 1)
                    if n % H == 0:
                        need(pe, y_sum, i, 1, n // H)
                    if n % 4 == 0:
                        pe.wait_ge(w_lo_ready, n % H + 4)
                    for t in range(TT):
                        for m, (l, r) in enumerate(((ot_hi, wo_hi), (ot_hi, wo_lo), (ot_lo, wo_hi))):
                            last = nc.tensor.matmul(wo_ps[:, t], l[:, n % 2, t * P:(t + 1) * P], r[:, n % H],
                                                    start=n % H == 0 and t == 0 and m == 0,
                                                    stop=n % H == H - 1 and m == 2, skip_group_check=True)
                    last.then_inc(wo_done, 1)
                n = c - 4
                if live(i, n):
                    need(pe, pt_ready, i, H // 2, n // 2 + 1)
                    need(pe, v_ready, i, H // 2, n // 2 + 1)
                    need(pe, ot_ready, i, H, n)
                    for t in range(TT):
                        last = nc.tensor.matmul(lo_ps[:, t * P:(t + 1) * P], pt[:, (n // 2) % 2, n % 2, t],
                                                v_ext[:, (n // 2) % VB, t, n % 2, 0:HD], start=True, stop=True)
                    last.then_inc(loc_done, 1)

            def boot(eng):
                eng.wait_ge(masks_ready, 3)
                transpose_xn(0, 1, qk_ps[0])

            run(pe, boot, step)

        @block.scalar
        def _(act):
            def split_weights(chunks):
                for m in chunks:
                    staged, hi = chunk(m, w_hi, wo_hi)
                    act.wait_ge(stage_loaded[m % SLOTS], 16 * (m // SLOTS + 1))
                    nc.scalar.copy(hi, staged).then_inc(w_hi_ready, 1)

            def split_xt(i, k, n):
                need(act, xt_done, i, 1, k)
                need(act, qk_done, i, H, n)
                need(act, v_done, i, H // 2, n // 2)
                nc.scalar.copy(xt_hi[:], qk_ps[0][:]).then_inc(xt_hi_ready, 1)

            def step(i, c):
                h = c % H
                if isinstance(i, int) and i == 0:
                    split_weights(CHUNKS_AT[c])
                if live(i, c):
                    need(act, qk_done, i, H, c + 1)
                    need(act, sc_done, i, H, c - 1)
                    nc.scalar.copy(qk[:, c % 2], qk_ps[c % 2][:]).then_inc(qk_copied, 1)
                    need(act, phi_joined, i, H, c - 1)
                    nc.scalar.activation(ez[:, c % 2], qk_ps[c % 2][:], ACT.Exp, bias=phi_b[:, h:h + 1],
                                         scale=phi_s[:, h:h + 1]).then_inc(e_ready, 1)
                n = c - 5
                if live(i, n):
                    need(act, ot_done, i, H, n + 1)
                    need(act, wo_done, i, H, n - 1)
                    nc.scalar.copy(ot_hi[:, n % 2], lo_ps[:, T:2 * T]).then_inc(ot_hi_ready, 1)
                if live(i, c):
                    nc.scalar.activation(z1[:, c % 2], qk_ps[c % 2][:], ACT.Identity, bias=phi_b1[:, h:h + 1],
                                         scale=phi_s[:, h:h + 1]).then_inc(z1_ready, 1)
                if live(i, c + 1) and h == H - 1:
                    split_xt(i, c // H + 2, c + 1)
                if live(i, c) and h % 2 == 0:
                    p = c // 2
                    need(act, v_done, i, H // 2, p + 1)
                    need(act, loc_done, i, H, 2 * (p - VB + 1))
                    need(act, num_done, i, H, 2 * (p - VB + 1))
                    nc.scalar.copy(v_ext[:, p % VB, :, :, 0:HD],
                                   v_ps[:].rearrange("p (t h d) -> p t h d", t=TT, h=2)).then_inc(v_ready, 1)
                if c % 2 == 0 and live(i, c - 2):
                    need(act, sc_ready, i, H // 2, c // 2)
                    need(act, prob_ready, i, H // 2, c // 2 - 1)
                    nc.scalar.activation(pexp[:], sc[:], ACT.Exp, scale=SCALING).then_inc(p_exp, 1)
                if c % 2 == 1 and live(i, c - 3):
                    p = (c - 3) // 2
                    need(act, pt_done, i, H // 2, p + 1)
                    need(act, loc_done, i, H, 2 * p - 2)
                    src = v_ps[:, 0:2 * P].rearrange("p (h t c) -> p h t c", h=2, t=2)
                    for r in range(2):
                        q = slice(r * BS, (r + 1) * BS)
                        last = nc.scalar.copy(pt[q, p % 2, :, :, r * BS:(r + 1) * BS], src[q])
                    last.then_inc(pt_ready, 1)
                n = c - 3
                if live(i, n):
                    need(act, rden_ready, i, H, n + 1)
                    need(act, o_ready, i, H, n - 1)
                    for t in range(TT):
                        last = nc.scalar.activation(num[:, n % 2, t], num_ps[:, t * (HD + 2):t * (HD + 2) + HD],
                                                    ACT.Copy, scale=rden[:, n % 2, t:t + 1])
                    last.then_inc(num_scaled, 1)

            def boot(eng):
                act.wait_ge(mem_zeroed, 4 + 4 * VB)
                split_weights(range(2))
                split_xt(0, 1, 0)
                split_weights(range(2, 4))
                act.wait_ge(masks_ready, 4)

            run(act, boot, step)

        @block.vector
        def _(dve):
            def split_weights(chunks):
                for m in chunks:
                    staged, lo = chunk(m, w_lo, wo_lo)
                    dve.wait_ge(w_hi_ready, m + 1)
                    nc.vector.tensor_tensor(lo, staged, chunk(m, w_hi, wo_hi)[1].bitcast(F32), ALU.subtract)\
                      .then_inc(w_lo_ready, 1)

            def layer_norm(i, k):
                need(dve, xln_loaded, i, 16, 16 * k)
                for t in range(TT):
                    nc.vector.bn_stats(stats[:, t], x_ln[:, t]).then_inc(ln_stats, 1)
                need(dve, ln_stats, i, TT, TT * k)
                nc.vector.tensor_copy(stats_count[:], stats[:, :, 0])
                for t in range(TT):
                    nc.vector.bn_aggr(mv[:, t], stats[:, t]).then_inc(ln_mv, 1)
                need(dve, ln_mv, i, TT, TT * k)
                nc.vector.tensor_scalar(var_eps[:], mv[:, :, 1], LN_EPS, None, ALU.add).then_inc(ln_var, 1)

            def normalise(i, k):
                need(dve, ln_rstd, i, 1, k)
                need(dve, xt_done, i, 1, k - 1)
                for t in range(TT):
                    last = nc.vector.tensor_scalar(xn[:, t], x_ln[:, t], mv[:, t, 0:1], rstd[:, t:t + 1],
                                                   ALU.subtract, ALU.mult)
                last.then_inc(xn_ready, 1)

            def split_xt(i, k):
                need(dve, xt_hi_ready, i, 1, k)
                nc.vector.tensor_tensor(xt_lo[:], qk_ps[0][:], xt_hi[:].bitcast(F32), ALU.subtract)\
                  .then_inc(xt_lo_ready, 1)

            def step(i, c):
                h = c % H
                if isinstance(i, int) and i == 0:
                    split_weights(CHUNKS_AT[c])
                n = c - 5
                if live(i, n):
                    need(dve, loc_done, i, H, n + 1)
                    need(dve, num_scaled, i, H, n + 1)
                    need(dve, ot_done, i, H, n - 1)
                    nc.vector.tensor_tensor(o[:, n % 2], lo_ps[:, 0:T].rearrange("p (t d) -> p t d", t=TT),
                                            num[:, n % 2], ALU.add).then_inc(o_ready, 1)
                n = c - 1
                if live(i, n):
                    need(dve, e_ready, i, H, n + 1)
                    need(dve, z1_ready, i, H, n + 1)
                    need(dve, phi_ready, i, H, n)
                    nc.vector.scalar_tensor_tensor(phi_raw[:], ez[:, n % 2], 1.0, z1[:, n % 2], ALU.min, ALU.max)\
                      .then_inc(phi_joined, 1)
                    need(dve, phi_joined, i, H, n + 1)
                    need(dve, at_done, i, H, n - 1)
                    nc.vector.tensor_scalar(phi_hi[:, n % 2], phi_raw[:], PHI_TOP, None, ALU.min)\
                      .then_inc(phi_hi_ready, 1)
                    need(dve, phi_hi_ready, i, H, n + 1)
                    nc.vector.scalar_tensor_tensor(phi_lo[:, n % 2], phi_raw[:], PHI_TOP, phi_hi[:, n % 2].bitcast(F32),
                                                   ALU.min, ALU.subtract).then_inc(phi_ready, 1)
                if live(i, c + 1) and h == H - 1:
                    split_xt(i, c // H + 2)
                n = c - 5
                if live(i, n):
                    need(dve, ot_hi_ready, i, H, n + 1)
                    nc.vector.tensor_tensor(ot_lo[:, n % 2], lo_ps[:, T:2 * T], ot_hi[:, n % 2].bitcast(F32),
                                            ALU.subtract).then_inc(ot_ready, 1)
                if c % 2 == 0 and live(i, c - 2):
                    p = (c - 2) // 2
                    need(dve, sc_done, i, H, c)
                    src = sc_ps[:, 0:4 * BS].rearrange("p (g s) -> p g s", g=4)
                    nc.vector.reduce_max(rmax[:], src, AX_X).then_inc(max_ready, 1)
                    need(dve, max_ready, i, H // 2, p + 1)
                    need(dve, p_exp, i, H // 2, p)
                    nc.vector.tensor_tensor(sc[:], src, rmax[:].unsqueeze(2).broadcast_to([P, 4, BS]), ALU.subtract)\
                      .then_inc(sc_ready, 1)
                n = c - 2
                if live(i, n):
                    need(dve, at_done, i, H, n + 1)
                    need(dve, num_done, i, H, n - 1)
                    nc.vector.tensor_tensor(at[:, n % 2], at_ps[:, 0:T + P], at_mask[:], ALU.mult).then_inc(at_ready, 1)
                n = c - 3
                if live(i, n):
                    need(dve, num_done, i, H, n + 1)
                    nc.vector.tensor_scalar(den[:], num_ps[:, HD:HD + 2 + HD + 1:HD + 2], DEN_EPS, None, ALU.max)\
                      .then_inc(den_ready, 1)
                    need(dve, den_ready, i, H, n + 1)
                    need(dve, num_scaled, i, H, n - 1)
                    nc.vector.reciprocal(rden[:, n % 2], den[:]).then_inc(rden_ready, 1)
                n = c - 6
                if live(i, n) and n % H == H - 1:
                    k = n // H + 1
                    need(dve, wo_done, i, H, n + 1)
                    need(dve, xres_loaded, i, 16, 16 * k)
                    nc.vector.tensor_tensor(y[:], wo_ps[:], x_res[:], ALU.add).then_inc(y_sum, 1)
                    need(dve, y_sum, i, 1, k)
                    nc.vector.tensor_tensor(y[:], y[:], bo_bc[:].unsqueeze(1).broadcast_to([P, TT, D]), ALU.add)\
                      .then_inc(y_ready, 1)
                if c % 2 == 0 and live(i, c - 2):
                    p = (c - 2) // 2
                    need(dve, p_exp, i, H // 2, p + 1)
                    nc.vector.reduce_sum(rsum[:], pexp[:], AX_X).then_inc(sum_ready, 1)
                    need(dve, sum_ready, i, H // 2, p + 1)
                    nc.vector.reciprocal(rinv[:], rsum[:]).then_inc(inv_ready, 1)
                    need(dve, inv_ready, i, H // 2, p + 1)
                    need(dve, pt_done, i, H // 2, p)
                    nc.vector.tensor_tensor(prob[:], pexp[:], rinv[:].unsqueeze(2).broadcast_to([P, 4, BS]), ALU.mult)\
                      .then_inc(prob_ready, 1)
                if h == 9 and live(i, c - h + H):
                    layer_norm(i, c // H + 2)
                if h == 11 and live(i, c - h + H):
                    normalise(i, c // H + 2)

            def boot(eng):
                layer_norm(0, 1)
                normalise(0, 1)
                split_weights(range(2))
                dve.wait_ge(mem_zeroed, 4 + 4 * VB)
                split_xt(0, 1)
                split_weights(range(2, 4))
                dve.wait_ge(consts_loaded, 48)
                nc.vector.tensor_scalar(phi_b1[:], phi_b[:], 1.0, None, ALU.add).then_inc(masks_ready, 1)
                dve.wait_ge(masks_ready, 4)

            run(dve, boot, step)


FI = 704
IT = -(-FI // P)
FR = FI - (IT - 1) * P
G = 512
GT = G // P
NG = B * T // G
TURN = 2 * IT


FULL = (IT - 1) * P
assert 2 * FR == P


def part(t):
    return slice(0, P) if t < IT - 1 else slice(FR, P)


class FfnWeights:

    def __init__(self, nc, ctx):
        def sb(name, shape, dt=F32):
            return ctx.enter_context(nc.sbuf_tensor("f_" + name, shape, dt))

        self.gate_hi = sb("gate_hi", [P, KT, FULL], F32R)
        self.gate_lo = sb("gate_lo", [P, KT, FULL], F32R)
        self.up_hi = sb("up_hi", [P, KT, FULL], F32R)
        self.up_lo = sb("up_lo", [P, KT, FULL], F32R)
        self.both_hi = sb("both_hi", [P, KT, 2 * FR], F32R)
        self.both_lo = sb("both_lo", [P, KT, 2 * FR], F32R)
        self.down_hi = sb("down_hi", [P, IT, D], F32R)
        self.down_lo = sb("down_lo", [P, IT, D], F32R)
        self.gate_s = sb("gate_s", [P, IT])
        self.up_s = sb("up_s", [P, IT])
        self.down_s = sb("down_s", [P, D])
        self.ident = sb("ident", [P, P])
        self.nc, self.ctx, self.sems = nc, ctx, {}

    def sem(self, name):
        if name not in self.sems:
            self.sems[name] = self.ctx.enter_context(self.nc.semaphore("f_" + name))
        return self.sems[name]


class PrepareFfn:

    def __init__(self, nc, io, fw, ctx, banks):
        def sb(name, shape, dt=F32):
            return ctx.enter_context(nc.sbuf_tensor("p_" + name, shape, dt))

        def sem(name):
            return ctx.enter_context(nc.semaphore("p_" + name))

        self.nc, self.io, self.fw, self.t_ps = nc, io, fw, banks
        self.gate = sb("gate", [P, IT, D])
        self.up = sb("up", [P, IT, D])
        self.down = sb("down", [P, KT, FI])
        self.gate_loaded, self.up_loaded, self.down_loaded = sem("gate_loaded"), sem("up_loaded"), sem("down_loaded")
        self.scales_loaded = sem("scales_loaded")
        self.ident_ready = sem("ident_ready")
        self.t_done, self.hi_ready, self.lo_ready = sem("t_done"), sem("hi_ready"), sem("lo_ready")

        self.pieces = []
        for nat, hi, lo, loaded in ((self.gate, fw.gate_hi, fw.gate_lo, self.gate_loaded),
                                    (self.up, fw.up_hi, fw.up_lo, self.up_loaded)):
            for k in range(KT):
                for t0, t1 in ((0, 4), (4, IT - 1)):
                    ins = [(nat[:, t, k * P:(k + 1) * P], (t - t0) * P, P, P) for t in range(t0, t1)]
                    at = slice(t0 * P, t1 * P)
                    self.pieces.append((loaded, 32, ins, hi[:, k, at], lo[:, k, at], slice(0, P), (t1 - t0) * P))
        for k in range(KT):
            ins = [(nat[0:FR, IT - 1, k * P:(k + 1) * P], j * FR, FR, P) for j, nat in enumerate((self.gate, self.up))]
            self.pieces.append((self.up_loaded, 32, ins, fw.both_hi[:, k], fw.both_lo[:, k], slice(0, P), 2 * FR))
        for t in range(IT):
            c0 = min(t * P, FI - P)
            ins = [(self.down[:, k, c0:c0 + P], k * P, P, P) for k in range(KT)]
            self.pieces.append((self.down_loaded, 16, ins, fw.down_hi[part(t), t], fw.down_lo[part(t), t], part(t), D))

    def load(self, sp):
        io, fw, cut = self.io, self.fw, (IT - 1) * P
        for w, dst, loaded in ((io["f_gate_w"], self.gate, self.gate_loaded), (io["f_up_w"], self.up, self.up_loaded)):
            sp.dma_start(dst[:, 0:IT - 1], w[0:cut].rearrange("(t p) d -> p t d", p=P)).then_inc(loaded, 16)
            sp.dma_start(dst[0:FR, IT - 1], w[cut:FI]).then_inc(loaded, 16)
        sp.dma_start(self.down[:], io["f_down_w"].rearrange("(k p) n -> p k n", p=P)).then_inc(self.down_loaded, 16)
        for s, dst, at in ((io["f_gate_s"], fw.gate_s, slice(0, FR)), (io["f_up_s"], fw.up_s, slice(FR, P))):
            sp.dma_start(dst[:, 0:IT - 1], s[0:cut].rearrange("(t p) -> p t", p=P),
                         allow_slow_non_contiguous=True).then_inc(self.scales_loaded, 16)
            sp.dma_start(dst[at, IT - 1:IT], s[cut:FI].rearrange("(p a) -> p a", a=1))\
              .then_inc(self.scales_loaded, 16)
        sp.dma_start(fw.down_s[:], io["f_down_s"].rearrange("(a n) -> a n", a=1).broadcast_to([P, D]))\
          .then_inc(self.scales_loaded, 16)

    def masks(self, pool):
        ident = self.fw.ident
        pool.memset(ident[:], 0.0).then_inc(self.ident_ready, 1)
        pool.wait_ge(self.ident_ready, 1)
        pool.affine_select(out=ident[:], in_=ident[:], compare_op=ALU.not_equal, fill=1.0, base=0,
                           pattern=[[-1, P]], channel_multiplier=1).then_inc(self.ident_ready, 1)

    def transpose(self, pe):
        for m, (loaded, count, ins, hi, lo, r, cols) in enumerate(self.pieces):
            pe.wait_ge(loaded, count)
            if m >= len(self.t_ps):
                pe.wait_ge(self.lo_ready, m - len(self.t_ps) + 1)
            for src, at, kin, kout in ins:
                last = self.nc.tensor.transpose(self.t_ps[m % len(self.t_ps)][0:kout, at:at + kin], src,
                                                self.fw.ident[0:kin, 0:kin])
            last.then_inc(self.t_done, 1)

    def split_hi(self, act):
        for m, (loaded, count, ins, hi, lo, r, cols) in enumerate(self.pieces):
            act.wait_ge(self.t_done, m + 1)
            self.nc.scalar.copy(hi, self.t_ps[m % len(self.t_ps)][r, 0:cols]).then_inc(self.hi_ready, 1)
        act.wait_ge(self.scales_loaded, 80)

    def split_lo(self, dve):
        for m, (loaded, count, ins, hi, lo, r, cols) in enumerate(self.pieces):
            dve.wait_ge(self.hi_ready, m + 1)
            self.nc.vector.tensor_tensor(lo, self.t_ps[m % len(self.t_ps)][r, 0:cols], hi.bitcast(F32),
                                         ALU.subtract).then_inc(self.lo_ready, 1)
        dve.wait_ge(self.scales_loaded, 80)


BH = 16
DK = 8
DV = 16
VH = DV // DK
KD = BH * DK
VD = BH * DV
LR = 16
B_EPS = 1e-5
GATE_NORM = 16.0
CQ, CK, CV, CG, CR, CN = 0, KD, 2 * KD, 2 * KD + VD, 2 * KD + 2 * VD, 2 * KD + 2 * VD + LR


class WeightsB:
    PARTS = 5

    def __init__(self, nc, io, ctx):
        def sb(n, shape, dt=F32):
            return ctx.enter_context(nc.sbuf_tensor("b_" + n, shape, dt))

        def sem(n):
            return ctx.enter_context(nc.semaphore("b_" + n))

        self.nc, self.io = nc, io
        self.w_hi = sb("w_hi", [P, KT, CN], F32R)
        self.w_lo = sb("w_lo", [P, KT, CN], F32R)
        self.wo_hi = sb("wo_hi", [P, VH, D], F32R)
        self.wo_lo = sb("wo_lo", [P, VH, D], F32R)
        self.gk2 = sb("gk2", [LR, KD])
        self.bgk2 = sb("bgk2", [P, 1])
        self.norm_w = sb("norm_w", [P, VH])
        self.head_of = sb("head_of", [P, BH])
        self.sum_keys = sb("sum_keys", [P, DK, BH, DK])
        self.mean_vals = sb("mean_vals", [P, BH, DK])
        self.w_loaded, self.consts_loaded, self.wo_scaled = sem("w_loaded"), sem("consts_loaded"), sem("wo_scaled")
        self.masks_set, self.sel_set = sem("masks_set"), sem("sel_set")
        self.w_hi_ready, self.w_lo_ready = sem("w_hi_ready"), sem("w_lo_ready")

    def stage(self, ctx):
        self.w_stage = ctx.enter_context(self.nc.sbuf_tensor("b_w_stage", [P, KT, CN], F32))
        self.wo_stage = ctx.enter_context(self.nc.sbuf_tensor("b_wo_stage", [P, VH, D], F32))

    def parts(self, w):
        gates = self.w_stage[:, :, CG:CR].rearrange("p k (h a v) -> p k h a v", h=BH, a=VH)
        parts = [(self.w_stage[:, :, 0:CG], w[:, :, 0:CG]), (self.w_stage[:, :, CR:CN], w[:, :, CR:CN])]
        for a in range(VH):
            parts.append((gates[:, :, :, a], w[:, :, CG + a * P:CG + (a + 1) * P]
                          .rearrange("p k (h v) -> p k h v", h=BH)))
        return parts

    def load(self, sp):
        io = self.io
        for n, c0, c1 in (("Wq", CQ, CK), ("Wk", CK, CV), ("Wv", CV, CG), ("Wg", CG, CR), ("Wgk1", CR, CN)):
            sp.dma_start(self.w_stage[:, :, c0:c1], io["b_" + n].rearrange("(k p) n -> p k n", p=P))\
              .then_inc(self.w_loaded, 16)
        for h in range(BH):
            at = slice(h * DK, (h + 1) * DK)
            sp.dma_start(self.wo_stage[at], io["b_Wo"][h * DV:(h + 1) * DV].rearrange("(a v) n -> v a n", a=VH))\
              .then_inc(self.w_loaded, 16)
            sp.dma_start(self.norm_w[at], io["b_norm_w"].rearrange("(a v) -> v a", a=VH),
                         allow_slow_non_contiguous=True).then_inc(self.consts_loaded, 16)
        sp.dma_start(self.gk2[:], io["b_Wgk2"]).then_inc(self.consts_loaded, 16)
        sp.dma_start(self.bgk2[:], io["b_bgk2"].rearrange("(p a) -> p a", a=1)).then_inc(self.consts_loaded, 16)

    def masks(self, pool):
        head_of = self.head_of
        pool.memset(head_of[:], 1.0).then_inc(self.masks_set, 1)
        pool.wait_ge(self.masks_set, 1)
        pool.affine_select(out=head_of[:], in_=head_of[:], compare_op=ALU.is_ge, fill=0.0, base=0,
                           pattern=[[-DK, BH]], channel_multiplier=1).then_inc(self.masks_set, 1)
        pool.wait_ge(self.masks_set, 2)
        pool.affine_select(out=head_of[:], in_=head_of[:], compare_op=ALU.is_ge, fill=0.0, base=DK - 1,
                           pattern=[[DK, BH]], channel_multiplier=-1).then_inc(self.masks_set, 1)

    def selectors(self, dve):
        dve.wait_ge(self.masks_set, 3)
        self.nc.vector.memset(self.sum_keys[:], 0.0).then_inc(self.sel_set, 1)
        self.nc.vector.tensor_scalar(self.mean_vals[:], self.head_of[:].unsqueeze(2).broadcast_to([P, BH, DK]),
                                     1.0 / DV, None, ALU.mult).then_inc(self.sel_set, 1)
        dve.wait_ge(self.sel_set, 2)
        for m in range(DK):
            last = self.nc.vector.tensor_copy(self.sum_keys[:, m, :, m], self.head_of[:])
        last.then_inc(self.sel_set, 1)

    def split_hi(self, act, m):
        if m == 0:
            act.wait_ge(self.w_loaded, 16 * (5 + BH))
            act.wait_ge(self.consts_loaded, 16 * (BH + 2))
        if m < self.PARTS - 1:
            staged, hi = self.parts(self.w_hi)[m]
            self.nc.scalar.copy(hi, staged).then_inc(self.w_hi_ready, 1)
        else:
            for a in range(VH):
                self.nc.scalar.mul(self.wo_stage[:, a], self.wo_stage[:, a], self.norm_w[:, a:a + 1])\
                    .then_inc(self.wo_scaled, 1)
            act.wait_ge(self.wo_scaled, VH)
            self.nc.scalar.copy(self.wo_hi[:], self.wo_stage[:]).then_inc(self.w_hi_ready, 1)

    def split_lo(self, dve, m):
        dve.wait_ge(self.w_hi_ready, m + 1)
        if m < self.PARTS - 1:
            (staged, lo), (_, hi) = self.parts(self.w_lo)[m], self.parts(self.w_hi)[m]
        else:
            staged, lo, hi = self.wo_stage[:], self.wo_lo[:], self.wo_hi[:]
        self.nc.vector.tensor_tensor(lo, staged, hi.bitcast(F32), ALU.subtract).then_inc(self.w_lo_ready, 1)


def ffn(nc, name, fw, x_in, x_out, io=None, bw=None):
    LAG = 6
    with ExitStack() as ctx:
        def sb(n, shape, dt=F32):
            return ctx.enter_context(nc.sbuf_tensor(name + n, shape, dt))

        def ps(n, shape):
            return ctx.enter_context(nc.psum_tensor(name + n, shape, F32))

        sem = fw.sem

        x = sb("x", [P, 2, GT, D])
        y = sb("y", [P, 2, GT, D])
        xn = sb("xn", [P, GT, D])
        stats = sb("stats", [P, GT, 6])
        stats_count = sb("stats_count", [P, GT])
        mv = sb("mv", [P, GT, 2])
        var_eps = sb("var_eps", [P, GT])
        half = sb("half", [P, GT])
        rstd = sb("rstd", [P, GT])
        xt_hi = sb("xt_hi", [P, 2, KT, G], F32R)
        xt_lo = sb("xt_lo", [P, 2, KT, G], F32R)
        act_g = sb("act_g", [P, 2, G])
        hid = sb("hid", [P, 2, G])
        hid_hi = sb("hid_hi", [P, 2, G], F32R)
        hid_lo = sb("hid_lo", [P, 2, G], F32R)

        gate_ps = [ps(f"gate_ps{i}", [P, G]) for i in range(2)]
        up_ps = [ps(f"up_ps{i}", [P, G]) for i in range(2)]
        xt_ps = [ps(f"xt_ps{k}", [P, G]) for k in range(KT)]
        down_ps = [ps(f"down_ps{i}", [P, 2, D]) for i in range(2)]

        x_loaded = [sem(f"x_loaded{i}") for i in range(2)]
        y_stored = [sem(f"y_stored{i}") for i in range(2)]
        half_ready = sem("half_ready")
        ln_stats, ln_mv, ln_var, ln_rstd = sem("ln_stats"), sem("ln_mv"), sem("ln_var"), sem("ln_rstd")
        xn_ready, xt_done, xt_hi_ready, xt_lo_ready = sem("xn_ready"), sem("xt_done"), sem("xt_hi_ready"), sem("xt_lo_ready")
        gate_up_done, silu_ready, hid_ready = sem("gate_up_done"), sem("silu_ready"), sem("hid_ready")
        hid_hi_ready, hid_lo_ready, down_done = sem("hid_hi_ready"), sem("hid_lo_ready"), sem("down_done")
        y_scaled, y_ready = sem("y_scaled"), sem("y_ready")

        prep = None
        B_PARTS_AT = ((), (), (), (), (0, 1), (2, 3, 4))
        if io:
            prep = PrepareFfn(nc, io, fw, ctx, gate_ps + up_ps)
            bw.stage(ctx)
        block = ctx.enter_context(nc.Block())
        TURNS = NG // 2

        def run(eng, boot, step):
            boot(eng)
            for c in range(LAG):
                step(0, c)
            with eng.Fori(0, TURNS - 1) as i:
                for c in range(LAG, LAG + TURN):
                    step(i, c)
            for c in range(LAG, TURN + LAG):
                step(TURNS - 1, c)

        def live(i, n):
            return not isinstance(i, int) or 0 <= TURN * i + n < IT * NG

        def tokens(x_dram, g):
            return x_dram.rearrange("b t d -> (b t) d")[g * G:(g + 1) * G].rearrange("(t p) d -> p t d", p=P)

        @block.sync
        def _(sp):
            sp.dma_start(x[:, 0], tokens(x_in, 0)).then_inc(x_loaded[0], 16)
            if prep:
                prep.load(sp)
            for g in range(NG):
                if g + 1 < NG:
                    if g >= 1:
                        sp.wait_ge(y_ready, g)
                        if g >= 2:
                            sp.wait_ge(y_stored[g % 2], 16 * (g // 2))
                    sp.dma_start(x[:, (g + 1) % 2], tokens(x_in, g + 1)).then_inc(x_loaded[(g + 1) % 2], 16)
                if prep and g == 0:
                    bw.load(sp)
                sp.wait_ge(y_ready, g + 1)
                sp.dma_start(tokens(x_out, g), y[:, g % 2]).then_inc(y_stored[g % 2], 16)
            for s in y_stored:
                sp.wait_ge(s, 16 * (NG // 2))

        @block.gpsimd
        def _(pool):
            if prep:
                prep.masks(pool)
            pool.memset(half[:], -0.5).then_inc(half_ready, 1)
            pool.wait_ge(half_ready, 1)

            def power(i, k):
                need(pool, ln_var, i, 1, k)
                pool.tensor_tensor(rstd[:], var_eps[:], half[:], ALU.pow).then_inc(ln_rstd, 1)

            power(0, 1)
            if prep:
                bw.masks(pool)
            with pool.Fori(0, NG - 1) as i:
                power(i, 2)

        @block.tensor
        def _(pe):
            def transpose_xn(i, k):
                need(pe, xn_ready, i, 2, k)
                need(pe, xt_lo_ready, i, 2, k - 1)
                for kt in range(KT):
                    for t in range(GT):
                        last = nc.tensor.transpose(xt_ps[kt][:, t * P:(t + 1) * P], xn[:, t, kt * P:(kt + 1) * P],
                                                   fw.ident[:])
                last.then_inc(xt_done, 1)

            def step(i, c):
                t = c % IT
                if live(i, c):
                    g = (c // IT) % 2
                    products = ((gate_ps, fw.gate_hi, fw.gate_lo), (up_ps, fw.up_hi, fw.up_lo))
                    cols = slice(t * P, t * P + P)
                    if t == IT - 1:
                        products, cols = ((gate_ps, fw.both_hi, fw.both_lo),), slice(0, 2 * FR)
                    if t == 0:
                        need(pe, xt_lo_ready, i, 2, c // IT + 1)
                    need(pe, hid_ready, i, TURN, c - 1)
                    for out, w_hi, w_lo in products:
                        for k in range(KT):
                            for m, (l, r) in enumerate(((w_hi, xt_hi), (w_hi, xt_lo), (w_lo, xt_hi))):
                                last = nc.tensor.matmul(out[c % 2][:], l[:, k, cols], r[:, g, k],
                                                        start=k == 0 and m == 0, stop=k == KT - 1 and m == 2)
                    last.then_inc(gate_up_done, 1)
                if t == IT - 1 and live(i, c - t + IT):
                    transpose_xn(i, c // IT + 2)
                n = c - 2
                if live(i, n):
                    u = n % IT
                    need(pe, hid_lo_ready, i, TURN, n + 1)
                    if u == 0:
                        need(pe, y_scaled, i, 2, n // IT)
                    for j in range(GT):
                        for m, (l, r) in enumerate(((hid_hi, fw.down_hi), (hid_hi, fw.down_lo), (hid_lo, fw.down_hi))):
                            last = nc.tensor.matmul(down_ps[j // 2][:, j % 2], l[part(u), n % 2, j * P:(j + 1) * P],
                                                    r[part(u), u], start=u == 0 and m == 0 and j % 2 == 0,
                                                    stop=u == IT - 1 and m == 2, skip_group_check=True)
                    last.then_inc(down_done, 1)

            def boot(eng):
                if prep:
                    pe.wait_ge(prep.ident_ready, 2)
                    prep.transpose(pe)
                transpose_xn(0, 1)
                if prep:
                    pe.wait_ge(prep.lo_ready, len(prep.pieces))

            run(pe, boot, step)

        @block.scalar
        def _(act):
            def split_xt(i, k, par):
                need(act, xt_done, i, 2, k)
                need(act, gate_up_done, i, TURN, (k - 2) * IT)
                for kt in range(KT):
                    last = nc.scalar.copy(xt_hi[:, par, kt], xt_ps[kt][:])
                last.then_inc(xt_hi_ready, 1)

            def step(i, c):
                t = c % IT
                if prep and isinstance(i, int) and i == 0:
                    for m in B_PARTS_AT[c]:
                        bw.split_hi(act, m)
                if t == IT - 1 and live(i, c - t + IT):
                    split_xt(i, c // IT + 2, (c // IT + 1) % 2)
                if live(i, c):
                    need(act, gate_up_done, i, TURN, c + 1)
                    need(act, hid_ready, i, TURN, c - 1)
                    src = slice(0, P) if t < IT - 1 else slice(0, FR)
                    nc.scalar.activation(act_g[part(t), c % 2], gate_ps[c % 2][src], ACT.Silu,
                                         scale=fw.gate_s[src, t:t + 1]).then_inc(silu_ready, 1)
                n = c - 1
                if live(i, n):
                    need(act, hid_ready, i, TURN, n + 1)
                    need(act, down_done, i, TURN, n - 1)
                    nc.scalar.copy(hid_hi[part(n % IT), n % 2], hid[part(n % IT), n % 2]).then_inc(hid_hi_ready, 1)

            def boot(eng):
                if prep:
                    prep.split_hi(act)
                split_xt(0, 1, 0)

            run(act, boot, step)

        @block.vector
        def _(dve):
            def layer_norm(i, k, par):
                need(dve, x_loaded[par], i, 16, 16 * ((k + 1) // 2))
                for t in range(GT):
                    nc.vector.bn_stats(stats[:, t], x[:, par, t]).then_inc(ln_stats, 1)
                need(dve, ln_stats, i, 2 * GT, GT * k)
                nc.vector.tensor_copy(stats_count[:], stats[:, :, 0])
                for t in range(GT):
                    nc.vector.bn_aggr(mv[:, t], stats[:, t]).then_inc(ln_mv, 1)
                need(dve, ln_mv, i, 2 * GT, GT * k)
                nc.vector.tensor_scalar(var_eps[:], mv[:, :, 1], LN_EPS, None, ALU.add).then_inc(ln_var, 1)

            def normalise(i, k, par):
                need(dve, ln_rstd, i, 2, k)
                need(dve, xt_done, i, 2, k - 1)
                for t in range(GT):
                    last = nc.vector.tensor_scalar(xn[:, t], x[:, par, t], mv[:, t, 0:1], rstd[:, t:t + 1],
                                                   ALU.subtract, ALU.mult)
                last.then_inc(xn_ready, 1)

            def split_xt(i, k, par):
                need(dve, xt_hi_ready, i, 2, k)
                for kt in range(KT):
                    last = nc.vector.tensor_tensor(xt_lo[:, par, kt], xt_ps[kt][:], xt_hi[:, par, kt].bitcast(F32),
                                                   ALU.subtract)
                last.then_inc(xt_lo_ready, 1)

            def step(i, c):
                t = c % IT
                if prep and isinstance(i, int) and i == 0:
                    if c == 0:
                        bw.selectors(dve)
                    for m in B_PARTS_AT[c]:
                        bw.split_lo(dve, m)
                if t == IT - 1 and live(i, c - t + IT):
                    split_xt(i, c // IT + 2, (c // IT + 1) % 2)
                if t == 4 and live(i, c - t + IT):
                    normalise(i, c // IT + 2, (c // IT + 1) % 2)
                if live(i, c):
                    need(dve, silu_ready, i, TURN, c + 1)
                    need(dve, hid_lo_ready, i, TURN, c - 1)
                    up = up_ps[c % 2] if t < IT - 1 else gate_ps[c % 2]
                    nc.vector.scalar_tensor_tensor(hid[part(t), c % 2], up[part(t)],
                                                   fw.up_s[part(t), t:t + 1], act_g[part(t), c % 2],
                                                   ALU.mult, ALU.mult).then_inc(hid_ready, 1)
                n = c - 1
                if live(i, n):
                    r = part(n % IT)
                    need(dve, hid_hi_ready, i, TURN, n + 1)
                    nc.vector.tensor_tensor(hid_lo[r, n % 2], hid[r, n % 2], hid_hi[r, n % 2].bitcast(F32),
                                            ALU.subtract).then_inc(hid_lo_ready, 1)
                n = c - 2
                if live(i, n) and n % IT == IT - 1:
                    k = n // IT + 1
                    par = (n // IT) % 2
                    need(dve, down_done, i, TURN, n + 1)
                    for j in range(2):
                        last = nc.vector.tensor_tensor(y[:, par, 2 * j:2 * j + 2], down_ps[j][:],
                                                       fw.down_s[:].unsqueeze(1).broadcast_to([P, 2, D]), ALU.mult)
                    last.then_inc(y_scaled, 1)
                    need(dve, y_scaled, i, 2, k)
                    nc.vector.tensor_tensor(y[:, par], y[:, par], x[:, par], ALU.add).then_inc(y_ready, 1)
                if t == 3 and live(i, c - t + IT):
                    layer_norm(i, c // IT + 2, (c // IT + 1) % 2)

            def boot(eng):
                layer_norm(0, 1, 0)
                normalise(0, 1, 0)
                if prep:
                    prep.split_lo(dve)
                split_xt(0, 1, 0)

            run(dve, boot, step)


def attention_b(nc, bw, fw, x_in, x_out):
    LAG = 7
    TURN = 4
    TURNS = (B - 1 - LAG) // TURN
    with ExitStack() as ctx:
        def sb(n, shape, dt=F32):
            return ctx.enter_context(nc.sbuf_tensor("b_" + n, shape, dt))

        def ps(n, shape):
            return ctx.enter_context(nc.psum_tensor("b_" + n, shape, F32))

        def sem(n):
            return ctx.enter_context(nc.semaphore("b_" + n))

        DVE_V = 12
        kv = sb("kv", [P, 4, DV, T])
        state = sb("state", [P, 2, DV, T])
        one = sb("one", [P, 1])
        x_ln = sb("x_ln", [P, TT, D])
        x_res = sb("x_res", [P, TT, D])
        y = sb("y", [P, TT, D])
        xn = sb("xn", [P, TT, D])
        stats = sb("stats", [P, TT, 6])
        stats_count = sb("stats_count", [P, TT])
        mv = sb("mv", [P, TT, 2])
        var_eps = sb("var_eps", [P, TT])
        half = sb("half", [P, TT])
        rstd = sb("rstd", [P, TT])
        xt_hi = sb("xt_hi", [P, KT, T], F32R)
        xt_lo = sb("xt_lo", [P, KT, T], F32R)
        q = sb("q", [P, 4, T])
        k_ = sb("k", [P, 4, T])
        v = sb("v", [P, VH, T])
        gk1 = sb("gk1", [LR, T])
        z = sb("z", [P, 2, T])
        z_abs = sb("z_abs", [P, T])
        log_sig = sb("log_sig", [P, T])
        decay = sb("decay", [P, 2, 2, T])
        swish = sb("swish", [P, 4, VH, T])
        o_sq = sb("o_sq", [P, VH, T])
        o = sb("o", [P, VH, T])
        ms = sb("ms", [P, T])
        ln_ms = sb("ln_ms", [P, T])
        rms0 = sb("rms0", [P, T])
        rms_sq = sb("rms_sq", [P, T])
        rms = sb("rms", [P, T])
        eps = sb("eps", [P, 1])
        on = sb("on", [P, VH, T])
        o_hi = sb("o_hi", [P, VH, T], F32R)
        o_lo = sb("o_lo", [P, VH, T], F32R)
        xt_ps, kq_ps, v_ps, g_ps, gk_ps = (ps(n, [P, 2, T]) for n in ("xt_ps", "kq_ps", "v_ps", "g_ps", "gk_ps"))
        o_ps, ms_ps, y_ps = (ps(n, [P, 2, T]) for n in ("o_ps", "ms_ps", "y_ps"))

        xln_loaded, xres_loaded = sem("xln_loaded"), sem("xres_loaded")
        v_stored, y_stored = sem("v_stored"), sem("y_stored")
        v_spread = [sem(f"v_spread{i}") for i in range(4)]
        consts_set = sem("consts_set")
        ln_stats, ln_mv, ln_var, ln_rstd, xn_ready = (sem(n) for n in
                                                      ("ln_stats", "ln_mv", "ln_var", "ln_rstd", "xn_ready"))
        xt_done, xt_hi_ready, xt_lo_ready = sem("xt_done"), sem("xt_hi_ready"), sem("xt_lo_ready")
        gk1_done, kq_done, v_done, g_done, gk2_done = (sem(n) for n in
                                                       ("gk1_done", "kq_done", "v_done", "g_done", "gk2_done"))
        o_done, ms_done, y_done = sem("o_done"), sem("ms_done"), sem("y_done")
        gk1_ready, k_ready, q_ready, v_ready = (sem(n) for n in ("gk1_ready", "k_ready", "q_ready", "v_ready"))
        abs_ready, e_ready, ln_ready, ls_ready, decay_ready = (
            sem(n) for n in ("abs_ready", "e_ready", "ln_ready", "ls_ready", "decay_ready"))
        swish_ready, o_ready = sem("swish_ready"), sem("o_ready")
        kv_ready, kv_ready_pool, state_ready, qs_ready = (sem(n) for n in
                                                          ("kv_ready", "kv_ready_pool", "state_ready", "qs_ready"))
        ln_ms_ready, rms0_ready, rms_sq_ready, rms_err_ready = (
            sem(n) for n in ("ln_ms_ready", "rms0_ready", "rms_sq_ready", "rms_err_ready"))
        sq_ready, ms_ready, rms_ready, on_ready, og_ready, o_hi_ready, o_lo_ready, y_ready = (
            sem(n) for n in ("sq_ready", "ms_ready", "rms_ready", "on_ready", "og_ready", "o_hi_ready", "o_lo_ready",
                             "y_ready"))

        v_dram = nc.dram_tensor("b_values", (B, VD, T), F32, kind="Internal").ap()
        block = ctx.enter_context(nc.Block())

        def run(eng, boot, step):
            boot(eng)
            for c in range(LAG):
                step(0, c)
            with eng.Fori(0, TURNS) as i:
                for c in range(LAG, LAG + TURN):
                    step(i, c)
            for c in range(LAG, B - TURN * TURNS + 5):
                step(TURNS, c)

        def live(i, n):
            return not isinstance(i, int) or 0 <= TURN * i + n < B

        @block.sync
        def _(sp):
            def tiles(x_dram, b):
                return x_dram[b].rearrange("(t p) d -> p t d", p=P)

            def load_ln(b):
                if b < B:
                    if b >= 1:
                        sp.wait_ge(xn_ready, b)
                    sp.dma_start(x_ln[:], tiles(x_in, b)).then_inc(xln_loaded, 16)

            load_ln(0)
            load_ln(1)
            for c in range(B + 5):
                load_ln(c + 2)
                if c < B:
                    sp.wait_ge(v_ready, c + 1)
                    sp.dma_start(v_dram[c].rearrange("(a p) t -> p a t", p=P), v[:]).then_inc(v_stored, 16)
                n = c - 5
                if n >= 0:
                    sp.wait_ge(y_ready, n + 1)
                    sp.dma_start(tiles(x_out, n), y[:]).then_inc(y_stored, 16)
                if 0 <= n + 1 < B:
                    sp.dma_start(x_res[:], tiles(x_in, n + 1)).then_inc(xres_loaded, 16)
                if c < B:
                    sp.wait_ge(v_stored, 16 * (c + 1))
                    if c >= 4:
                        sp.wait_ge(state_ready, DV * (c - 3))
                    src = v_dram[c].rearrange("(h v) t -> h (v t)", h=BH).unsqueeze(1).broadcast_to([BH, DK, DV * T])
                    sp.dma_start(kv[:, c % 4].rearrange("p v t -> p (v t)"), src).then_inc(v_spread[c % 4], 16)
            sp.wait_ge(y_stored, 16 * B)

        @block.gpsimd
        def _(pool):
            pool.memset(half[:], -0.5).then_inc(consts_set, 1)
            pool.memset(one[:], 1.0).then_inc(consts_set, 1)
            pool.memset(eps[:], B_EPS).then_inc(consts_set, 1)
            pool.memset(decay[:, :, :, 0:1], 0.0).then_inc(consts_set, 1)
            pool.wait_ge(consts_set, 4)

            def power(i, k):
                need(pool, ln_var, i, TURN, k)
                pool.tensor_tensor(rstd[:], var_eps[:], half[:], ALU.pow).then_inc(ln_rstd, 1)

            def step(i, c):
                if live(i, c + 1):
                    power(i, c + 2)
                n = c - 2
                if live(i, n):
                    need(pool, v_spread[n % 4], i, 16, 16 * (n // 4 + 1))
                    need(pool, k_ready, i, TURN, n + 1)
                    last = kv[:, n % 4, DVE_V:DV]
                    pool.tensor_tensor(last, last, k_[:, n % 4].unsqueeze(1).broadcast_to([P, DV - DVE_V, T]),
                                       ALU.mult).then_inc(kv_ready_pool, 1)
                    need(pool, q_ready, i, TURN, n + 1)
                    for j in range(2):
                        vs = slice(j * DK, (j + 1) * DK)
                        need(pool, state_ready, i, DV * TURN, DV * n + DK * (j + 1))
                        pool.tensor_tensor(state[:, n % 2, vs], state[:, n % 2, vs],
                                           q[:, n % 4].unsqueeze(1).broadcast_to([P, DK, T]), ALU.mult)\
                            .then_inc(qs_ready, 1)

            def boot(eng):
                for used in fw.sems.values():
                    pool.sem_clear(used)
                power(0, 1)

            run(pool, boot, step)

        @block.tensor
        def _(pe):
            def project(out, c0, m=P):
                for k in range(KT):
                    for j, (l, r) in enumerate(((bw.w_hi, xt_hi), (bw.w_hi, xt_lo), (bw.w_lo, xt_hi))):
                        last = nc.tensor.matmul(out, l[:, k, c0:c0 + m], r[:, k], start=k == 0 and j == 0,
                                                stop=k == KT - 1 and j == 2)
                return last

            def transpose_xn(i, k):
                need(pe, xn_ready, i, TURN, k)
                need(pe, xt_lo_ready, i, TURN, k - 1)
                for kt in range(KT):
                    for t in range(TT):
                        last = nc.tensor.transpose(xt_ps[:, kt, t * P:(t + 1) * P], xn[:, t, kt * P:(kt + 1) * P],
                                                   fw.ident[:])
                last.then_inc(xt_done, 1)

            def step(i, c):
                if live(i, c):
                    need(pe, xt_lo_ready, i, TURN, c + 1)
                    need(pe, abs_ready, i, TURN, c)
                    need(pe, q_ready, i, TURN, c)
                    need(pe, v_ready, i, TURN, c)
                    project(gk_ps[0:LR, 0], CR, LR).then_inc(gk1_done, 1)
                    project(kq_ps[:, 1], CQ)
                    project(kq_ps[:, 0], CK).then_inc(kq_done, 1)
                    for a in range(VH):
                        last = project(v_ps[:, a], CV + a * P)
                    last.then_inc(v_done, 1)
                    need(pe, swish_ready, i, TURN, c)
                    for a in range(VH):
                        last = project(g_ps[:, a], CG + a * P)
                    last.then_inc(g_done, 1)
                    need(pe, gk1_ready, i, TURN, c + 1)
                    nc.tensor.matmul(gk_ps[:, 1], bw.gk2[:], gk1[:], start=True, stop=True).then_inc(gk2_done, 1)
                n = c - 5
                if live(i, n):
                    need(pe, o_lo_ready, i, TURN, n + 1)
                    need(pe, y_ready, i, TURN, n)
                    for t in range(TT):
                        rows_t = slice(t * P, (t + 1) * P)
                        for a in range(VH):
                            for m, (l, r) in enumerate(((o_hi, bw.wo_hi), (o_hi, bw.wo_lo), (o_lo, bw.wo_hi))):
                                last = nc.tensor.matmul(y_ps[:, t], l[:, a, rows_t], r[:, a], start=a == 0 and m == 0,
                                                        stop=a == VH - 1 and m == 2)
                    last.then_inc(y_done, 1)
                n = c - 3
                if live(i, n):
                    need(pe, o_ready, i, TURN, n)
                for a in range(VH):
                    if a == 1 and live(i, c + 1):
                        transpose_xn(i, c + 2)
                    if live(i, n):
                        need(pe, qs_ready, i, 2 * TURN, 2 * n + a + 1)
                        for m in range(DK):
                            last = nc.tensor.matmul(o_ps[:, a], bw.sum_keys[:, m], state[:, n % 2, a * DK + m],
                                                    start=m == 0, stop=m == DK - 1)
                if live(i, n):
                    last.then_inc(o_done, 1)
                if live(i, n):
                    need(pe, sq_ready, i, TURN, n + 1)
                    need(pe, ln_ms_ready, i, TURN, n)
                    for a in range(VH):
                        last = nc.tensor.matmul(ms_ps[:, 0], bw.mean_vals[:], o_sq[:, a], start=a == 0, stop=a == VH - 1)
                    last.then_inc(ms_done, 1)

            def boot(eng):
                pe.wait_ge(bw.consts_loaded, 16 * (BH + 2))
                pe.wait_ge(bw.w_lo_ready, bw.PARTS)
                pe.wait_ge(bw.sel_set, 3)
                transpose_xn(0, 1)

            run(pe, boot, step)

        @block.scalar
        def _(act):
            def split_xt(i, k):
                need(act, xt_done, i, TURN, k)
                need(act, g_done, i, TURN, k - 1)
                nc.scalar.copy(xt_hi[:], xt_ps[:]).then_inc(xt_hi_ready, 1)

            def step(i, c):
                filling = isinstance(i, int) and i == 0 and c < 3
                if live(i, c):
                    need(act, gk1_done, i, TURN, c + 1)
                    nc.scalar.copy(gk1[:], gk_ps[0:LR, 0]).then_inc(gk1_ready, 1)
                if live(i, c - 1):
                    need(act, g_done, i, TURN, c)
                    need(act, og_ready, i, TURN, c - 4)
                    nc.scalar.activation(swish[:, (c - 1) % 4], g_ps[:], ACT.Silu).then_inc(swish_ready, 1)
                n = c - 4
                if live(i, n):
                    need(act, ln_ms_ready, i, TURN, n + 1)
                    need(act, rms_ready, i, TURN, n)
                    nc.scalar.activation(rms0[:], ln_ms[:], ACT.Exp, scale=-0.5).then_inc(rms0_ready, 1)
                if live(i, c - 1):
                    need(act, ls_ready, i, TURN, c)
                    need(act, state_ready, i, DV * TURN, DV * (c - 2))
                    nc.scalar.activation(decay[:, (c - 1) % 2, :, 1:T],
                                         log_sig[:, 1:T].unsqueeze(1).broadcast_to([P, 2, T - 1]), ACT.Exp, scale=1.0 / GATE_NORM)\
                      .then_inc(decay_ready, 1)
                if live(i, c):
                    need(act, kq_done, i, TURN, c + 1)
                    need(act, kv_ready, i, TURN, c - 3)
                    need(act, kv_ready_pool, i, TURN, c - 3)
                    nc.scalar.copy(k_[:, c % 4], kq_ps[:, 0]).then_inc(k_ready, 1)
                    need(act, qs_ready, i, 2 * TURN, 2 * (c - 3))
                    nc.scalar.mul(q[:, c % 4], kq_ps[:, 1], float(DK) ** -0.5).then_inc(q_ready, 1)
                    need(act, gk2_done, i, TURN, c + 1)
                    nc.scalar.activation(z[:, c % 2], gk_ps[:, 1], ACT.Identity, bias=bw.bgk2[:])
                    need(act, ls_ready, i, TURN, c)
                    nc.scalar.activation(z_abs[:], gk_ps[:, 1], ACT.Abs, bias=bw.bgk2[:]).then_inc(abs_ready, 1)
                    if filling:
                        split_xt(0, c + 2)
                    need(act, abs_ready, i, TURN, c + 1)
                    nc.scalar.activation(z_abs[:], z_abs[:], ACT.Exp, scale=-1.0).then_inc(e_ready, 1)
                if live(i, c):
                    need(act, v_done, i, TURN, c + 1)
                    need(act, v_stored, i, 16 * TURN, 16 * c)
                    nc.scalar.copy(v[:], v_ps[:]).then_inc(v_ready, 1)
                    need(act, e_ready, i, TURN, c + 1)
                    nc.scalar.activation(z_abs[:], z_abs[:], ACT.Ln, bias=one[:]).then_inc(ln_ready, 1)
                if live(i, c + 1) and not filling:
                    split_xt(i, c + 2)
                n = c - 3
                if live(i, n):
                    need(act, o_done, i, TURN, n + 1)
                    nc.scalar.activation(o_sq[:], o_ps[:], ACT.Square).then_inc(sq_ready, 1)
                    need(act, on_ready, i, TURN, n)
                    nc.scalar.copy(o[:], o_ps[:]).then_inc(o_ready, 1)
                if live(i, c - 4):
                    need(act, og_ready, i, TURN, c - 3)
                    need(act, y_done, i, TURN, c - 4)
                    nc.scalar.copy(o_hi[:], on[:]).then_inc(o_hi_ready, 1)
                if live(i, n):
                    need(act, ms_done, i, TURN, n + 1)
                    need(act, rms_ready, i, TURN, n)
                    nc.scalar.activation(ms[:], ms_ps[:, 0], ACT.Identity, bias=eps[:]).then_inc(ms_ready, 1)
                    need(act, rms0_ready, i, TURN, n)
                    nc.scalar.activation(ln_ms[:], ms_ps[:, 0], ACT.Ln, bias=eps[:]).then_inc(ln_ms_ready, 1)

            def boot(eng):
                act.wait_ge(consts_set, 4)
                split_xt(0, 1)

            run(act, boot, step)

        @block.vector
        def _(dve):
            def layer_norm(i, k):
                need(dve, xln_loaded, i, 16 * TURN, 16 * k)
                for t in range(TT):
                    nc.vector.bn_stats(stats[:, t], x_ln[:, t]).then_inc(ln_stats, 1)
                need(dve, ln_stats, i, TT * TURN, TT * k)
                nc.vector.tensor_copy(stats_count[:], stats[:, :, 0])
                for t in range(TT):
                    nc.vector.bn_aggr(mv[:, t], stats[:, t]).then_inc(ln_mv, 1)
                need(dve, ln_mv, i, TT * TURN, TT * k)
                nc.vector.tensor_scalar(var_eps[:], mv[:, :, 1], LN_EPS, None, ALU.add).then_inc(ln_var, 1)

            def normalise(i, k):
                need(dve, ln_rstd, i, TURN, k)
                need(dve, xt_done, i, TURN, k - 1)
                for t in range(TT):
                    last = nc.vector.tensor_scalar(xn[:, t], x_ln[:, t], mv[:, t, 0:1], rstd[:, t:t + 1],
                                                   ALU.subtract, ALU.mult)
                last.then_inc(xn_ready, 1)

            def split_xt(i, k):
                need(dve, xt_hi_ready, i, TURN, k)
                nc.vector.tensor_tensor(xt_lo[:], xt_ps[:], xt_hi[:].bitcast(F32), ALU.subtract).then_inc(xt_lo_ready, 1)

            def step(i, c):
                if live(i, c + 1):
                    layer_norm(i, c + 2)
                if live(i, c - 1):
                    need(dve, ln_ready, i, TURN, c)
                    need(dve, decay_ready, i, TURN, c - 1)
                    nc.vector.scalar_tensor_tensor(log_sig[:], z[:, (c - 1) % 2], 0.0, z_abs[:], ALU.min, ALU.subtract)\
                      .then_inc(ls_ready, 1)
                n = c - 5
                if live(i, n):
                    need(dve, o_hi_ready, i, TURN, n + 1)
                    nc.vector.tensor_tensor(o_lo[:], on[:], o_hi[:].bitcast(F32), ALU.subtract).then_inc(o_lo_ready, 1)
                n = c - 2
                if live(i, n):
                    need(dve, k_ready, i, TURN, n + 1)
                    need(dve, v_spread[n % 4], i, 16, 16 * (n // 4 + 1))
                    first = kv[:, n % 4, 0:DVE_V]
                    nc.vector.tensor_tensor(first, first, k_[:, n % 4].unsqueeze(1).broadcast_to([P, DVE_V, T]),
                                            ALU.mult).then_inc(kv_ready, 1)
                if live(i, c + 1):
                    normalise(i, c + 2)
                n = c - 2
                if live(i, n):
                    need(dve, kv_ready, i, TURN, n + 1)
                    need(dve, decay_ready, i, TURN, n + 1)
                    need(dve, o_done, i, TURN, n - 1)
                    for m in range(0, DV, 2):
                        if m == DVE_V:
                            need(dve, kv_ready_pool, i, TURN, n + 1)
                        nc.vector.tensor_tensor_scan(state[:, n % 2, m:m + 2].rearrange("p v t -> p (v t)"),
                                                     decay[:, n % 2].rearrange("p v t -> p (v t)"),
                                                     kv[:, n % 4, m:m + 2].rearrange("p v t -> p (v t)"), 0.0,
                                                     ALU.mult, ALU.add).then_inc(state_ready, 2)
                n = c - 5
                if live(i, n):
                    need(dve, y_done, i, TURN, n + 1)
                    need(dve, xres_loaded, i, 16 * TURN, 16 * (n + 1))
                    need(dve, y_stored, i, 16 * TURN, 16 * n)
                    nc.vector.tensor_tensor(y[:], y_ps[:], x_res[:], ALU.add).then_inc(y_ready, 1)
                n = c - 4
                if live(i, n):
                    need(dve, rms0_ready, i, TURN, n + 1)
                    nc.vector.tensor_tensor(rms_sq[:], rms0[:], rms0[:], ALU.mult).then_inc(rms_sq_ready, 1)
                    need(dve, rms_sq_ready, i, TURN, n + 1)
                    need(dve, ms_ready, i, TURN, n + 1)
                    nc.vector.scalar_tensor_tensor(rms_sq[:], ms[:], -0.5, rms_sq[:], ALU.mult, ALU.mult)\
                      .then_inc(rms_err_ready, 1)
                    need(dve, rms_err_ready, i, TURN, n + 1)
                    nc.vector.scalar_tensor_tensor(rms[:], rms_sq[:], 1.5, rms0[:], ALU.add, ALU.mult)\
                      .then_inc(rms_ready, 1)
                    need(dve, rms_ready, i, TURN, n + 1)
                    need(dve, o_ready, i, TURN, n + 1)
                    nc.vector.tensor_tensor(on[:], o[:], rms[:].unsqueeze(1).broadcast_to([P, VH, T]), ALU.mult)\
                      .then_inc(on_ready, 1)
                    need(dve, on_ready, i, TURN, n + 1)
                    need(dve, swish_ready, i, TURN, n + 1)
                    nc.vector.tensor_tensor(on[:], on[:], swish[:, n % 4], ALU.mult).then_inc(og_ready, 1)
                if live(i, c + 1):
                    split_xt(i, c + 2)

            def boot(eng):
                dve.wait_ge(consts_set, 4)
                layer_norm(0, 1)
                normalise(0, 1)
                split_xt(0, 1)

            run(dve, boot, step)


def build(nc, io, x_in, out):
    x1, x2, x3 = (nc.dram_tensor(n, (B, T, D), F32, kind="Internal").ap() for n in ("x1", "x2", "x3"))
    attention_a(nc, io, x_in, x1)
    with ExitStack() as ctx:
        fw = FfnWeights(nc, ctx)
        bw = WeightsB(nc, io, ctx)
        ffn(nc, "f1_", fw, x1, x2, io, bw)
        attention_b(nc, bw, fw, x2, x3)
        ffn(nc, "f2_", fw, x3, out)


_PRE = {"L0_attn_a_": "", "L0_attn_b_": "b_", "L0_ffn_": "f_"}


def kernel(**inputs):
    import numpy as _np
    import concourse.bacc as _bacc
    from concourse import mybir as _mybir
    from concourse.bass_utils import run_bass_kernel_spmd as _run

    nc = _bacc.Bacc("TRN2", target_bir_lowering=False, num_devices=1)
    arrays, io = {}, {}
    for name, array in inputs.items():
        a = _np.ascontiguousarray(array)
        arrays[f"in_{name}_dram"] = a
        short = name
        for long, pre in _PRE.items():
            if name.startswith(long):
                short = pre + name[len(long):]
        io[short] = nc.dram_tensor(f"in_{name}_dram", a.shape, _mybir.dt.from_np(a.dtype), kind="ExternalInput").ap()
    out = nc.dram_tensor("out_0_dram", (B, T, D), _mybir.dt.float32, kind="ExternalOutput").ap()
    build(nc, io, io["x"], out)
    r = _run(nc, [arrays], core_ids=[0])
    return r.results[0]["out_0_dram"]
```
